# Optimizing a Trainium2 kernel written in Bass

```python
import numpy as np
import jax
import jax.numpy as jnp

def _softmax(x, axis=-1):
    return jax.nn.softmax(x, axis=axis)

def _gelu(x):
    return jax.nn.gelu(x, approximate=True)

def _silu(x):
    return jax.nn.silu(x)

def _sigmoid(x):
    return jax.nn.sigmoid(x)

def _layernorm(x, axis=-1, eps=1e-05):
    m = jnp.mean(x, axis=axis, keepdims=True)
    v = jnp.var(x, axis=axis, keepdims=True)
    return (x - m) / jnp.sqrt(v + eps)

def _scatter_add(tgt, idx, src, axis=0):
    return tgt.at[idx].add(src)

def _segment_sum(src, seg, n):
    return jax.ops.segment_sum(src, seg, n)
kernel_name = 'mk_adaln_d2_jaxref_r8_d1abb9'

def setup_inputs(seed: int=0):
    np.random.seed(seed)
    _w = jnp.asarray

    def _L0_attn_setup():
        import jax, jax.numpy as jnp
        import numpy as np
        import math
        D_MODEL = 256
        N_HEADS = 16
        D_HEAD = 128
        BATCH = 2
        SEQ = 256
        key = jax.random.key(seed)
        ks = jax.random.split(key, 5)
        std = 0.02
        x = jax.random.normal(ks[0], (BATCH, SEQ, D_MODEL), dtype=jnp.float32)
        W_Q = std * jax.random.normal(ks[1], (N_HEADS, D_HEAD, D_MODEL), dtype=jnp.float32)
        W_K = std * jax.random.normal(ks[2], (N_HEADS, D_HEAD, D_MODEL), dtype=jnp.float32)
        W_V = std * jax.random.normal(ks[3], (N_HEADS, D_HEAD, D_MODEL), dtype=jnp.float32)
        W_O = std * jax.random.normal(ks[4], (N_HEADS, D_MODEL, D_HEAD), dtype=jnp.float32)
        return {'x': x, 'W_Q': W_Q, 'W_K': W_K, 'W_V': W_V, 'W_O': W_O}
    _L0_attn_in = _L0_attn_setup()

    def _L0_ffn_setup():
        import jax, jax.numpy as jnp
        import numpy as np
        H, LAT, INTER, E, G, TOPK_G, TOP_K = (256, 128, 128, 32, 4, 2, 8)
        SHARED_INTER = 512
        ROUTED_SCALE = 2.5
        B, S = (2, 128)

        def relu2(x):
            return jnp.square(jax.nn.relu(x))
        key = jax.random.key(seed)
        ks = jax.random.split(key, 9)
        w = 0.02
        return {'hidden_states': jax.random.normal(ks[0], (B, S, H), jnp.float32), 'gate_w': jax.random.normal(ks[1], (E, H), jnp.float32) * w, 'gate_bias': jax.random.normal(ks[2], (E,), jnp.float32) * w, 'fc1_w': jax.random.normal(ks[3], (LAT, H), jnp.float32) * w, 'fc2_w': jax.random.normal(ks[4], (H, LAT), jnp.float32) * w, 'w1': jax.random.normal(ks[5], (E, INTER, LAT), jnp.float32) * w, 'w2': jax.random.normal(ks[6], (E, LAT, INTER), jnp.float32) * w, 'shared_up_w': jax.random.normal(ks[7], (SHARED_INTER, H), jnp.float32) * w, 'shared_down_w': jax.random.normal(ks[8], (H, SHARED_INTER), jnp.float32) * w}
    _L0_ffn_in = _L0_ffn_setup()
    _L0_c = _w((lambda *s: np.random.randn(*s).astype(np.float32) * 0.05)(1, 256))
    _L0_wmod = _w((lambda *s: np.random.randn(*s).astype(np.float32) * 0.05)(256, 6 * 256) * 256 ** (-0.5))

    def _L1_attn_setup():
        import jax, jax.numpy as jnp
        import numpy as np
        B, S, D = (4, 256, 256)
        H = 16
        HD = D // H
        key = jax.random.key(seed)
        ks = jax.random.split(key, 6)
        x = jax.random.normal(ks[0], (B, S, D), dtype=jnp.float32)
        Wq = jax.random.normal(ks[1], (D, D), dtype=jnp.float32) * 0.02
        Wk = jax.random.normal(ks[2], (D, D), dtype=jnp.float32) * 0.02
        Wv = jax.random.normal(ks[3], (D, D), dtype=jnp.float32) * 0.02
        Wo = jax.random.normal(ks[4], (D, D), dtype=jnp.float32) * 0.02
        bo = jax.random.normal(ks[5], (D,), dtype=jnp.float32) * 0.02
        return {'x': x, 'Wq': Wq, 'Wk': Wk, 'Wv': Wv, 'Wo': Wo, 'bo': bo}
    _L1_attn_in = _L1_attn_setup()

    def _L1_ffn_setup():
        import jax, jax.numpy as jnp
        import numpy as np
        DIM = 256
        INTER = 176
        E = 16
        TOPK = 4
        G = 4
        TOPK_G = 2
        N_SHARED = 2
        ROUTE_SCALE = 1.0
        INIT_STD = 0.02
        B, S = (1, 256)
        key = jax.random.key(seed)
        ks = jax.random.split(key, 9)
        std = INIT_STD
        x = jax.random.normal(ks[0], (B, S, DIM), jnp.float32)
        gate_w = jax.random.normal(ks[1], (E, DIM), jnp.float32) * std
        expert_bias = jnp.zeros((E,), jnp.float32)
        w1 = jax.random.normal(ks[2], (E, DIM, INTER), jnp.float32) * std
        w3 = jax.random.normal(ks[3], (E, DIM, INTER), jnp.float32) * std
        w2 = jax.random.normal(ks[4], (E, INTER, DIM), jnp.float32) * std
        sh = N_SHARED * INTER
        sw1 = jax.random.normal(ks[5], (DIM, sh), jnp.float32) * std
        sw3 = jax.random.normal(ks[6], (DIM, sh), jnp.float32) * std
        sw2 = jax.random.normal(ks[7], (sh, DIM), jnp.float32) * std
        return {'x': x, 'gate_w': gate_w, 'expert_bias': expert_bias, 'w1': w1, 'w2': w2, 'w3': w3, 'sw1': sw1, 'sw2': sw2, 'sw3': sw3}
    _L1_ffn_in = _L1_ffn_setup()
    _L1_c = _w((lambda *s: np.random.randn(*s).astype(np.float32) * 0.05)(1, 256))
    _L1_wmod = _w((lambda *s: np.random.randn(*s).astype(np.float32) * 0.05)(256, 6 * 256) * 256 ** (-0.5))
    _d = {'L0_attn_x': _L0_attn_in['x'], 'L0_attn_W_Q': _L0_attn_in['W_Q'], 'L0_attn_W_K': _L0_attn_in['W_K'], 'L0_attn_W_V': _L0_attn_in['W_V'], 'L0_attn_W_O': _L0_attn_in['W_O'], 'L0_ffn_gate_w': _L0_ffn_in['gate_w'], 'L0_ffn_gate_bias': _L0_ffn_in['gate_bias'], 'L0_ffn_fc1_w': _L0_ffn_in['fc1_w'], 'L0_ffn_fc2_w': _L0_ffn_in['fc2_w'], 'L0_ffn_w1': _L0_ffn_in['w1'], 'L0_ffn_w2': _L0_ffn_in['w2'], 'L0_ffn_shared_up_w': _L0_ffn_in['shared_up_w'], 'L0_ffn_shared_down_w': _L0_ffn_in['shared_down_w'], 'L0_c': _L0_c, 'L0_wmod': _L0_wmod, 'L1_attn_Wq': _L1_attn_in['Wq'], 'L1_attn_Wk': _L1_attn_in['Wk'], 'L1_attn_Wv': _L1_attn_in['Wv'], 'L1_attn_Wo': _L1_attn_in['Wo'], 'L1_attn_bo': _L1_attn_in['bo'], 'L1_ffn_gate_w': _L1_ffn_in['gate_w'], 'L1_ffn_expert_bias': _L1_ffn_in['expert_bias'], 'L1_ffn_w1': _L1_ffn_in['w1'], 'L1_ffn_w2': _L1_ffn_in['w2'], 'L1_ffn_w3': _L1_ffn_in['w3'], 'L1_ffn_sw1': _L1_ffn_in['sw1'], 'L1_ffn_sw2': _L1_ffn_in['sw2'], 'L1_ffn_sw3': _L1_ffn_in['sw3'], 'L1_c': _L1_c, 'L1_wmod': _L1_wmod}
    _x0 = _d['L0_attn_x']
    _d['L0_attn_x'] = jax.random.normal(jax.random.fold_in(jax.random.key(seed), 1), (1, 2048, 256), dtype=_x0.dtype)
    del _x0
    return _d

def reference(L0_attn_x, L0_attn_W_Q, L0_attn_W_K, L0_attn_W_V, L0_attn_W_O, L0_ffn_gate_w, L0_ffn_gate_bias, L0_ffn_fc1_w, L0_ffn_fc2_w, L0_ffn_w1, L0_ffn_w2, L0_ffn_shared_up_w, L0_ffn_shared_down_w, L0_c, L0_wmod, L1_attn_Wq, L1_attn_Wk, L1_attn_Wv, L1_attn_Wo, L1_attn_bo, L1_ffn_gate_w, L1_ffn_expert_bias, L1_ffn_w1, L1_ffn_w2, L1_ffn_w3, L1_ffn_sw1, L1_ffn_sw2, L1_ffn_sw3, L1_c, L1_wmod):

    def _L0_attn_ref(x, W_Q, W_K, W_V, W_O):
        import jax, jax.numpy as jnp
        import numpy as np
        import math
        D_MODEL = 256
        N_HEADS = 16
        D_HEAD = 128
        BATCH = 2
        SEQ = 256
        d_head = W_Q.shape[1]
        seq_len = x.shape[1]
        scale = 1.0 / math.sqrt(d_head)
        q = jnp.einsum('bsd,hed->bhse', x, W_Q)
        k = jnp.einsum('bsd,hed->bhse', x, W_K)
        v = jnp.einsum('bsd,hed->bhse', x, W_V)
        scores = jnp.einsum('bhse,bhme->bhsm', q, k) * scale
        causal = jnp.triu(jnp.ones((seq_len, seq_len), dtype=bool), k=1)
        scores = jnp.where(causal, jnp.float32(-1000000000.0), scores)
        pattern = jax.nn.softmax(scores, axis=-1)
        z = jnp.einsum('bhsm,bhme->bhse', pattern, v)
        out = jnp.einsum('bhse,hde->bsd', z, W_O)
        return out

    def _L0_ffn_ref(hidden_states, gate_w, gate_bias, fc1_w, fc2_w, w1, w2, shared_up_w, shared_down_w):
        import jax, jax.numpy as jnp
        import numpy as np
        H, LAT, INTER, E, G, TOPK_G, TOP_K = (256, 128, 128, 32, 4, 2, 8)
        SHARED_INTER = 512
        ROUTED_SCALE = 2.5
        B, S = (2, 128)

        def relu2(x):
            return jnp.square(jax.nn.relu(x))
        orig_shape = hidden_states.shape
        x = hidden_states.reshape(-1, H)
        T = x.shape[0]
        logits = jnp.einsum('th,eh->te', x.astype(jnp.float32), gate_w)
        scores = jax.nn.sigmoid(logits)
        sb = scores + gate_bias
        grp = sb.reshape(T, G, E // G)
        group_scores = jax.lax.top_k(grp, 2)[0].sum(-1)
        _, gidx = jax.lax.top_k(group_scores, TOPK_G)
        gmask = jax.nn.one_hot(gidx, G, dtype=sb.dtype).sum(1)
        masked = jnp.where(gmask[:, :, None] > 0, grp, -jnp.inf).reshape(T, E)
        _, topi = jax.lax.top_k(masked, TOP_K)
        wsel = jnp.take_along_axis(scores, topi, axis=1)
        wsel = wsel / wsel.sum(-1, keepdims=True) * ROUTED_SCALE
        cw = jnp.zeros((T, E), jnp.float32).at[jnp.arange(T)[:, None], topi].add(wsel)
        x_lat = x @ fc1_w.T
        h = relu2(jnp.einsum('tl,eil->eti', x_lat, w1))
        h = h * cw.T[:, :, None]
        y_lat = jnp.einsum('eti,eli->tl', h, w2)
        routed = y_lat @ fc2_w.T
        shared = relu2(x @ shared_up_w.T) @ shared_down_w.T
        return (shared + routed).reshape(orig_shape)

    def _L1_attn_ref(x, Wq, Wk, Wv, Wo, bo):
        import jax, jax.numpy as jnp
        import numpy as np
        B, S, D = (4, 256, 256)
        H = 16
        HD = D // H
        b, s, _ = x.shape
        q = (x @ Wq).reshape(b, s, H, HD).transpose(0, 2, 1, 3)
        k = (x @ Wk).reshape(b, s, H, HD).transpose(0, 2, 1, 3)
        v = (x @ Wv).reshape(b, s, H, HD).transpose(0, 2, 1, 3)
        scores = jnp.einsum('bhqd,bhkd->bhqk', q, k)
        causal = jnp.tril(jnp.ones((s, s), dtype=bool))
        scores = jnp.where(causal, scores, -jnp.inf)
        scale = 1.0 / np.sqrt(HD).astype(np.float32)
        attn = jax.nn.softmax(scores * scale, axis=-1)
        ctx = jnp.einsum('bhqk,bhkd->bqhd', attn, v).reshape(b, s, D)
        return ctx @ Wo + bo

    def _L1_ffn_ref(x, gate_w, expert_bias, w1, w2, w3, sw1, sw2, sw3):
        import jax, jax.numpy as jnp
        import numpy as np
        DIM = 256
        INTER = 176
        E = 16
        TOPK = 4
        G = 4
        TOPK_G = 2
        N_SHARED = 2
        ROUTE_SCALE = 1.0
        INIT_STD = 0.02
        B, S = (1, 256)
        b, s, d = x.shape
        T = b * s
        xf = x.reshape(T, d)
        scores = jax.nn.sigmoid(xf @ gate_w.T)
        original_scores = scores
        scores = scores + expert_bias
        sg = scores.reshape(T, G, E // G)
        group_scores = sg.max(axis=-1)
        _, gidx = jax.lax.top_k(group_scores, TOPK_G)
        gmask = jnp.zeros((T, G), bool).at[jnp.arange(T)[:, None], gidx].set(True)
        masked = jnp.where(gmask[:, :, None], sg, -jnp.inf).reshape(T, E)
        _, idx = jax.lax.top_k(masked, TOPK)
        w = jnp.take_along_axis(original_scores, idx, axis=1)
        w = w / jnp.sum(w, axis=-1, keepdims=True)
        w = w * ROUTE_SCALE
        cw = jnp.zeros((T, E), x.dtype).at[jnp.arange(T)[:, None], idx].add(w)
        h = jax.nn.silu(jnp.einsum('td,edh->teh', xf, w1)) * jnp.einsum('td,edh->teh', xf, w3)
        y = jnp.einsum('teh,ehd,te->td', h, w2, cw)
        z = jax.nn.silu(xf @ sw1) * (xf @ sw3) @ sw2
        return (y + z).reshape(b, s, d)
    x = L0_attn_x
    mod = (_silu(L0_c) @ L0_wmod).reshape(L0_c.shape[0], 6, 1, -1)
    sa, ca, ga, sb, cb, gb = (mod[:, 0], mod[:, 1], mod[:, 2], mod[:, 3], mod[:, 4], mod[:, 5])
    ga = (2 * (ga >= 0) - 1) * jnp.maximum(jnp.abs(ga), 0.25)
    gb = (2 * (gb >= 0) - 1) * jnp.maximum(jnp.abs(gb), 0.25)
    h = _layernorm(x, axis=-1) * (1 + ca) + sa
    x = x + ga * _L0_attn_ref(h, L0_attn_W_Q, L0_attn_W_K, L0_attn_W_V, L0_attn_W_O)
    h = _layernorm(x, axis=-1) * (1 + cb) + sb
    x = x + gb * _L0_ffn_ref(h, L0_ffn_gate_w, L0_ffn_gate_bias, L0_ffn_fc1_w, L0_ffn_fc2_w, L0_ffn_w1, L0_ffn_w2, L0_ffn_shared_up_w, L0_ffn_shared_down_w)
    mod = (_silu(L1_c) @ L1_wmod).reshape(L1_c.shape[0], 6, 1, -1)
    sa, ca, ga, sb, cb, gb = (mod[:, 0], mod[:, 1], mod[:, 2], mod[:, 3], mod[:, 4], mod[:, 5])
    ga = (2 * (ga >= 0) - 1) * jnp.maximum(jnp.abs(ga), 0.25)
    gb = (2 * (gb >= 0) - 1) * jnp.maximum(jnp.abs(gb), 0.25)
    h = _layernorm(x, axis=-1) * (1 + ca) + sa
    x = x + ga * _L1_attn_ref(h, L1_attn_Wq, L1_attn_Wk, L1_attn_Wv, L1_attn_Wo, L1_attn_bo)
    h = _layernorm(x, axis=-1) * (1 + cb) + sb
    x = x + gb * _L1_ffn_ref(h, L1_ffn_gate_w, L1_ffn_expert_bias, L1_ffn_w1, L1_ffn_w2, L1_ffn_w3, L1_ffn_sw1, L1_ffn_sw2, L1_ffn_sw3)
    return x

_drawn_inputs = setup_inputs


def setup_inputs(seed=0):
    import zlib

    import numpy as np

    out = dict(_drawn_inputs(seed))
    spreads = {'L1_ffn_expert_bias': (0.0, 0.8)}
    factors = {'L0_attn_W_Q': 8.0,
     'L0_attn_W_K': 8.0,
     'L0_attn_W_V': 8.0,
     'L0_attn_W_O': 8.0,
     'L0_ffn_gate_w': 8.0,
     'L0_ffn_gate_bias': 8.0,
     'L0_ffn_fc1_w': 8.0,
     'L0_ffn_fc2_w': 8.0,
     'L0_ffn_w1': 8.0,
     'L0_ffn_w2': 8.0,
     'L0_ffn_shared_up_w': 4.372,
     'L0_ffn_shared_down_w': 3.958,
     'L0_c': 3.965,
     'L0_wmod': 3.689,
     'L1_attn_Wq': 8.0,
     'L1_attn_Wk': 8.0,
     'L1_attn_Wv': 8.0,
     'L1_attn_Wo': 8.0,
     'L1_attn_bo': 200.0,
     'L1_ffn_gate_w': 8.0,
     'L1_ffn_w1': 8.0,
     'L1_ffn_w2': 8.0,
     'L1_ffn_w3': 8.0,
     'L1_ffn_sw1': 8.0,
     'L1_ffn_sw2': 8.0,
     'L1_ffn_sw3': 8.0,
     'L1_c': 7.079,
     'L1_wmod': 6.718}
    for name, (base, spread) in spreads.items():
        noise = np.random.default_rng([zlib.crc32(name.encode()), seed]).standard_normal(out[name].shape)
        drawn = base * np.exp(spread * noise) if base else spread * noise
        out[name] = jnp.asarray(drawn.astype(out[name].dtype))
    for name, factor in factors.items():
        out[name] = (out[name] * factor).astype(out[name].dtype)
    return out
```

```python
from contextlib import ExitStack

import concourse.bass as bass
from concourse import mybir
from concourse.alu_op_type import AluOpType as ALU

ACT = mybir.ActivationFunctionType
AX_X = mybir.AxisListType.X
F32 = mybir.dt.float32
F32R = mybir.dt.float32r
F16 = mybir.dt.float16
BF16 = mybir.dt.bfloat16

P = 128
T = 2048
D = 256
KC = D // P
NT = T // P
QB = 512
NB = T // QB
TPB = QB // P
EPS = 1e-5
MASKED = -1e30
LOWEST = -3e38


def f32(ap):
    return ap.bitcast(F32)


class Memory:

    def __init__(self, nc, ctx, prefix, reuse=False):
        self.nc, self.ctx, self.prefix, self.sems = nc, ctx, prefix, [] if reuse else None
        if reuse:
            ctx.callback(self.clear)

    def sb(self, name, shape, dt=F32):
        return self.ctx.enter_context(self.nc.sbuf_tensor(f"{self.prefix}_{name}", shape, dt))

    def ps(self, name, shape, dt=F32):
        return self.ctx.enter_context(self.nc.psum_tensor(f"{self.prefix}_{name}", shape, dt))

    def sem(self, name):
        if self.sems is None:
            return self.ctx.enter_context(self.nc.semaphore(f"{self.prefix}_{name}"))
        self.sems.append(self.nc.alloc_semaphore(name=f"{self.prefix}_{name}"))
        return self.sems[-1]

    def clear(self):
        self.nc.clear_and_free_semaphores(self.sems)
        self.nc.all_engine_barrier()



def setup_phase(nc, x_dram, c_dram, wmod_dram, x, ident, ident_bf, ident_h, mask_q, mask_t, coef, gate):
    with ExitStack() as ctx:
        m = Memory(nc, ctx, "set")
        c_col = m.sb("c_col", [P, 2, KC])
        sig = m.sb("sig", [P, 2, KC])
        silu = m.sb("silu", [P, 2, KC])
        silu_bc = m.sb("silu_bc", [P, 2, KC, P])
        wmod = m.sb("wmod", [P, 2, KC, 6 * D])
        sign = m.sb("sign", [P, 2, 2, D])
        size = m.sb("size", [P, 2, 2, D])
        ps_col = m.ps("ps_col", [P, 2, 512])
        ps_gate = m.ps("ps_gate", [P, 2, 2, D])
        loaded, x_loaded, made = m.sem("loaded"), m.sem("x_loaded"), m.sem("made")
        sig_ready, silu_ready = m.sem("sig_ready"), m.sem("silu_ready")
        cols_ready, gates_ready, dve_done = m.sem("cols_ready"), m.sem("gates_ready"), m.sem("dve_done")
        block = ctx.enter_context(nc.Block())

        @block.sync
        def _(sp):
            for layer in range(2):
                sp.dma_start(c_col[:, layer], c_dram[layer]).then_inc(loaded, 16)
            for layer in range(2):
                sp.dma_start(wmod[:, layer], wmod_dram[layer].rearrange("(k p) n -> p k n", p=P)).then_inc(loaded, 16)
            xt = x_dram.rearrange("a (t p) d -> p (a t) d", p=P)
            for b in range(NB):
                sp.dma_start(x[:, b * TPB:(b + 1) * TPB], xt[:, b * TPB:(b + 1) * TPB]).then_inc(x_loaded, 16)
            sp.wait_ge(x_loaded, 16 * NB)

        @block.gpsimd
        def _(pool):
            nc.gpsimd.memset(ident[:], 0.0).then_inc(made, 1)
            nc.gpsimd.memset(mask_q[:], 0.0).then_inc(made, 1)
            nc.gpsimd.memset(mask_t[:], 0.0).then_inc(made, 1)
            pool.wait_ge(made, 3)
            nc.gpsimd.affine_select(out=ident[:], in_=ident[:], compare_op=ALU.not_equal, fill=1.0, base=0,
                                    pattern=[[-1, P]], channel_multiplier=1).then_inc(made, 1)
            nc.gpsimd.affine_select(out=mask_q[:], in_=mask_q[:], compare_op=ALU.is_ge, fill=MASKED, base=0,
                                    pattern=[[-1, P]], channel_multiplier=1).then_inc(made, 1)
            nc.gpsimd.affine_select(out=mask_t[:], in_=mask_t[:], compare_op=ALU.is_ge, fill=MASKED, base=0,
                                    pattern=[[1, P]], channel_multiplier=-1).then_inc(made, 1)

        @block.scalar
        def _(act):
            act.wait_ge(loaded, 64)
            nc.scalar.activation(sig[:], c_col[:], ACT.Sigmoid).then_inc(sig_ready, 1)

        @block.vector
        def _(dve):
            dve.wait_ge(made, 6)
            nc.vector.tensor_copy(ident_bf[:], ident[:]).then_inc(dve_done, 1)
            nc.vector.tensor_copy(ident_h[:], ident[:]).then_inc(dve_done, 1)
            dve.wait_ge(sig_ready, 1)
            nc.vector.tensor_tensor(silu[:], c_col[:], sig[:], ALU.mult).then_inc(silu_ready, 1)
            dve.wait_ge(silu_ready, 1)
            nc.vector.tensor_copy(silu_bc[:], silu[:].unsqueeze(3).broadcast_to([P, 2, KC, P])).then_inc(silu_ready, 1)
            dve.wait_ge(cols_ready, 1)
            for layer in range(2):
                nc.vector.tensor_copy(coef[:, layer], ps_col[:, layer, 0:8]).then_inc(dve_done, 1)
            dve.wait_ge(dve_done, 4)
            for layer in range(2):
                for k in range(2):
                    c = coef[:, layer, 4 * k + 2:4 * k + 4]
                    nc.vector.tensor_scalar(c, c, 1.0, None, ALU.add).then_inc(dve_done, 1)
            dve.wait_ge(gates_ready, 1)
            nc.vector.tensor_scalar(sign[:], ps_gate[:], 0.0, 2.0, ALU.is_ge, ALU.mult).then_inc(dve_done, 1)
            nc.vector.tensor_scalar(size[:], ps_gate[:], -1.0, None, ALU.mult).then_inc(dve_done, 1)
            dve.wait_ge(dve_done, 10)
            nc.vector.tensor_tensor(size[:], size[:], ps_gate[:], ALU.max).then_inc(dve_done, 1)
            dve.wait_ge(dve_done, 11)
            nc.vector.tensor_scalar(size[:], size[:], 0.25, None, ALU.max).then_inc(dve_done, 1)
            dve.wait_ge(dve_done, 12)
            nc.vector.scalar_tensor_tensor(gate[:], sign[:], -1.0, size[:], ALU.add, ALU.mult).then_inc(dve_done, 1)

        @block.tensor
        def _(pe):
            pe.wait_ge(silu_ready, 1)
            chunk = [0, 1, 2, 3, 6, 7, 8, 9]
            for layer in range(2):
                for j, c in enumerate(chunk):
                    for k in range(KC):
                        last = nc.tensor.matmul(ps_col[:, layer, j:j + 1], wmod[:, layer, k, c * P:(c + 1) * P],
                                                silu[:, layer, k:k + 1], start=(k == 0), stop=(k == KC - 1))
            last.then_inc(cols_ready, 1)
            pe.wait_ge(silu_ready, 2)
            for layer in range(2):
                for g in range(2):
                    for k in range(KC):
                        last = nc.tensor.matmul(ps_gate[:, layer, g], silu_bc[:, layer, k],
                                                wmod[:, layer, k, (2 + 3 * g) * D:(3 + 3 * g) * D],
                                                start=(k == 0), stop=(k == KC - 1))
            last.then_inc(gates_ready, 1)



def norm_phase(nc, name, x, ident, shift_scale, h_hi, h_lo):
    with ExitStack() as ctx:
        m = Memory(nc, ctx, name)
        stats = m.sb("stats", [P, NT, 6])
        mv = m.sb("mv", [P, NT, 2])
        std = m.sb("std", [P, NT])
        rstd = m.sb("rstd", [P, NT])
        xn = m.sb("xn", [P, NT, D])
        h32 = m.sb("h32", [P, 2, QB])
        ps = m.ps("ps", [P, 4, QB])
        stat_done, std_ready, xn_ready = m.sem("stat_done"), m.sem("std_ready"), m.sem("xn_ready")
        turned, h32_ready, hi_ready, lo_ready = m.sem("turned"), m.sem("h32_ready"), m.sem("hi_ready"), m.sem("lo_ready")
        block = ctx.enter_context(nc.Block())
        units = [(b, k) for b in range(NB) for k in range(KC)]

        @block.vector
        def _(dve):
            for t in range(NT):
                nc.vector.bn_stats(stats[:, t], x[:, t]).then_inc(stat_done, 1)
            dve.wait_ge(stat_done, NT)
            for t in range(NT):
                nc.vector.bn_aggr(mv[:, t], stats[:, t]).then_inc(stat_done, 1)
            dve.wait_ge(stat_done, 2 * NT)
            nc.vector.tensor_scalar(rstd[:], mv[:, :, 1], EPS, None, ALU.add).then_inc(stat_done, 1)
            dve.wait_ge(std_ready, 1)
            nc.vector.reciprocal(rstd[:], std[:]).then_inc(stat_done, 1)
            dve.wait_ge(stat_done, 2 * NT + 2)

            def normalize(b):
                for t in range(b * TPB, (b + 1) * TPB):
                    nc.vector.tensor_scalar(xn[:, t], x[:, t], mv[:, t, 0:1], rstd[:, t:t + 1],
                                            ALU.subtract, ALU.mult).then_inc(xn_ready, 1)

            normalize(0)
            for n, (b, k) in enumerate(units):
                if k == 0 and b + 1 < NB:
                    normalize(b + 1)
                dve.wait_ge(hi_ready, n + 1)
                nc.vector.tensor_tensor(h_lo[:, k, b * QB:(b + 1) * QB], h32[:, n % 2],
                                        f32(h_hi[:, k, b * QB:(b + 1) * QB]), ALU.subtract).then_inc(lo_ready, 1)

        @block.tensor
        def _(pe):
            for n, (b, k) in enumerate(units):
                pe.wait_ge(xn_ready, (b + 1) * TPB)
                if n >= 4:
                    pe.wait_ge(h32_ready, n - 3)
                for j in range(TPB):
                    last = nc.tensor.transpose(ps[:, n % 4, j * P:(j + 1) * P],
                                               xn[:, b * TPB + j, k * P:(k + 1) * P], ident[:])
                last.then_inc(turned, 1)

        @block.scalar
        def _(act):
            act.wait_ge(stat_done, 2 * NT + 1)
            nc.scalar.activation(std[:], rstd[:], ACT.Sqrt).then_inc(std_ready, 1)
            for n, (b, k) in enumerate(units):
                act.wait_ge(turned, n + 1)
                if n >= 2:
                    act.wait_ge(lo_ready, n - 1)
                nc.scalar.activation(h32[:, n % 2], ps[:, n % 4], ACT.Identity,
                                     bias=shift_scale[:, k:k + 1], scale=shift_scale[:, 2 + k:3 + k]).then_inc(h32_ready, 1)
                act.wait_ge(h32_ready, n + 1)
                nc.scalar.activation(h_hi[:, k, b * QB:(b + 1) * QB], h32[:, n % 2], ACT.Copy).then_inc(hi_ready, 1)



HEADS0 = 16
DH0 = 128
WO_SCALE = 64.0
UNITS = [(qb, kt) for qb in range(NB) for kt in range(TPB * (qb + 1))]
MAXES = [(qt, kb) for qt in range(NT) for kb in range(qt // TPB + 1)]


def first_col(qb, kt):
    return P * max(0, kt - TPB * qb)


def attention0_steps():
    def prep(h):
        items = [("QK", h, which, b) for b in range(NB) for which in "KQ"]
        if h % 2 == 0:
            items += [("V", h, tp) for tp in range(NT // 2)]
        return items + [("MAX", h, qt, kb) for qt, kb in MAXES]

    def cost(item):
        return 0.4 if item[0] == "MAX" else 1.3

    start = [("LOADW", -1), ("LOADW", 0), ("SPLIT", -1), ("LOADW", 1), ("SPLIT", 0), ("LOADW", 2)]
    start += prep(0) + [("COMBINE", 0), ("MROW", 0)]
    periods = []
    late = []
    for h in range(HEADS0):
        steps = []

        def tick():
            nonlocal late
            due = [s for n, s in late if n == 0]
            late = [(n - 1, s) for n, s in late if n > 0]
            steps.extend(due)

        ahead = prep(h + 1) if h + 1 < HEADS0 else []
        whole = sum(map(cost, ahead))
        spent = 0.0
        for u, (qb, kt) in enumerate(UNITS):
            steps.append(("S", h, u))
            while ahead and spent < whole * (u + 1) / 34:
                spent += cost(ahead[0])
                steps.append(ahead.pop(0))
            if h + 1 < HEADS0:
                if u == 35:
                    steps.append(("COMBINE", h + 1))
                if u == 36:
                    steps.append(("MROW", h + 1))
                if u == 14:
                    steps.append(("SPLIT", h + 1))
                    steps.append(("LOADW", h + 3))
            steps.append(("LO", h, u))
            tick()
            late.append((1, ("PV", h, u)))
            if kt == TPB * (qb + 1) - 1:
                late += [(1, ("ZNORM", h, qb)), (2, ("ZLO", h, qb)), (3, ("ZTURN", h, qb)),
                         (5, ("WO", h, qb, 0)), (5, ("WO", h, qb, 1))]
            if h % 2 == 0 and u == 4:
                steps.append(("VCOPY", h + 1))
        periods.append(steps)
    tail = []
    while late:
        tail += [s for n, s in late if n == 0]
        late = [(n - 1, s) for n, s in late if n > 0]
    return start, periods, tail


STREAMS = {"S": "S", "QK": "AUX", "V": "AUX", "MAX": "AUX", "WO": "AUX", "ZTURN": "T", "MROW": "T",
           "ZNORM": "Z", "SPLIT": "W", "COMBINE": "C", "VCOPY": "VC"}
HI_STREAM = {"QK": "HI", "V": "HI"}


def number_steps(steps, streams):
    place, length = {}, {}
    for s in steps:
        if s[0] in streams:
            stream = streams[s[0]]
            place[s] = length.get(stream, 0)
            length[stream] = place[s] + 1
    return place, length


def attention0_phase(nc, w_even, w_odd, x, h_hi, h_lo, ident, ident_bf, ident_h, mask_q, mask_t, gate_row):
    start, periods, tail = attention0_steps()
    place, _ = number_steps(start + sum(periods, []) + tail, STREAMS)
    hi_place, _ = number_steps(start + sum(periods, []), HI_STREAM)
    one_round = number_steps(periods[1] + periods[2], STREAMS)[1] | number_steps(periods[1] + periods[2], HI_STREAM)[1]
    for a in (1, 2):
        for h in range(a, HEADS0 - 1, 2):
            assert [(s[0], s[1] - h + a, *s[2:]) for s in periods[h]] == periods[a]
    scale = DH0 ** -0.5
    SB, AB, PR, EB = 2, 3, 4, 2
    assert one_round["AUX"] % AB == 0 and len(UNITS) % PR == 0

    with ExitStack() as ctx:
        m = Memory(nc, ctx, "a0", reuse=True)
        stage = [m.sb("stage_even", [P, 768]), m.sb("stage_odd", [P, 1280])]
        wqk_hi = [m.sb(f"wqk_hi{i}", [P, KC, 2, P], F32R) for i in range(2)]
        wqk_lo = [m.sb(f"wqk_lo{i}", [P, KC, 2, P], F32R) for i in range(2)]
        wv_hi = m.sb("wv_hi", [P, KC, 2 * P], F32R)
        wv_lo = m.sb("wv_lo", [P, KC, 2 * P], F32R)
        wo_gated = m.sb("wo_gated", [P, D])
        wo_hi = [m.sb(f"wo_hi{i}", [P, D], F16) for i in range(2)]
        wo_lo = [m.sb(f"wo_lo{i}", [P, D], F16) for i in range(2)]
        gate64 = m.sb("gate64", [P, D])
        q_hi, q_lo = m.sb("q_hi", [P, 2, T], F16), m.sb("q_lo", [P, 2, T], F16)
        k_hi, k_lo = m.sb("k_hi", [P, 2, T], F16), m.sb("k_lo", [P, 2, T], F16)
        EVEN, ODD, NEXT_ODD = range(3)
        v_hi = [m.sb(f"v_hi{i}", [P, NT, P + 2], F16) for i in range(3)]
        v_lo = [m.sb(f"v_lo{i}", [P, NT, P], F16) for i in range(3)]
        partial = m.sb("partial", [P, NT, NB])
        neg_max = m.sb("neg_max", [P, NT])
        neg_max_t = m.sb("neg_max_t", [NT, P], F16)
        neg_row = m.sb("neg_row", [1, 2, T], F16)
        ones = m.sb("ones", [1, P], F16)
        p32 = m.sb("p32", [P, 2, QB])
        p_hi, p_lo = m.sb("p_hi", [P, PR, QB], F16), m.sb("p_lo", [P, PR, QB], F16)
        rden = m.sb("rden", [P, 2, 2])
        zn = m.sb("zn", [P, TPB, P])
        z_hi, z_lo = m.sb("z_hi", [P, TPB, P], F16), m.sb("z_lo", [P, TPB, P], F16)
        z_t = m.sb("z_t", [P, 2, TPB, P], F16)
        ps_s = m.ps("ps_s", [P, SB, QB])
        ps_z = m.ps("ps_z", [P, 2, 2, 256])
        ps_t = m.ps("ps_t", [P, QB])
        ps_aux = m.ps("ps_aux", [P, AB, QB])

        const_ready = m.sem("const_ready")
        w_loaded = [m.sem("w_loaded_even"), m.sem("w_loaded_odd")]
        gated, w_ready = m.sem("gated"), m.sem("w_ready")
        w_hi_ready = [m.sem("w_hi_ready_even"), m.sem("w_hi_ready_odd")]
        s_filled, s_exped, p32_ready, p_lo_ready = m.sem("s_filled"), m.sem("s_exped"), m.sem("p32_ready"), m.sem("p_lo_ready")
        pv_done = m.sem("pv_done")
        aux_filled, aux_hi, aux_free = m.sem("aux_filled"), m.sem("aux_hi"), m.sem("aux_free")
        max_ready, row_loaded = m.sem("max_ready"), m.sem("row_loaded")
        t_filled, t_free = m.sem("t_filled"), m.sem("t_free")
        rden_ready, z_free, z_hi_ready, z_lo_ready = m.sem("rden_ready"), m.sem("z_free"), m.sem("z_hi_ready"), m.sem("z_lo_ready")
        v_copied = m.sem("v_copied")
        block = ctx.enter_context(nc.Block())

        def whole_program(eng, step):
            def in_line(n, stream):
                return n

            for s in start + periods[0]:
                step(s, in_line, 0)
            with eng.Fori(0, (HEADS0 - 2) // 2) as i:
                for s in periods[1] + periods[2]:
                    step(s, lambda n, stream: n + i * one_round[stream], i)
            for s in periods[HEADS0 - 1] + tail:
                step(s, in_line, 0)

        def weight_set(period):
            return (1, (period + 1) // 2) if period % 2 else (0, period // 2)

        def turned_before(h, qb):
            if (h, qb) == (0, 0):
                return 1
            hb, qbb = (h, qb - 1) if qb else (h - 1, NB - 1)
            return place["ZTURN", hb, qbb] + 1

        def pv(h, u):
            return place["S", h, u]

        @block.sync
        def _(sp):
            def step(s, at, i):
                kind, h = s[0], s[1]
                if kind == "LOADW":
                    parity, j = weight_set(h)
                    if h > 0:
                        sp.wait_ge(w_ready, at(place["SPLIT", h - 2], "W") + 1)
                    src = w_odd if parity else w_even
                    sp.dma_start(stage[parity][:], src[i + j]).then_inc(w_loaded[parity], 16)
                elif kind == "MROW":
                    sp.wait_ge(t_free, at(place[s], "T") + 2)
                    sp.dma_start(neg_row[0:1, h % 2].rearrange("a (t p) -> a t p", p=P), neg_max_t[:]).then_inc(row_loaded, 16)

            whole_program(sp, step)
            for parity in range(2):
                sp.wait_ge(w_loaded[parity], 16 * (HEADS0 // 2 + 1 + parity))

        @block.gpsimd
        def _(pool):
            for i in range(3):
                nc.gpsimd.memset(v_hi[i][:, :, P:P + 2], 1.0).then_inc(const_ready, 1)
            nc.gpsimd.memset(ones[:], 1.0).then_inc(const_ready, 1)
            nc.gpsimd.memset(partial[:], LOWEST).then_inc(const_ready, 1)

        @block.tensor
        def _(pe):
            pe.wait_ge(const_ready, 5)
            pe.sem_inc(pv_done, PR)

            def step(s, at, i):
                kind, h = s[0], s[1]
                if kind in ("QK", "V", "MAX", "WO"):
                    n = place[s]
                    pe.wait_ge(aux_free, at(n, "AUX") + 1)
                    bank = ps_aux[:, n % AB]
                    par = (h + 1) % 2
                if kind == "QK":
                    which, b = s[2:]
                    if b == 0:
                        pe.wait_ge(w_ready, at(place["SPLIT", h - 1], "W") + 1)
                    col = "QK".index(which)
                    tok = slice(b * QB, (b + 1) * QB)
                    for k in range(KC):
                        for w, act in ((wqk_hi, h_hi), (wqk_hi, h_lo), (wqk_lo, h_hi)):
                            last = nc.tensor.matmul(bank, w[par][:, k, col], act[:, k, tok],
                                                    start=(k == 0 and w is wqk_hi and act is h_hi),
                                                    stop=(k == KC - 1 and w is wqk_lo))
                    last.then_inc(aux_filled, 1)
                elif kind == "V":
                    for j in range(2):
                        tok = slice((2 * s[2] + j) * P, (2 * s[2] + j + 1) * P)
                        for k in range(KC):
                            for act, w in ((h_hi, wv_hi), (h_hi, wv_lo), (h_lo, wv_hi)):
                                last = nc.tensor.matmul(bank[:, j * 256:(j + 1) * 256], act[:, k, tok], w[:, k],
                                                        start=(k == 0 and act is h_hi and w is wv_hi),
                                                        stop=(k == KC - 1 and act is h_lo))
                    last.then_inc(aux_filled, 1)
                elif kind == "MAX":
                    qt, kb = s[2:]
                    if kb == 0:
                        pe.wait_ge(aux_hi, at(hi_place["QK", h, "Q", qt // TPB], "HI") + 1)
                    diagonal = kb == qt // TPB
                    n = min(QB, (qt + 1) * P - kb * QB)
                    nc_last = nc.tensor.matmul(bank[:, 0:n], q_hi[:, h % 2, qt * P:(qt + 1) * P],
                                               k_hi[:, h % 2, kb * QB:kb * QB + n], start=True, stop=not diagonal)
                    if diagonal:
                        nc_last = nc.tensor.matmul(bank[:, n - P:n], ident_bf[:], mask_q[:], start=False, stop=True)
                    nc_last.then_inc(aux_filled, 1)
                elif kind == "WO":
                    qb, pair = s[2:]
                    pe.wait_ge(t_free, at(place["ZTURN", h, qb], "T") + 2)
                    for j in range(2):
                        t = 2 * pair + j
                        for a, w in ((0, wo_hi), (0, wo_lo), (1, wo_hi)):
                            last = nc.tensor.matmul(bank[:, j * D:(j + 1) * D], z_t[:, a, t], w[h % 2][:],
                                                    start=(a == 0 and w is wo_hi), stop=(a == 1))
                    last.then_inc(aux_filled, 1)
                elif kind == "S":
                    u = s[2]
                    qb, kt = UNITS[u]
                    if u == 0:
                        pe.wait_ge(aux_free, at(place["MAX", h, NT - 1, NB - 1], "AUX") + 1 + AB)
                        pe.wait_ge(row_loaded, 16 * (at(place["COMBINE", h], "C") + 1))
                        if h % 2:
                            pe.wait_ge(v_copied, 2 * (at(place["VCOPY", h], "VC") + 1))
                    pe.wait_ge(s_exped, at(place[s], "S") + 1)
                    c = first_col(qb, kt)
                    out = ps_s[:, u % SB, c:QB]
                    keys = slice(kt * P, (kt + 1) * P)
                    q = slice(qb * QB + c, (qb + 1) * QB)
                    nc.tensor.matmul(out, k_hi[:, h % 2, keys], q_hi[:, h % 2, q], start=True, stop=False)
                    nc.tensor.matmul(out, k_hi[:, h % 2, keys], q_lo[:, h % 2, q], start=False, stop=False)
                    nc.tensor.matmul(out, k_lo[:, h % 2, keys], q_hi[:, h % 2, q], start=False, stop=False)
                    diagonal = kt >= TPB * qb
                    last = nc.tensor.matmul(out, ones[0:1, :], neg_row[0:1, h % 2, q], start=False, stop=not diagonal)
                    if diagonal:
                        last = nc.tensor.matmul(ps_s[:, u % SB, c:c + P], ident_bf[:], mask_t[:], start=False, stop=True)
                    last.then_inc(s_filled, 1)
                elif kind == "PV":
                    u = s[2]
                    qb, kt = UNITS[u]
                    if kt == 0:
                        pe.wait_ge(z_free, at(place["ZNORM", h, qb], "Z") + 1)
                    pe.wait_ge(p_lo_ready, at(pv(h, u), "S") + 1 + EB)
                    v = ODD if h % 2 else EVEN
                    for t in range(first_col(qb, kt) // P, TPB):
                        q = slice(t * P, (t + 1) * P)
                        end = t % 2 == 1 and kt == TPB * qb + t
                        z = ps_z[:, t // 2, t % 2]
                        nc.tensor.matmul(z[:, 0:P + 1], p_hi[:, u % PR, q], v_hi[v][:, kt, 0:P + 1], start=(kt == 0 and t % 2 == 0), stop=False)
                        nc.tensor.matmul(z[:, 0:P], p_hi[:, u % PR, q], v_lo[v][:, kt], start=False, stop=False)
                        last = nc.tensor.matmul(z[:, 0:P + 1], p_lo[:, u % PR, q], v_hi[v][:, kt, 0:P + 1], start=False, stop=end)
                    last.then_inc(pv_done, 1)
                elif kind == "ZTURN":
                    qb = s[2]
                    pe.wait_ge(t_free, at(place[s], "T") + 1)
                    pe.wait_ge(z_lo_ready, at(place["ZNORM", h, qb], "Z") + 1)
                    pt = ps_t[:].bitcast(F16).rearrange("p (a t n) -> p a t n", a=2, t=TPB)
                    for a, z in enumerate((z_hi, z_lo)):
                        for t in range(TPB):
                            last = nc.tensor.transpose(pt[:, a, t], z[:, t], ident_h[:])
                    last.then_inc(t_filled, 1)
                elif kind == "MROW":
                    pe.wait_ge(t_free, at(place[s], "T") + 1)
                    pe.wait_ge(max_ready, at(place["COMBINE", h], "C") + 1)
                    nc.tensor.transpose(ps_t[0:NT, 0:P], neg_max[:], ident[:]).then_inc(t_filled, 1)

            whole_program(pe, step)

        @block.scalar
        def _(act):
            act.sem_inc(s_exped, SB)
            act.sem_inc(t_free, 1)

            def step(s, at, i):
                kind, h = s[0], s[1]
                if kind == "SPLIT":
                    parity, j = weight_set(h)
                    act.wait_ge(w_loaded[parity], 16 * (i + j + 1))
                    w = stage[parity]
                    if h >= 2:
                        act.wait_ge(aux_filled, at(place["WO", h - 2, NB - 1, 1], "AUX") + 1)
                    elif h == 1:
                        act.wait_ge(aux_filled, place["V", 0, NT // 2 - 1] + 1)
                    nc.scalar.activation(wqk_hi[parity][:].rearrange("p k c n -> p (k c n)"), w[:, 0:512], ACT.Copy).then_inc(w_hi_ready[parity], 1)
                    if parity:
                        nc.scalar.activation(wv_hi[:].rearrange("p k n -> p (k n)"), w[:, 512:1024], ACT.Copy).then_inc(w_hi_ready[parity], 1)
                    act.wait_ge(gated, at(place[s], "W") + 2)
                    nc.scalar.activation(wo_hi[parity][:], wo_gated[:], ACT.Copy).then_inc(w_hi_ready[parity], 1)
                elif kind == "QK":
                    which, b = s[2:]
                    n = place[s]
                    act.wait_ge(aux_filled, at(n, "AUX") + 1)
                    out = (q_hi if which == "Q" else k_hi)[:, h % 2, b * QB:(b + 1) * QB]
                    nc.scalar.activation(out, ps_aux[:, n % AB], ACT.Copy).then_inc(aux_hi, 1)
                elif kind == "V":
                    n = place[s]
                    act.wait_ge(aux_filled, at(n, "AUX") + 1)
                    src = ps_aux[:, n % AB].rearrange("p (t h e) -> p t h e", t=2, h=2)
                    t = slice(2 * s[2], 2 * s[2] + 2)
                    nc.scalar.activation(v_hi[EVEN][:, t, 0:P], src[:, :, 0], ACT.Copy)
                    if s[2] == 0 and h >= 2:
                        act.wait_ge(v_copied, 2 * at(place["VCOPY", h - 1], "VC") + 2)
                    nc.scalar.activation(v_hi[NEXT_ODD][:, t, 0:P], src[:, :, 1], ACT.Copy).then_inc(aux_hi, 1)
                elif kind == "S":
                    u = s[2]
                    qb, kt = UNITS[u]
                    c = first_col(qb, kt)
                    n = at(place[s], "S")
                    act.wait_ge(s_filled, n + 1)
                    act.wait_ge(p_lo_ready, n + 1)
                    act.wait_ge(pv_done, n + 1)
                    nc.scalar.activation(p32[:, u % 2, c:QB], ps_s[:, u % SB, c:QB], ACT.Exp, scale=scale).then_inc(p32_ready, 1)
                    nc.scalar.activation(p_hi[:, u % PR, c:QB], ps_s[:, u % SB, c:QB], ACT.Exp, scale=scale).then_inc(s_exped, 1)
                elif kind == "ZLO":
                    n = at(place["ZNORM", h, s[2]], "Z")
                    act.wait_ge(z_free, n + 2)
                    act.wait_ge(t_filled, at(turned_before(h, s[2]), "T"))
                    nc.scalar.activation(z_hi[:], zn[:], ACT.Copy).then_inc(z_hi_ready, 1)
                elif kind == "ZTURN":
                    n = at(place[s], "T")
                    act.wait_ge(t_filled, n + 1)
                    if (h, s[2]) != (0, 0):
                        hb, qbb = (h, s[2] - 1) if s[2] else (h - 1, NB - 1)
                        act.wait_ge(aux_filled, at(place["WO", hb, qbb, 1], "AUX") + 1)
                    nc.scalar.activation(z_t[:].rearrange("p a t n -> p (a t n)"), ps_t[:].bitcast(F16), ACT.Copy).then_inc(t_free, 1)
                elif kind == "MROW":
                    n = at(place[s], "T")
                    act.wait_ge(t_filled, n + 1)
                    if h > 0:
                        act.wait_ge(row_loaded, 16 * at(place["COMBINE", h], "C"))
                    nc.scalar.activation(neg_max_t[:], ps_t[0:NT, 0:P], ACT.Copy).then_inc(t_free, 1)

            whole_program(act, step)

        @block.vector
        def _(dve):
            nc.vector.tensor_scalar(gate64[:], gate_row, WO_SCALE, None, ALU.mult).then_inc(gated, 1)
            dve.sem_inc(aux_free, AB)
            dve.sem_inc(z_free, 1)
            dve.sem_inc(p_lo_ready, EB)
            dve.wait_ge(gated, 1)
            dve.wait_ge(const_ready, 5)

            def step(s, at, i):
                kind, h = s[0], s[1]
                if kind == "SPLIT":
                    parity, j = weight_set(h)
                    n = at(place[s], "W")
                    dve.wait_ge(w_loaded[parity], 16 * (i + j + 1))
                    w = stage[parity]
                    if h >= 0:
                        dve.wait_ge(w_ready, n)
                    nc.vector.tensor_tensor(wo_gated[:], w[:, -D:], gate64[:], ALU.mult).then_inc(gated, 1)
                    dve.wait_ge(w_hi_ready[parity], (2 + parity) * (i + j + 1))
                    nc.vector.tensor_tensor(wqk_lo[parity][:].rearrange("p k c n -> p (k c n)"), w[:, 0:512],
                                            f32(wqk_hi[parity][:]).rearrange("p k c n -> p (k c n)"), ALU.subtract)
                    if parity:
                        nc.vector.tensor_tensor(wv_lo[:].rearrange("p k n -> p (k n)"), w[:, 512:1024],
                                                f32(wv_hi[:]).rearrange("p k n -> p (k n)"), ALU.subtract)
                    nc.vector.tensor_tensor(wo_lo[parity][:], wo_gated[:], wo_hi[parity][:], ALU.subtract).then_inc(w_ready, 1)
                elif kind == "QK":
                    which, b = s[2:]
                    n = place[s]
                    dve.wait_ge(aux_hi, at(hi_place[s], "HI") + 1)
                    hi, lo = (q_hi, q_lo) if which == "Q" else (k_hi, k_lo)
                    tok = slice(b * QB, (b + 1) * QB)
                    nc.vector.tensor_tensor(lo[:, h % 2, tok], ps_aux[:, n % AB], hi[:, h % 2, tok], ALU.subtract).then_inc(aux_free, 1)
                elif kind == "V":
                    n = place[s]
                    dve.wait_ge(aux_hi, at(hi_place[s], "HI") + 1)
                    src = ps_aux[:, n % AB].rearrange("p (t h e) -> p t h e", t=2, h=2)
                    t = slice(2 * s[2], 2 * s[2] + 2)
                    nc.vector.tensor_tensor(v_lo[EVEN][:, t], src[:, :, 0], v_hi[EVEN][:, t, 0:P], ALU.subtract)
                    nc.vector.tensor_tensor(v_lo[NEXT_ODD][:, t], src[:, :, 1], v_hi[NEXT_ODD][:, t, 0:P], ALU.subtract).then_inc(aux_free, 1)
                elif kind == "MAX":
                    qt, kb = s[2:]
                    n = place[s]
                    dve.wait_ge(aux_filled, at(n, "AUX") + 1)
                    if (qt, kb) == (0, 0) and h > 0:
                        dve.wait_ge(max_ready, at(place["COMBINE", h], "C"))
                    cols = min(QB, (qt + 1) * P - kb * QB)
                    nc.vector.tensor_reduce(partial[:, qt, kb:kb + 1], ps_aux[:, n % AB, 0:cols], AX_X, ALU.max).then_inc(aux_free, 1)
                elif kind == "COMBINE":
                    n = at(place[s], "C")
                    dve.wait_ge(aux_free, at(place["MAX", h, NT - 1, NB - 1], "AUX") + 1 + AB)
                    if h > 0:
                        dve.wait_ge(t_filled, at(place["MROW", h - 1], "T") + 1)
                    nc.vector.tensor_reduce(neg_max[:], partial[:], AX_X, ALU.max, negate=True).then_inc(max_ready, 1)
                elif kind == "WO":
                    qb, pair = s[2:]
                    n = place[s]
                    dve.wait_ge(aux_filled, at(n, "AUX") + 1)
                    xs = x[:, qb * TPB + 2 * pair:qb * TPB + 2 * pair + 2].rearrange("p t d -> p (t d)")
                    nc.vector.scalar_tensor_tensor(xs, ps_aux[:, n % AB], 1.0 / WO_SCALE, xs, ALU.mult, ALU.add).then_inc(aux_free, 1)
                elif kind == "LO":
                    u = s[2]
                    n = at(place["S", h, u], "S")
                    c = first_col(*UNITS[u])
                    dve.wait_ge(s_exped, n + 1 + SB)
                    nc.vector.tensor_tensor(p_lo[:, u % PR, c:QB], p32[:, u % 2, c:QB], p_hi[:, u % PR, c:QB], ALU.subtract).then_inc(p_lo_ready, 1)
                elif kind == "ZNORM":
                    qb = s[2]
                    n = at(place[s], "Z")
                    dve.wait_ge(pv_done, at(pv(h, UNITS.index((qb, TPB * (qb + 1) - 1))), "S") + 1 + PR)
                    if (h, qb) != (0, 0):
                        dve.wait_ge(z_lo_ready, n)
                    nc.vector.reciprocal(rden[:], ps_z[:, :, :, P]).then_inc(rden_ready, 1)
                    dve.wait_ge(rden_ready, n + 1)
                    nc.vector.tensor_tensor(zn[:].rearrange("p (a b) n -> p a b n", a=2), ps_z[:, :, :, 0:P],
                                            rden[:].unsqueeze(3).broadcast_to([P, 2, 2, P]), ALU.mult).then_inc(z_free, 1)
                elif kind == "ZLO":
                    n = at(place["ZNORM", h, s[2]], "Z")
                    dve.wait_ge(z_hi_ready, n + 1)
                    nc.vector.tensor_tensor(z_lo[:], zn[:], z_hi[:], ALU.subtract).then_inc(z_lo_ready, 1)

                elif kind == "VCOPY":
                    dve.wait_ge(aux_free, at(place["V", h - 1, NT // 2 - 1], "AUX") + 1 + AB)
                    if h > 2:
                        dve.wait_ge(pv_done, at(pv(h - 2, len(UNITS) - 1), "S") + 1 + PR)
                    nc.vector.tensor_copy(v_hi[ODD][:, :, 0:P], v_hi[NEXT_ODD][:, :, 0:P]).then_inc(v_copied, 1)
                    nc.vector.tensor_copy(v_lo[ODD][:], v_lo[NEXT_ODD][:]).then_inc(v_copied, 1)

            whole_program(dve, step)



def routing_phase(nc, name, gw_dram, bias_dram, cw_dram, h_hi, h_lo, ident_h, experts, groups, group_best,
                  top_k, route_scale, always):
    E, G, A = experts, groups, always
    per = E // G
    with ExitStack() as ctx:
        m = Memory(nc, ctx, name)
        gw = m.sb("gw", [P, KC, E])
        gw_x = m.sb("gw_x", [P, KC, 2 * P], F32R)
        gw_zero = m.sb("gw_zero", [P, KC, 2 * P])
        bias = m.sb("bias", [P, E])
        logit = m.sb("logit", [P, NT, E])
        score = m.sb("score", [P, NT, E])
        biased = m.sb("biased", [P, NT, E])
        best = m.sb("best", [P, NT, G, 8])
        gscore = m.sb("gscore", [P, NT, G])
        ahead = m.sb("ahead", [P, NT, G, G])
        chosen_g = m.sb("chosen_g", [P, NT, G])
        penalty = m.sb("penalty", [P, NT, G])
        top = m.sb("top", [P, NT, 8])
        above = m.sb("above", [P, NT, E])
        equal = m.sb("equal", [P, NT, E])
        carry = m.sb("carry", [P, NT, E])
        order = m.sb("order", [P, NT, E])
        room = m.sb("room", [P, NT])
        weight = m.sb("weight", [P, NT, E])
        total = m.sb("total", [P, NT])
        parts = m.sb("parts", [P, NT, E + A, 2], F16)
        rows = m.sb("rows", [2 * (E + A), T], F16)
        ps = m.ps("ps", [P, 4, 2, 256])
        ps_r = m.ps("ps_r", [P, 2, 1024], F16)
        loaded, step_done = m.sem("loaded"), m.sem("step_done")
        gw_ready, filled, first_read, freed = m.sem("gw_ready"), m.sem("filled"), m.sem("first_read"), m.sem("freed")
        scored, parts_ready, turned, rows_ready, stored = (m.sem("scored"), m.sem("parts_ready"), m.sem("turned"),
                                                           m.sem("rows_ready"), m.sem("stored"))
        hi_done = m.sem("hi_done")
        block = ctx.enter_context(nc.Block())

        @block.sync
        def _(sp):
            sp.dma_start(gw[:], gw_dram).then_inc(loaded, 16)
            sp.dma_start(bias[:], bias_dram).then_inc(loaded, 16)
            sp.wait_ge(rows_ready, 2)
            sp.dma_start(cw_dram, rows[:]).then_inc(stored, 16)
            sp.wait_ge(stored, 16)

        @block.tensor
        def _(pe):
            pe.wait_ge(gw_ready, 1)
            for n in range(NT // 2):
                if n >= 4:
                    pe.wait_ge(freed, n - 3)
                for j in range(2):
                    tok = slice((2 * n + j) * P, (2 * n + j + 1) * P)
                    for k in range(KC):
                        for h in (h_hi, h_lo):
                            last = nc.tensor.matmul(ps[:, n % 4, j], h[:, k, tok], gw_x[:, k],
                                                    start=(k == 0 and h is h_hi), stop=(k == KC - 1 and h is h_lo))
                last.then_inc(filled, 1)
            pe.wait_ge(parts_ready, 1)
            for t in range(NT):
                last = nc.tensor.transpose(ps_r[0:2 * (E + A), t // 8, (t % 8) * P:(t % 8 + 1) * P],
                                           parts[:, t].rearrange("p e a -> p (e a)"), ident_h[:])
                if t % 8 == 7:
                    last.then_inc(turned, 1)

        @block.scalar
        def _(act):
            act.wait_ge(loaded, 32)
            act.wait_ge(step_done, 1)
            nc.scalar.activation(gw_x[:], gw_zero[:], ACT.Copy).then_inc(hi_done, 1)
            act.wait_ge(hi_done, 1)
            nc.scalar.activation(gw_x[:, :, 0:E], gw[:], ACT.Copy).then_inc(hi_done, 1)
            for n in range(NT // 2):
                act.wait_ge(filled, n + 1)
                nc.scalar.activation(logit[:, 2 * n:2 * n + 2], ps[:, n % 4, :, 0:E], ACT.Copy).then_inc(first_read, 1)
            act.wait_ge(freed, NT // 2)
            nc.scalar.activation(score[:], logit[:], ACT.Sigmoid).then_inc(scored, 1)
            for half in range(2):
                act.wait_ge(turned, half + 1)
                nc.scalar.activation(rows[:, half * 1024:(half + 1) * 1024], ps_r[0:2 * (E + A), half], ACT.Copy).then_inc(rows_ready, 1)

        @block.vector
        def _(dve):
            done = [0]

            def chain(instruction):
                done[0] += 1
                instruction.then_inc(step_done, 1)
                dve.wait_ge(step_done, done[0])

            def over_experts(ap):
                return ap.unsqueeze(3).broadcast_to([P, NT, G, per])

            def grouped(tile):
                return tile[:].rearrange("p t (g e) -> p t g e", g=G)

            chain(nc.vector.memset(gw_zero[:], 0.0))
            dve.wait_ge(hi_done, 2)
            nc.vector.tensor_tensor(gw_x[:, :, E:2 * E], gw[:], f32(gw_x[:, :, 0:E]), ALU.subtract).then_inc(gw_ready, 1)
            for n in range(NT // 2):
                dve.wait_ge(first_read, n + 1)
                out = logit[:, 2 * n:2 * n + 2]
                nc.vector.tensor_tensor(out, ps[:, n % 4, :, E:2 * E], out, ALU.add).then_inc(freed, 1)
            nc.vector.memset(ahead[:], 0.0)
            nc.vector.memset(carry[:], 1.0)
            chain(nc.vector.memset(parts[:], 0.0))
            nc.vector.memset(carry[:, :, 0:1], 0.0)
            if A:
                nc.vector.memset(parts[:, :, E:, 0:1], 1.0)
            dve.wait_ge(scored, 1)
            chain(nc.vector.tensor_tensor(biased[:], score[:], bias[:].unsqueeze(1).broadcast_to([P, NT, E]), ALU.add))
            if group_best == 2:
                for t in range(NT):
                    for g in range(G):
                        last = nc.vector.max(best[:, t, g], biased[:, t, g * per:(g + 1) * per])
                chain(last)
                chain(nc.vector.tensor_tensor(gscore[:], best[:, :, :, 0], best[:, :, :, 1], ALU.add))
            else:
                chain(nc.vector.tensor_reduce(gscore[:], grouped(biased), AX_X, ALU.max))
            for j in range(G):
                other = gscore[:, :, j:j + 1]
                if j + 1 < G:
                    last = nc.vector.tensor_tensor(ahead[:, :, j + 1:, j], other.broadcast_to([P, NT, G - 1 - j]),
                                                   gscore[:, :, j + 1:], ALU.is_ge)
                if j:
                    last = nc.vector.tensor_tensor(ahead[:, :, 0:j, j], other.broadcast_to([P, NT, j]),
                                                   gscore[:, :, 0:j], ALU.is_gt)
            chain(last)
            chain(nc.vector.tensor_reduce(chosen_g[:], ahead[:], AX_X, ALU.add))
            chain(nc.vector.tensor_scalar(chosen_g[:], chosen_g[:], 2.0, None, ALU.is_lt))
            chain(nc.vector.tensor_scalar(penalty[:], chosen_g[:], 1.0, -LOWEST, ALU.subtract, ALU.mult))
            chain(nc.vector.tensor_tensor(grouped(biased), grouped(biased), over_experts(chosen_g[:]), ALU.mult))
            chain(nc.vector.tensor_tensor(grouped(biased), grouped(biased), over_experts(penalty[:]), ALU.add))
            for t in range(NT):
                last = nc.vector.max(top[:, t], biased[:, t])
            chain(last)
            least = top[:, :, top_k - 1:top_k].broadcast_to([P, NT, E])
            nc.vector.tensor_tensor(above[:], biased[:], least, ALU.is_gt)
            chain(nc.vector.tensor_tensor(equal[:], biased[:], least, ALU.is_equal))
            nc.vector.tensor_reduce(room[:], above[:], AX_X, ALU.add)
            chain(nc.vector.tensor_tensor_scan(order[:].rearrange("p t e -> p (t e)"), carry[:].rearrange("p t e -> p (t e)"),
                                               equal[:].rearrange("p t e -> p (t e)"), 0.0, ALU.mult, ALU.add))
            chain(nc.vector.tensor_scalar(room[:], room[:], -1.0, float(top_k), ALU.mult, ALU.add))
            chain(nc.vector.tensor_tensor(order[:], order[:], room[:].unsqueeze(2).broadcast_to([P, NT, E]), ALU.is_le))
            chain(nc.vector.tensor_tensor(equal[:], equal[:], order[:], ALU.mult))
            chain(nc.vector.tensor_tensor(above[:], above[:], equal[:], ALU.add))
            chain(nc.vector.tensor_tensor(weight[:], above[:], score[:], ALU.mult))
            chain(nc.vector.tensor_reduce(total[:], weight[:], AX_X, ALU.add))
            chain(nc.vector.reciprocal(room[:], total[:]))
            chain(nc.vector.scalar_tensor_tensor(weight[:], weight[:], route_scale,
                                                 room[:].unsqueeze(2).broadcast_to([P, NT, E]), ALU.mult, ALU.mult))
            chain(nc.vector.tensor_copy(parts[:, :, 0:E, 0], weight[:]))
            nc.vector.tensor_tensor(parts[:, :, 0:E, 1], weight[:], parts[:, :, 0:E, 0], ALU.subtract).then_inc(parts_ready, 1)



THREE = ((0, 0), (0, 1), (1, 0))


def pipeline(eng, rounds, units, stages):
    deepest = max(lead for lead, _ in stages)

    def run(i, u, last):
        for lead, step in stages:
            v = u + lead
            if 0 <= v < units:
                step(i, v)
            elif v >= units and not last:
                step(i + 1, v - units)

    for u in range(-deepest, 0):
        run(0, u, False)
    if rounds > 1:
        with eng.Fori(0, rounds - 1) as i:
            for u in range(units):
                run(i, u, False)
    for u in range(units):
        run(rounds - 1, u, True)

E0, GROUP0 = 32, 4
SHARED0 = 4


def ffn0_phase(nc, w_dram, out_dram, w_exp_dram, cw_dram, x, h_hi, h_lo, gate_row):
    with ExitStack() as outer:
        m = Memory(nc, outer, "f0")
        fc1_cols, width = KC * P, KC * P + KC * SHARED0 * P
        w_hi, w_lo = m.sb("w_hi", [P, width], F32R), m.sb("w_lo", [P, width], F32R)
        y_acc = m.sb("y_acc", [P, T])
        fc1 = [w[:, 0:fc1_cols].rearrange("p (k n) -> p k n", k=KC) for w in (w_hi, w_lo)]
        up = [w[:, fc1_cols:].rearrange("p (k n) -> p k n", k=KC) for w in (w_hi, w_lo)]
        experts0_block(nc, w_dram, w_exp_dram, cw_dram, h_hi, h_lo, w_hi, w_lo, fc1, y_acc)
        output0_block(nc, out_dram, up, y_acc, x, h_hi, h_lo, gate_row)


def experts0_block(nc, w_dram, w_exp_dram, cw_dram, h_hi, h_lo, w_hi, w_lo, fc1, y_acc):
    width = w_hi.shape[1]
    ROUNDS = E0 // GROUP0 // 2
    UNITS_ROUND = 2 * NB * GROUP0
    GROUP_UNITS = NB * GROUP0
    RR, TR = 4, 4
    HB, CB, YB = 4, 2, 2
    round_units = [(half, b, e) for half in range(2) for b in range(NB) for e in range(GROUP0)]
    with ExitStack() as ctx:
        m = Memory(nc, ctx, "f0e")
        w32 = m.sb("w32", [P, width])
        lat = [m.sb("lat_hi", [P, T], F32R), m.sb("lat_lo", [P, T], F32R)]
        stage = m.sb("stage", [P, 2, GROUP0, 2, P])
        we = [m.sb("we_hi", [P, 2, GROUP0, 2, P], F32R), m.sb("we_lo", [P, 2, GROUP0, 2, P], F32R)]
        crow = m.sb("crow", [2 * GROUP0, 2, T], F16)
        pick = m.sb("pick", [2 * GROUP0, GROUP0, P], F16)
        relu = m.sb("relu", [P, RR, QB])
        scaled = m.sb("scaled", [P, RR, QB])
        prod = m.sb("prod", [P, RR, QB])
        split = [m.sb("t_hi", [P, TR, QB], F32R), m.sb("t_lo", [P, TR, QB], F32R)]
        ps_h, ps_c, ps_y = m.ps("ps_h", [P, HB, QB]), m.ps("ps_c", [P, CB, QB]), m.ps("ps_y", [P, YB, QB])
        loaded, w_hi_ready, w_ready = m.sem("loaded"), m.sem("w_hi_ready"), m.sem("w_ready")
        lat_filled, lat_hi_ready, lat_ready = m.sem("lat_filled"), m.sem("lat_hi_ready"), m.sem("lat_ready")
        zeroed, picked = m.sem("zeroed"), m.sem("picked")
        e_loaded, c_loaded = [[m.sem(f"{what}_loaded{half}") for half in range(2)] for what in "ec"]
        e_hi, e_ready = m.sem("e_hi"), m.sem("e_ready")
        h_filled, c_filled, relu_ready = m.sem("h_filled"), m.sem("c_filled"), m.sem("relu_ready")
        scaled_ready, prod_ready, t_hi_ready, t_ready = m.sem("scaled_ready"), m.sem("prod_ready"), m.sem("t_hi_ready"), m.sem("t_ready")
        second_done, y_free = m.sem("second_done"), m.sem("y_free")
        block = ctx.enter_context(nc.Block())

        @block.sync
        def _(sp):
            sp.dma_start(w32[:], w_dram).then_inc(loaded, 16)

            def load(group, half):
                sp.dma_start(stage[:, half].rearrange("p e c n -> p (e c n)"), w_exp_dram[group]).then_inc(e_loaded[half], 16)
                sp.dma_start(crow[:, half], cw_dram[group]).then_inc(c_loaded[half], 16)

            load(0, 0)
            load(1, 1)
            with sp.Fori(0, ROUNDS - 1) as i:
                for half in range(2):
                    sp.wait_ge(c_filled, (2 * i + half + 1) * GROUP_UNITS)
                    load(2 * i + half + 2, half)
            for half in range(2):
                sp.wait_ge(e_loaded[half], 16 * ROUNDS)
                sp.wait_ge(c_loaded[half], 16 * ROUNDS)

        @block.gpsimd
        def _(pool):
            pool.sem_inc(prod_ready, RR)
            nc.gpsimd.memset(pick[:], 1.0).then_inc(zeroed, 1)
            pool.wait_ge(zeroed, 1)
            for e in range(GROUP0):
                nc.gpsimd.affine_select(out=pick[:, e], in_=pick[:, e], compare_op=ALU.is_ge, fill=0.0, base=-2 * e,
                                        pattern=[[0, P]], channel_multiplier=1).then_inc(zeroed, 1)
            pool.wait_ge(zeroed, 1 + GROUP0)
            for e in range(GROUP0):
                nc.gpsimd.affine_select(out=pick[:, e], in_=pick[:, e], compare_op=ALU.is_ge, fill=0.0, base=2 * e + 1,
                                        pattern=[[0, P]], channel_multiplier=-1).then_inc(picked, 1)

            def square(i, u):
                n = i * UNITS_ROUND + u
                pool.wait_ge(t_ready, n + 1)
                pool.wait_ge(scaled_ready, n + 1 + CB)
                nc.gpsimd.tensor_tensor(prod[:, u % RR], scaled[:, u % RR], relu[:, u % RR], ALU.mult).then_inc(prod_ready, 1)

            pipeline(pool, ROUNDS, UNITS_ROUND, [(0, square)])

        @block.tensor
        def _(pe):
            pe.sem_inc(second_done, TR)
            pe.wait_ge(w_ready, 1)
            for b in range(NB):
                tok = slice(b * QB, (b + 1) * QB)
                for k in range(KC):
                    for wi, hi in THREE:
                        last = nc.tensor.matmul(ps_h[:, b], fc1[wi][:, k], (h_hi, h_lo)[hi][:, k, tok],
                                                start=(k == 0 and (wi, hi) == (0, 0)), stop=(k == KC - 1 and (wi, hi) == (1, 0)))
                last.then_inc(lat_filled, 1)
            pe.wait_ge(lat_ready, NB)
            pe.wait_ge(picked, GROUP0)

            def first(i, u):
                half, b, e = round_units[u]
                n = i * UNITS_ROUND + u
                if (b, e) == (0, 0):
                    pe.wait_ge(e_ready, 2 * i + half + 1)
                    pe.wait_ge(c_loaded[half], 16 * (i + 1))
                tok = slice(b * QB, (b + 1) * QB)
                pe.wait_ge(relu_ready, n + 1)
                for wi, li in THREE:
                    last = nc.tensor.matmul(ps_h[:, u % HB], we[wi][:, half, e, 0], lat[li][:, tok],
                                            start=(wi, li) == (0, 0), stop=(wi, li) == (1, 0))
                last.then_inc(h_filled, 1)
                pe.wait_ge(scaled_ready, n + 1)
                nc.tensor.matmul(ps_c[:, u % CB], pick[:, e], crow[:, half, tok], start=True, stop=True).then_inc(c_filled, 1)

            def second(i, u):
                half, b, e = round_units[u]
                n = i * UNITS_ROUND + u
                if e == 0:
                    pe.wait_ge(y_free, i * (UNITS_ROUND // GROUP0) + u // GROUP0 + 1)
                pe.wait_ge(t_ready, n + 1 + RR)
                for wi, ti in THREE:
                    last = nc.tensor.matmul(ps_y[:, b % YB], we[wi][:, half, e, 1], split[ti][:, u % TR],
                                            start=(e == 0 and (wi, ti) == (0, 0)), stop=(e == GROUP0 - 1 and (wi, ti) == (1, 0)))
                last.then_inc(second_done, 1)

            pipeline(pe, ROUNDS, UNITS_ROUND, [(4, first), (0, second)])

        @block.scalar
        def _(act):
            act.sem_inc(relu_ready, HB)
            act.wait_ge(loaded, 16)
            nc.scalar.activation(w_hi[:], w32[:], ACT.Copy).then_inc(w_hi_ready, 1)
            for b in range(NB):
                act.wait_ge(lat_filled, b + 1)
                nc.scalar.activation(lat[0][:, b * QB:(b + 1) * QB], ps_h[:, b], ACT.Copy).then_inc(lat_hi_ready, 1)

            def split_weights(group, half, i):
                act.wait_ge(e_loaded[half], 16 * (i + 1))
                if half or not isinstance(group, int):
                    act.wait_ge(second_done, (group - 1) * GROUP_UNITS + TR)
                nc.scalar.activation(we[0][:, half], stage[:, half], ACT.Copy).then_inc(e_hi, 1)

            split_weights(0, 0, 0)

            def weights(i, u):
                if u % GROUP_UNITS == 6 and not (u > GROUP_UNITS and isinstance(i, int) and i == ROUNDS - 1):
                    g = u // GROUP_UNITS
                    split_weights(2 * i + g + 1, 1 - g, i + g)

            def rectify(i, u):
                n = i * UNITS_ROUND + u
                act.wait_ge(h_filled, n + 1)
                act.wait_ge(prod_ready, n + 1)
                nc.scalar.activation(relu[:, u % RR], ps_h[:, u % HB], ACT.Relu).then_inc(relu_ready, 1)

            def leading(i, u):
                n = i * UNITS_ROUND + u
                act.wait_ge(prod_ready, n + 1 + RR)
                act.wait_ge(second_done, n + 1)
                nc.scalar.activation(split[0][:, u % TR], prod[:, u % RR], ACT.Copy).then_inc(t_hi_ready, 1)

            pipeline(act, ROUNDS, UNITS_ROUND, [(3, rectify), (0, leading), (0, weights)])

        @block.vector
        def _(dve):
            dve.sem_inc(scaled_ready, CB)
            dve.sem_inc(t_ready, RR)
            dve.sem_inc(y_free, YB)
            nc.vector.memset(y_acc[:], 0.0)
            dve.wait_ge(w_hi_ready, 1)
            nc.vector.tensor_tensor(w_lo[:], w32[:], f32(w_hi[:]), ALU.subtract).then_inc(w_ready, 1)
            for b in range(NB):
                dve.wait_ge(lat_hi_ready, b + 1)
                tok = slice(b * QB, (b + 1) * QB)
                nc.vector.tensor_tensor(lat[1][:, tok], ps_h[:, b], f32(lat[0][:, tok]), ALU.subtract).then_inc(lat_ready, 1)

            def split_weights(group, half, i):
                dve.wait_ge(e_hi, group + 1)
                nc.vector.tensor_tensor(we[1][:, half], stage[:, half], f32(we[0][:, half]), ALU.subtract).then_inc(e_ready, 1)

            split_weights(0, 0, 0)

            def weights(i, u):
                if u % GROUP_UNITS == 6 and not (u > GROUP_UNITS and isinstance(i, int) and i == ROUNDS - 1):
                    g = u // GROUP_UNITS
                    split_weights(2 * i + g + 1, 1 - g, i + g)

            def scale(i, u):
                n = i * UNITS_ROUND + u
                dve.wait_ge(c_filled, n + 1)
                dve.wait_ge(relu_ready, n + 1 + HB)
                dve.wait_ge(prod_ready, n + 1)
                nc.vector.tensor_tensor(scaled[:, u % RR], ps_c[:, u % CB], relu[:, u % RR], ALU.mult).then_inc(scaled_ready, 1)

            def rest(i, u):
                n = i * UNITS_ROUND + u
                dve.wait_ge(t_hi_ready, n + 1)
                nc.vector.tensor_tensor(split[1][:, u % TR], prod[:, u % RR], f32(split[0][:, u % TR]), ALU.subtract).then_inc(t_ready, 1)

            def collect(i, u):
                half, b, e = round_units[u]
                if e == GROUP0 - 1:
                    dve.wait_ge(second_done, i * UNITS_ROUND + u + 1 + TR)
                    tok = slice(b * QB, (b + 1) * QB)
                    nc.vector.tensor_tensor(y_acc[:, tok], y_acc[:, tok], ps_y[:, b % YB], ALU.add).then_inc(y_free, 1)

            pipeline(dve, ROUNDS, UNITS_ROUND, [(4, scale), (1, rest), (0, collect), (0, weights)])


def output0_block(nc, out_dram, up, y_acc, x, h_hi, h_lo, gate_row):
    with ExitStack() as ctx:
        m = Memory(nc, ctx, "f0o")
        y = [m.sb("y_hi", [P, T], F32R), m.sb("y_lo", [P, T], F32R)]
        stage = m.sb("stage", [P, 5, D])
        gated = m.sb("gated", [P, 5, D])
        out_w = [m.sb("out_hi", [P, 5, D], F32R), m.sb("out_lo", [P, 5, D], F32R)]
        relu = m.sb("relu", [P, 4, QB])
        prod = m.sb("prod", [P, 4, QB])
        inner = [m.sb("inner_hi", [P, 2, SHARED0, QB], F32R), m.sb("inner_lo", [P, 2, SHARED0, QB], F32R)]
        UB, OB = 4, 4
        ps_u, ps_o = m.ps("ps_u", [P, UB, QB]), m.ps("ps_o", [P, OB, 2, D])
        loaded = m.sem("loaded")
        gated_ready, out_hi_ready, out_ready = m.sem("gated_ready"), m.sem("out_hi_ready"), m.sem("out_ready")
        y_hi_ready, y_ready = m.sem("y_hi_ready"), m.sem("y_ready")
        u_filled, relu_ready, prod_ready = m.sem("u_filled"), m.sem("relu_ready"), m.sem("prod_ready")
        in_hi_ready, in_ready, o_filled, o_free = m.sem("in_hi_ready"), m.sem("in_ready"), m.sem("o_filled"), m.sem("o_free")
        block = ctx.enter_context(nc.Block())
        units = [(b, c) for b in range(NB) for c in range(SHARED0)]

        @block.sync
        def _(sp):
            sp.dma_start(stage[:].rearrange("p c n -> p (c n)"), out_dram).then_inc(loaded, 16)
            sp.wait_ge(loaded, 16)

        @block.tensor
        def _(pe):
            def up_block(b):
                for c in range(SHARED0):
                    n = b * SHARED0 + c
                    if n >= UB:
                        pe.wait_ge(relu_ready, n - UB + 1)
                    for k in range(KC):
                        for wi, hi in THREE:
                            last = nc.tensor.matmul(ps_u[:, n % UB], up[wi][:, k, c * P:(c + 1) * P],
                                                    (h_hi, h_lo)[hi][:, k, b * QB:(b + 1) * QB],
                                                    start=(k == 0 and (wi, hi) == (0, 0)), stop=(k == KC - 1 and (wi, hi) == (1, 0)))
                    last.then_inc(u_filled, 1)

            def out_block(b):
                for pair in range(TPB // 2):
                    n = b * (TPB // 2) + pair
                    if n >= OB:
                        pe.wait_ge(o_free, n - OB + 1)
                    for j in range(2):
                        t = 2 * pair + j
                        for c in range(SHARED0 + 1):
                            for ai, wi in THREE:
                                a = y[ai][:, (b * TPB + t) * P:(b * TPB + t + 1) * P] if c == 0 else inner[ai][:, b % 2, c - 1, t * P:(t + 1) * P]
                                last = nc.tensor.matmul(ps_o[:, n % OB, j], a, out_w[wi][:, c],
                                                        start=(c == 0 and (ai, wi) == (0, 0)), stop=(c == SHARED0 and (ai, wi) == (1, 0)))
                    last.then_inc(o_filled, 1)

            up_block(0)
            pe.wait_ge(out_ready, 1)
            for b in range(NB):
                if b + 1 < NB:
                    up_block(b + 1)
                pe.wait_ge(in_ready, (b + 1) * SHARED0)
                pe.wait_ge(y_ready, b + 1)
                out_block(b)

        @block.gpsimd
        def _(pool):
            for n in range(len(units)):
                pool.wait_ge(relu_ready, n + 1)
                if n >= 4:
                    pool.wait_ge(in_ready, n - 3)
                nc.gpsimd.tensor_tensor(prod[:, n % 4], relu[:, n % 4], relu[:, n % 4], ALU.mult).then_inc(prod_ready, 1)

        @block.scalar
        def _(act):
            act.wait_ge(gated_ready, 1)
            nc.scalar.activation(out_w[0][:], gated[:], ACT.Copy).then_inc(out_hi_ready, 1)
            for b in range(NB):
                nc.scalar.activation(y[0][:, b * QB:(b + 1) * QB], y_acc[:, b * QB:(b + 1) * QB], ACT.Copy).then_inc(y_hi_ready, 1)

            def leading(n):
                b, c = units[n]
                act.wait_ge(prod_ready, n + 1)
                if b >= 2:
                    act.wait_ge(o_filled, (b - 1) * (TPB // 2))
                nc.scalar.activation(inner[0][:, b % 2, c], prod[:, n % 4], ACT.Copy).then_inc(in_hi_ready, 1)

            for n in range(len(units)):
                act.wait_ge(u_filled, n + 1)
                if n >= 4:
                    act.wait_ge(prod_ready, n - 3)
                nc.scalar.activation(relu[:, n % 4], ps_u[:, n % UB], ACT.Relu).then_inc(relu_ready, 1)
                if n >= 2:
                    leading(n - 2)
            leading(len(units) - 2)
            leading(len(units) - 1)

        @block.vector
        def _(dve):
            dve.wait_ge(loaded, 16)
            nc.vector.tensor_tensor(gated[:], stage[:], gate_row.unsqueeze(1).broadcast_to([P, 5, D]), ALU.mult).then_inc(gated_ready, 1)
            dve.wait_ge(out_hi_ready, 1)
            nc.vector.tensor_tensor(out_w[1][:], gated[:], f32(out_w[0][:]), ALU.subtract).then_inc(out_ready, 1)
            for b in range(NB):
                dve.wait_ge(y_hi_ready, b + 1)
                tok = slice(b * QB, (b + 1) * QB)
                nc.vector.tensor_tensor(y[1][:, tok], y_acc[:, tok], f32(y[0][:, tok]), ALU.subtract).then_inc(y_ready, 1)

            def collect(b):
                for pair in range(TPB // 2):
                    n = b * (TPB // 2) + pair
                    dve.wait_ge(o_filled, n + 1)
                    xs = x[:, 2 * n:2 * n + 2]
                    nc.vector.tensor_tensor(xs, xs, ps_o[:, n % OB], ALU.add).then_inc(o_free, 1)

            for n, (b, c) in enumerate(units):
                dve.wait_ge(in_hi_ready, n + 1)
                nc.vector.tensor_tensor(inner[1][:, b % 2, c], prod[:, n % 4], f32(inner[0][:, b % 2, c]), ALU.subtract).then_inc(in_ready, 1)
                if c == 2 and b >= 1:
                    collect(b - 1)
            collect(NB - 1)



HEADS1 = 16
DH1 = D // HEADS1
STACK = 4 * DH1
VW = 2 * DH1 + 1
WIDE = 2 * QB
WIDE_MAXES = [(qt, w) for qt in range(NT) for w in range(qt * P // WIDE + 1)]


def project1_block(nc, w_dram, qk_dram, v_all, h_hi, h_lo):
    with ExitStack() as ctx:
        m = Memory(nc, ctx, "p1")
        w32 = m.sb("w32", [P, KC, 3, D])
        w = [m.sb("w_hi", [P, KC, 3, D], F32R), m.sb("w_lo", [P, KC, 3, D], F32R)]
        parts = [m.sb("hi", [P, 2, 2, T], F16), m.sb("lo", [P, 2, 2, T], F16)]
        ps = m.ps("ps", [P, 8, QB])
        loaded, w_hi_ready, w_ready = m.sem("loaded"), m.sem("w_hi_ready"), m.sem("w_ready")
        filled, hi_ready, freed, stored, ones_ready = m.sem("filled"), m.sem("hi_ready"), m.sem("freed"), m.sem("stored"), m.sem("ones_ready")
        block = ctx.enter_context(nc.Block())
        qk = [(c, which, b) for c in range(KC) for which in range(2) for b in range(NB)]
        vs = list(range(NT // 2))

        @block.sync
        def _(sp):
            sp.dma_start(w32[:].rearrange("p k w n -> p (k w n)"), w_dram).then_inc(loaded, 16)
            for n, (c, which) in enumerate((c, which) for c in range(KC) for which in range(2)):
                sp.wait_ge(freed, (n + 1) * NB)
                for a in range(2):
                    sp.dma_start(qk_dram[which, a, c * P:(c + 1) * P], parts[a][:, which, c]).then_inc(stored, 16)
            sp.wait_ge(stored, 16 * 8)

        @block.gpsimd
        def _(pool):
            nc.gpsimd.memset(v_all[:, :, :, VW - 1:VW], 1.0).then_inc(ones_ready, 1)

        @block.tensor
        def _(pe):
            pe.wait_ge(w_ready, 1)
            for n, (c, which, b) in enumerate(qk):
                if n >= 8:
                    pe.wait_ge(freed, n - 7)
                for k in range(KC):
                    for wi, hi in THREE:
                        last = nc.tensor.matmul(ps[:, n % 8], w[wi][:, k, which, c * P:(c + 1) * P], (h_hi, h_lo)[hi][:, k, b * QB:(b + 1) * QB],
                                                start=(k == 0 and (wi, hi) == (0, 0)), stop=(k == KC - 1 and (wi, hi) == (1, 0)))
                last.then_inc(filled, 1)
            for pair in vs:
                n = len(qk) + pair
                pe.wait_ge(freed, n - 7)
                for j in range(2):
                    t = 2 * pair + j
                    for k in range(KC):
                        for hi, wi in THREE:
                            last = nc.tensor.matmul(ps[:, n % 8, j * D:(j + 1) * D], (h_hi, h_lo)[hi][:, k, t * P:(t + 1) * P], w[wi][:, k, 2],
                                                    start=(k == 0 and (wi, hi) == (0, 0)), stop=(k == KC - 1 and (hi, wi) == (1, 0)))
                last.then_inc(filled, 1)

        def v_part(pair, a):
            return v_all[:, :, 2 * pair:2 * pair + 2, a * DH1:(a + 1) * DH1].rearrange("p h t d -> p t h d")

        def v_sums(n):
            return ps[:, n % 8].rearrange("p (t h d) -> p t h d", t=2, d=DH1)

        @block.scalar
        def _(act):
            act.wait_ge(loaded, 16)
            nc.scalar.activation(w[0][:], w32[:], ACT.Copy).then_inc(w_hi_ready, 1)
            for n, (c, which, b) in enumerate(qk):
                act.wait_ge(filled, n + 1)
                nc.scalar.activation(parts[0][:, which, c, b * QB:(b + 1) * QB], ps[:, n % 8], ACT.Copy).then_inc(hi_ready, 1)
            for pair in vs:
                n = len(qk) + pair
                act.wait_ge(filled, n + 1)
                for j in range(2):
                    last = nc.scalar.activation(v_part(pair, 0)[:, j], v_sums(n)[:, j], ACT.Copy)
                last.then_inc(hi_ready, 1)

        @block.vector
        def _(dve):
            dve.wait_ge(w_hi_ready, 1)
            nc.vector.tensor_tensor(w[1][:], w32[:], f32(w[0][:]), ALU.subtract).then_inc(w_ready, 1)
            for n, (c, which, b) in enumerate(qk):
                dve.wait_ge(hi_ready, n + 1)
                tok = slice(b * QB, (b + 1) * QB)
                nc.vector.tensor_tensor(parts[1][:, which, c, tok], ps[:, n % 8], parts[0][:, which, c, tok], ALU.subtract).then_inc(freed, 1)
            for pair in vs:
                n = len(qk) + pair
                dve.wait_ge(hi_ready, n + 1)
                for j in range(2):
                    last = nc.vector.tensor_tensor(v_part(pair, 1)[:, j], v_sums(n)[:, j], v_part(pair, 0)[:, j], ALU.subtract)
                last.then_inc(freed, 1)


def lo_owner(u):
    return u % 2


def attention1_steps():
    def prep(h):
        return [("MAX", h, qt, w) for qt, w in WIDE_MAXES]

    start = [("LOAD", 0)] + prep(0) + [("COMBINE", 0), ("MROW", 0)]
    periods, late = [], []
    for h in range(HEADS1):
        steps = []
        more = h + 1 < HEADS1
        ahead = prep(h + 1) if more else []
        for u, (qb, kt) in enumerate(UNITS):
            steps.append(("S", h, u))
            if more and u == 5:
                steps.append(("LOAD", h + 1))
            if u >= 9 and len(WIDE_MAXES) - len(ahead) < len(WIDE_MAXES) * (u - 8) // 25:
                if ahead:
                    steps.append(ahead.pop(0))
            if more and u == 35:
                assert not ahead
                steps.append(("COMBINE", h + 1))
            if more and u == 36:
                steps.append(("MROW", h + 1))
            steps.append((("LOV", "LOG")[lo_owner(u)], h, u))
            steps += [s for n, s in late if n == 0]
            late = [(n - 1, s) for n, s in late if n > 0]
            late.append((2, ("PV", h, u)))
            if kt == TPB * (qb + 1) - 1:
                late.append((2, ("ZOUT", h, qb)))
        periods.append(steps)
    tail = [s for _, s in sorted(late, key=lambda x: x[0])]
    return start, periods, tail


def attention1_block(nc, qk_dram, v_all, context, ident, ident_bf, mask_q, mask_t):
    start, periods, tail = attention1_steps()
    streams = {"S": "S", "LOV": "LOV", "LOG": "LOG", "MAX": "AUX", "MROW": "T", "ZOUT": "Z", "COMBINE": "C"}
    place, _ = number_steps(start + sum(periods, []) + tail, streams)
    _, one_round = number_steps(periods[1] + periods[2], streams)
    for a in (1, 2):
        for h in range(a, HEADS1 - 1, 2):
            assert [(s[0], s[1] - h + a, *s[2:]) for s in periods[h]] == periods[a]
    scale = DH1 ** -0.5
    SB, AB, PR = 2, 2, 8
    qk_heads = qk_dram.rearrange("w a (h d) t -> w a h d t", d=DH1)
    context_heads = context[:].rearrange("p t (h d) -> p h t d", d=DH1)
    with ExitStack() as ctx:
        m = Memory(nc, ctx, "a1")
        q_stack, k_stack = m.sb("q_stack", [P, 2, T], F16), m.sb("k_stack", [P, 2, T], F16)
        zero_row = m.sb("zero_row", [1, T], F16)
        v_head = m.sb("v_head", [P, 2, NT, VW], F16)
        partial = m.sb("partial", [P, NT, T // WIDE])
        neg_max = m.sb("neg_max", [P, NT])
        neg_max_t = m.sb("neg_max_t", [NT, P], F16)
        p32 = m.sb("p32", [P, PR, QB])
        p_hi, p_lo = m.sb("p_hi", [P, PR, QB], F16), m.sb("p_lo", [P, PR, QB], F16)
        z = m.sb("z", [P, TPB, DH1])
        rden = m.sb("rden", [P, TPB])
        ps_s = m.ps("ps_s", [P, SB, QB])
        ps_z = m.ps("ps_z", [P, TPB, P])
        ps_t = m.ps("ps_t", [P, QB])
        ps_m = m.ps("ps_m", [P, AB, WIDE])
        const_ready = m.sem("const_ready")
        row_loaded = m.sem("row_loaded")
        loaded = [m.sem(f"loaded{s}") for s in range(2)]
        s_filled, s_exped, pv_done = m.sem("s_filled"), m.sem("s_exped"), m.sem("pv_done")
        lo_ready = [m.sem("lo_ready_vector"), m.sem("lo_ready_gpsimd")]
        max_filled, max_read, max_ready = m.sem("max_filled"), m.sem("max_read"), m.sem("max_ready")
        t_filled, t_read, z_read, z_out = m.sem("t_filled"), m.sem("t_read"), m.sem("z_read"), m.sem("z_out")
        block = ctx.enter_context(nc.Block())
        PER_LOAD = 16 * 6

        def whole_program(eng, step):
            def in_line(n, stream):
                return n

            for s in start + periods[0]:
                step(s, in_line, 0)
            with eng.Fori(0, (HEADS1 - 2) // 2) as i:
                for s in periods[1] + periods[2]:
                    step(s, lambda n, stream: n + i * one_round[stream], i)
            for s in periods[HEADS1 - 1] + tail:
                step(s, in_line, 0)

        def rest(eng, unit, s, at):
            h, u = s[1:]
            c = first_col(*UNITS[u])
            eng.wait_ge(s_exped, at(place["S", h, u], "S") + 1 + SB)
            unit.tensor_tensor(p_lo[:, u % PR, c:QB], p32[:, u % PR, c:QB], p_hi[:, u % PR, c:QB],
                               ALU.subtract).then_inc(lo_ready[lo_owner(u)], 1)

        @block.sync
        def _(sp):
            sp.wait_ge(const_ready, 5)

            def step(s, at, i):
                kind, h = s[0], s[1]
                if kind == "LOAD":
                    slot = h % 2
                    if h >= 2:
                        sp.wait_ge(pv_done, at(place["S", h - 2, len(UNITS) - 1], "S") + 1 + PR)
                    head = 2 * i + h
                    for j in range(2):
                        rows = slice(2 * j * DH1, 2 * (j + 1) * DH1)
                        sp.dma_start(q_stack[rows, slot], qk_heads[0, j, head].unsqueeze(0).broadcast_to([2, DH1, T])).then_inc(loaded[slot], 16)
                        sp.dma_start(k_stack[rows, slot], qk_heads[1, :, head]).then_inc(loaded[slot], 16)
                    sp.dma_start(q_stack[STACK:STACK + 1, slot], zero_row[:]).then_inc(loaded[slot], 16)
                    sp.dma_start(v_head[:, slot], v_all[:, head]).then_inc(loaded[slot], 16)
                elif kind == "MROW":
                    sp.wait_ge(t_read, at(place[s], "T") + 1)
                    sp.dma_start(q_stack[STACK:STACK + 1, h % 2].rearrange("a (t p) -> a t p", p=P), neg_max_t[:]).then_inc(row_loaded, 16)

            whole_program(sp, step)

        @block.gpsimd
        def _(pool):
            consts = [(q_stack[STACK:], 0.0), (zero_row[:], 0.0), (partial[:], LOWEST), (k_stack[STACK:], 0.0), (k_stack[STACK:STACK + 1], 1.0)]
            for n, (out, value) in enumerate(consts):
                if n:
                    pool.wait_ge(const_ready, n)
                nc.gpsimd.memset(out, value).then_inc(const_ready, 1)

            def step(s, at, i):
                if s[0] == "LOG":
                    rest(pool, nc.gpsimd, s, at)

            whole_program(pool, step)

        @block.tensor
        def _(pe):
            pe.wait_ge(const_ready, 5)
            pe.sem_inc(pv_done, PR)

            def step(s, at, i):
                kind, h = s[0], s[1]
                slot = h % 2
                if kind == "MAX":
                    qt, w = s[2:]
                    n = place[s]
                    if (qt, w) == (0, 0):
                        pe.wait_ge(loaded[slot], PER_LOAD * (i + h // 2 + 1))
                    pe.wait_ge(max_read, at(n, "AUX") + 1)
                    end = min((w + 1) * WIDE, (qt + 1) * P) - w * WIDE
                    for c in range(0, end, QB):
                        to = min(c + QB, end)
                        diagonal = w * WIDE + to == (qt + 1) * P
                        last = nc.tensor.matmul(ps_m[:, n % AB, c:to], q_stack[:, slot, qt * P:(qt + 1) * P],
                                                k_stack[:, slot, w * WIDE + c:w * WIDE + to], start=True, stop=not diagonal)
                        if diagonal:
                            last = nc.tensor.matmul(ps_m[:, n % AB, to - P:to], ident_bf[:], mask_q[:], start=False, stop=True)
                    last.then_inc(max_filled, 1)
                elif kind == "MROW":
                    pe.wait_ge(max_ready, at(place["COMBINE", h], "C") + 1)
                    if h > 0:
                        pe.wait_ge(t_read, at(place[s], "T"))
                    nc.tensor.transpose(ps_t[0:NT, 0:P], neg_max[:], ident[:]).then_inc(t_filled, 1)
                elif kind == "S":
                    u = s[2]
                    qb, kt = UNITS[u]
                    if u == 0:
                        pe.wait_ge(row_loaded, 16 * (at(place["COMBINE", h], "C") + 1))
                    pe.wait_ge(s_exped, at(place[s], "S") + 1)
                    c = first_col(qb, kt)
                    diagonal = kt >= TPB * qb
                    last = nc.tensor.matmul(ps_s[:, u % SB, c:QB], k_stack[:, slot, kt * P:(kt + 1) * P],
                                            q_stack[:, slot, qb * QB + c:(qb + 1) * QB], start=True, stop=not diagonal)
                    if diagonal:
                        last = nc.tensor.matmul(ps_s[:, u % SB, c:c + P], ident_bf[:], mask_t[:], start=False, stop=True)
                    last.then_inc(s_filled, 1)
                elif kind == "PV":
                    u = s[2]
                    qb, kt = UNITS[u]
                    if kt == 0:
                        pe.wait_ge(z_read, at(place["ZOUT", h, qb], "Z") + 1)
                    owner = lo_owner(u)
                    stream = ("LOV", "LOG")[owner]
                    pe.wait_ge(lo_ready[owner], at(place[stream, h, u], stream) + 1)
                    for t in range(first_col(qb, kt) // P, TPB):
                        end = t == TPB - 1 and kt == TPB * (qb + 1) - 1
                        for part in (p_hi, p_lo):
                            last = nc.tensor.matmul(ps_z[:, t, 0:VW], part[:, u % PR, t * P:(t + 1) * P], v_head[:, slot, kt],
                                                    start=(kt == 0 and t == 0 and part is p_hi), stop=(end and part is p_lo))
                    last.then_inc(pv_done, 1)

            whole_program(pe, step)

        @block.scalar
        def _(act):
            act.sem_inc(s_exped, SB)

            def step(s, at, i):
                kind, h = s[0], s[1]
                if kind == "S":
                    u = s[2]
                    c = first_col(*UNITS[u])
                    n = at(place[s], "S")
                    act.wait_ge(s_filled, n + 1)
                    act.wait_ge(pv_done, n + 1)
                    nc.scalar.activation(p32[:, u % PR, c:QB], ps_s[:, u % SB, c:QB], ACT.Exp, scale=scale)
                    nc.scalar.activation(p_hi[:, u % PR, c:QB], ps_s[:, u % SB, c:QB], ACT.Exp, scale=scale).then_inc(s_exped, 1)
                elif kind == "MROW":
                    n = at(place[s], "T")
                    act.wait_ge(t_filled, n + 1)
                    if h > 0:
                        act.wait_ge(row_loaded, 16 * n)
                    nc.scalar.activation(neg_max_t[:], ps_t[0:NT, 0:P], ACT.Copy).then_inc(t_read, 1)

            whole_program(act, step)

        @block.vector
        def _(dve):
            dve.sem_inc(max_read, AB)
            dve.sem_inc(z_read, 1)
            dve.wait_ge(const_ready, 5)

            def step(s, at, i):
                kind, h = s[0], s[1]
                if kind == "MAX":
                    qt, w = s[2:]
                    n = place[s]
                    if (qt, w) == (0, 0) and h > 0:
                        dve.wait_ge(max_ready, at(place["COMBINE", h], "C"))
                    dve.wait_ge(max_filled, at(n, "AUX") + 1)
                    end = min((w + 1) * WIDE, (qt + 1) * P) - w * WIDE
                    nc.vector.tensor_reduce(partial[:, qt, w:w + 1], ps_m[:, n % AB, 0:end], AX_X, ALU.max).then_inc(max_read, 1)
                elif kind == "COMBINE":
                    dve.wait_ge(max_read, at(place["MAX", h, NT - 1, T // WIDE - 1], "AUX") + 1 + AB)
                    if h > 0:
                        dve.wait_ge(t_filled, at(place["MROW", h - 1], "T") + 1)
                    nc.vector.tensor_reduce(neg_max[:], partial[:], AX_X, ALU.max, negate=True).then_inc(max_ready, 1)
                elif kind == "LOV":
                    rest(dve, nc.vector, s, at)
                elif kind == "ZOUT":
                    qb = s[2]
                    n = at(place[s], "Z")
                    dve.wait_ge(pv_done, at(place["S", h, UNITS.index((qb, TPB * (qb + 1) - 1))], "S") + 1 + PR)
                    if (h, qb) != (0, 0):
                        dve.wait_ge(z_out, n)
                    nc.vector.reciprocal(rden[:], ps_z[:, :, VW - 1])
                    nc.vector.tensor_reduce(z[:], ps_z[:, :, 0:2 * DH1].rearrange("p t (a d) -> p t d a", a=2), AX_X,
                                            ALU.add).then_inc(z_read, 1)
                    dve.wait_ge(z_read, n + 2)
                    nc.vector.tensor_tensor(context_heads[:, 2 * i + h, qb * TPB:(qb + 1) * TPB], z[:],
                                            rden[:].unsqueeze(2).broadcast_to([P, TPB, DH1]), ALU.mult).then_inc(z_out, 1)

            whole_program(dve, step)


def output1_block(nc, w_dram, b_dram, context, x, ident, h_hi, h_lo, gate_row):
    with ExitStack() as ctx:
        m = Memory(nc, ctx, "o1")
        wo, gated, bias, bias_gated = m.sb("wo", [P, KC, D]), m.sb("gated", [P, KC, D]), m.sb("bias", [P, D]), m.sb("bias_gated", [P, D])
        w = [m.sb("w_hi", [P, KC, D], F32R), m.sb("w_lo", [P, KC, D], F32R)]
        ps_t, ps_o = m.ps("ps_t", [P, 4, QB]), m.ps("ps_o", [P, 4, 2, D])
        loaded, gated_ready, w_hi_ready, w_ready = m.sem("loaded"), m.sem("gated_ready"), m.sem("w_hi_ready"), m.sem("w_ready")
        bias_ready, biased = m.sem("bias_ready"), m.sem("biased")
        turned, hi_ready, lo_ready, filled, added = m.sem("turned"), m.sem("hi_ready"), m.sem("lo_ready"), m.sem("filled"), m.sem("added")
        block = ctx.enter_context(nc.Block())
        units = [(b, k) for b in range(NB) for k in range(KC)]

        @block.sync
        def _(sp):
            sp.dma_start(wo[:].rearrange("p k n -> p (k n)"), w_dram).then_inc(loaded, 16)
            sp.dma_start(bias[:], b_dram).then_inc(loaded, 16)
            sp.wait_ge(loaded, 32)

        @block.gpsimd
        def _(pool):
            pool.wait_ge(loaded, 32)
            nc.gpsimd.tensor_tensor(gated[:], wo[:], gate_row.unsqueeze(1).broadcast_to([P, KC, D]), ALU.mult).then_inc(gated_ready, 1)
            nc.gpsimd.tensor_tensor(bias_gated[:], bias[:], gate_row, ALU.mult).then_inc(bias_ready, 1)
            pool.wait_ge(bias_ready, 1)
            for b in range(NB):
                xs = x[:, b * TPB:(b + 1) * TPB]
                nc.gpsimd.tensor_tensor(xs, xs, bias_gated[:].unsqueeze(1).broadcast_to([P, TPB, D]), ALU.add).then_inc(biased, 1)

        @block.tensor
        def _(pe):
            for n, (b, k) in enumerate(units):
                if n >= 4:
                    pe.wait_ge(lo_ready, n - 3)
                for j in range(TPB):
                    last = nc.tensor.transpose(ps_t[:, n % 4, j * P:(j + 1) * P], context[:, b * TPB + j, k * P:(k + 1) * P], ident[:])
                last.then_inc(turned, 1)
            pe.wait_ge(w_ready, 1)
            for n in range(NT // 2):
                pe.wait_ge(lo_ready, KC * (n // 2 + 1))
                if n >= 4:
                    pe.wait_ge(added, n - 3)
                for j in range(2):
                    tok = slice((2 * n + j) * P, (2 * n + j + 1) * P)
                    for k in range(KC):
                        for hi, wi in THREE:
                            last = nc.tensor.matmul(ps_o[:, n % 4, j], (h_hi, h_lo)[hi][:, k, tok], w[wi][:, k],
                                                    start=(k == 0 and (hi, wi) == (0, 0)), stop=(k == KC - 1 and (hi, wi) == (1, 0)))
                last.then_inc(filled, 1)

        @block.scalar
        def _(act):
            act.wait_ge(gated_ready, 1)
            nc.scalar.activation(w[0][:], gated[:], ACT.Copy).then_inc(w_hi_ready, 1)
            for n, (b, k) in enumerate(units):
                act.wait_ge(turned, n + 1)
                nc.scalar.activation(h_hi[:, k, b * QB:(b + 1) * QB], ps_t[:, n % 4], ACT.Copy).then_inc(hi_ready, 1)

        @block.vector
        def _(dve):
            dve.wait_ge(w_hi_ready, 1)
            nc.vector.tensor_tensor(w[1][:], gated[:], f32(w[0][:]), ALU.subtract).then_inc(w_ready, 1)
            for n, (b, k) in enumerate(units):
                dve.wait_ge(hi_ready, n + 1)
                tok = slice(b * QB, (b + 1) * QB)
                nc.vector.tensor_tensor(h_lo[:, k, tok], ps_t[:, n % 4], f32(h_hi[:, k, tok]), ALU.subtract).then_inc(lo_ready, 1)
            for n in range(NT // 2):
                dve.wait_ge(biased, n // 2 + 1)
                dve.wait_ge(filled, n + 1)
                xs = x[:, 2 * n:2 * n + 2]
                nc.vector.tensor_tensor(xs, xs, ps_o[:, n % 4], ALU.add).then_inc(added, 1)


def attention1_phase(nc, w_dram, wo_dram, bo_dram, qk_dram, x, h_hi, h_lo, ident, ident_bf, mask_q, mask_t, gate_row):
    with ExitStack() as outer:
        m = Memory(nc, outer, "l1")
        v_all = m.sb("v_all", [P, HEADS1, NT, VW], F16)
        context = m.sb("context", [P, NT, D])
        project1_block(nc, w_dram, qk_dram, v_all, h_hi, h_lo)
        attention1_block(nc, qk_dram, v_all, context, ident, ident_bf, mask_q, mask_t)
        output1_block(nc, wo_dram, bo_dram, context, x, ident, h_hi, h_lo, gate_row)



E1, INNER1, ALWAYS1 = 16, 176, 2
PAIRS1 = (E1 + ALWAYS1) // 2
TAIL1 = INNER1 - P
CHUNKS1 = 3


def ffn1_block(nc, w_dram, cw_dram, x, h_hi, h_lo, gate_row):
    SLOTS = 3
    ROUNDS = PAIRS1 // SLOTS
    PAIR_UNITS = NB * CHUNKS1
    UNITS_ROUND = SLOTS * PAIR_UNITS
    FB, R = 2, 4
    DONE = PAIR_UNITS + R
    round_units = [(s, b, c) for s in range(SLOTS) for b in range(NB) for c in range(CHUNKS1)]
    IN = KC * CHUNKS1 * P
    OUT = CHUNKS1 * D
    with ExitStack() as ctx:
        m = Memory(nc, ctx, "f1")
        stage = m.sb("stage", [P, SLOTS, 2 * IN + OUT])
        gated = m.sb("gated", [P, CHUNKS1, D])
        w_in = [m.sb("w_in_hi", [P, SLOTS, 2, KC, CHUNKS1, P], F32R), m.sb("w_in_lo", [P, SLOTS, 2, KC, CHUNKS1, P], F32R)]
        w_out = [m.sb("w_out_hi", [P, SLOTS, CHUNKS1, D], F32R), m.sb("w_out_lo", [P, SLOTS, CHUNKS1, D], F32R)]
        crow = m.sb("crow", [4, SLOTS, T], F16)
        pick = m.sb("pick", [4, CHUNKS1, P], F16)
        silu, both, prod = m.sb("silu", [P, R, QB]), m.sb("both", [P, R, QB]), m.sb("prod", [P, R, QB])
        split = [m.sb("t_hi", [P, R, QB], F32R), m.sb("t_lo", [P, R, QB], F32R)]
        ps_g, ps_u, ps_c = m.ps("ps_g", [P, FB, QB]), m.ps("ps_u", [P, FB, QB]), m.ps("ps_c", [P, FB, QB])
        ps_y = m.ps("ps_y", [P, TPB, D])
        ones_ready, picked = m.sem("ones_ready"), m.sem("picked")
        w_loaded, c_loaded = [[m.sem(f"{what}_loaded{slot}") for slot in range(SLOTS)] for what in "wc"]
        gated_ready, w_hi_ready, w_ready = m.sem("gated_ready"), m.sem("w_hi_ready"), m.sem("w_ready")
        g_filled, filled, silu_ready, both_ready = m.sem("g_filled"), m.sem("filled"), m.sem("silu_ready"), m.sem("both_ready")
        prod_ready, hi_ready, t_ready = m.sem("prod_ready"), m.sem("hi_ready"), m.sem("t_ready")
        second_done, y_read = m.sem("second_done"), m.sem("y_read")
        block = ctx.enter_context(nc.Block())

        @block.sync
        def _(sp):
            def load(pair, slot):
                sp.dma_start(stage[:, slot], w_dram[pair]).then_inc(w_loaded[slot], 16)
                sp.dma_start(crow[:, slot], cw_dram[pair]).then_inc(c_loaded[slot], 16)

            for slot in range(SLOTS):
                load(slot, slot)
            with sp.Fori(0, ROUNDS - 1) as i:
                for slot in range(SLOTS):
                    sp.wait_ge(filled, (SLOTS * i + slot + 1) * PAIR_UNITS)
                    load(SLOTS * i + slot + SLOTS, slot)
            for slot in range(SLOTS):
                sp.wait_ge(w_loaded[slot], 16 * ROUNDS)
                sp.wait_ge(c_loaded[slot], 16 * ROUNDS)

        def at_next_pair(i, u, step):
            if u % PAIR_UNITS == 5 and not (isinstance(i, int) and i == ROUNDS - 1 and u >= (SLOTS - 1) * PAIR_UNITS):
                s = u // PAIR_UNITS + 1
                step(SLOTS * i + s, s % SLOTS, i + s // SLOTS + 1)

        @block.gpsimd
        def _(pool):
            nc.gpsimd.memset(pick[:], 1.0).then_inc(ones_ready, 1)
            pool.wait_ge(ones_ready, 1)
            for chunk, c0, c1, base, step in ((0, 0, P, 1, -1), (1, 0, P, -2, 1), (2, 0, P // 2, 1, -1), (2, P // 2, P, -2, 1)):
                nc.gpsimd.affine_select(out=pick[:, chunk, c0:c1], in_=pick[:, chunk, c0:c1], compare_op=ALU.is_ge, fill=0.0,
                                        base=base, pattern=[[0, c1 - c0]], channel_multiplier=step).then_inc(picked, 1)

            def weights(pair, slot, loads):
                pool.wait_ge(w_ready, pair)
                pool.wait_ge(w_loaded[slot], 16 * loads)
                nc.gpsimd.tensor_tensor(gated[:], stage[:, slot, 2 * IN:].rearrange("p (c d) -> p c d", c=CHUNKS1),
                                        gate_row.unsqueeze(1).broadcast_to([P, CHUNKS1, D]), ALU.mult).then_inc(gated_ready, 1)

            weights(0, 0, 1)
            pipeline(pool, ROUNDS, UNITS_ROUND, [(0, lambda i, u: at_next_pair(i, u, weights))])

        @block.tensor
        def _(pe):
            pe.sem_inc(second_done, DONE)
            pe.wait_ge(picked, 4)

            def first(i, u):
                s, b, c = round_units[u]
                n = i * UNITS_ROUND + u
                if (b, c) == (0, 0):
                    pe.wait_ge(w_ready, SLOTS * i + s + 1)
                    pe.wait_ge(c_loaded[s], 16 * (i + 1))
                tok = slice(b * QB, (b + 1) * QB)
                pe.wait_ge(prod_ready, n + 1)
                for which, ps in ((0, ps_g), (1, ps_u)):
                    for k in range(KC):
                        for wi, hi in THREE:
                            last = nc.tensor.matmul(ps[:, u % FB], w_in[wi][:, s, which, k, c], (h_hi, h_lo)[hi][:, k, tok],
                                                    start=(k == 0 and (wi, hi) == (0, 0)), stop=(k == KC - 1 and (wi, hi) == (1, 0)))
                    if which == 0:
                        last.then_inc(g_filled, 1)
                nc.tensor.matmul(ps_c[:, u % FB], pick[:, c], crow[:, s, tok], start=True, stop=True).then_inc(filled, 1)

            def second(i, u):
                s, b, c = round_units[u]
                n = i * UNITS_ROUND + u
                if c == 0:
                    pe.wait_ge(y_read, i * (UNITS_ROUND // CHUNKS1) + u // CHUNKS1 + 1)
                pe.wait_ge(t_ready, n + 1)
                for t in range(TPB):
                    for ti, wi in THREE:
                        last = nc.tensor.matmul(ps_y[:, t], split[ti][:, u % R, t * P:(t + 1) * P], w_out[wi][:, s, c],
                                                start=(c == 0 and t % 2 == 0 and (ti, wi) == (0, 0)),
                                                stop=(c == CHUNKS1 - 1 and t % 2 == 1 and (ti, wi) == (1, 0)))
                last.then_inc(second_done, 1)

            pipeline(pe, ROUNDS, UNITS_ROUND, [(2, first), (0, second)])

        @block.scalar
        def _(act):
            def weights(pair, slot, loads):
                act.wait_ge(w_loaded[slot], 16 * loads)
                if not isinstance(pair, int) or pair > 1:
                    act.wait_ge(second_done, (pair - 2) * PAIR_UNITS + DONE)
                nc.scalar.activation(w_in[0][:, slot].rearrange("p w k c n -> p (w k c n)"), stage[:, slot, 0:2 * IN], ACT.Copy)
                act.wait_ge(gated_ready, pair + 1)
                nc.scalar.activation(w_out[0][:, slot], gated[:], ACT.Copy).then_inc(w_hi_ready, 1)

            weights(0, 0, 1)

            def gate(i, u):
                n = i * UNITS_ROUND + u
                act.wait_ge(g_filled, n + 1)
                act.wait_ge(prod_ready, n + 1)
                nc.scalar.activation(silu[:, u % R], ps_g[:, u % FB], ACT.Silu).then_inc(silu_ready, 1)

            def leading(i, u):
                n = i * UNITS_ROUND + u
                act.wait_ge(prod_ready, n + 1 + FB)
                act.wait_ge(second_done, n + 1 - R + DONE)
                nc.scalar.activation(split[0][:, u % R], prod[:, u % R], ACT.Copy).then_inc(hi_ready, 1)

            pipeline(act, ROUNDS, UNITS_ROUND, [(1, gate), (0, leading), (0, lambda i, u: at_next_pair(i, u, weights))])

        @block.vector
        def _(dve):
            dve.sem_inc(prod_ready, FB)
            dve.sem_inc(y_read, 1)

            def weights(pair, slot, loads):
                dve.wait_ge(w_hi_ready, pair + 1)
                nc.vector.tensor_tensor(w_in[1][:, slot].rearrange("p w k c n -> p (w k c n)"), stage[:, slot, 0:2 * IN],
                                        f32(w_in[0][:, slot]).rearrange("p w k c n -> p (w k c n)"), ALU.subtract)
                nc.vector.tensor_tensor(w_out[1][:, slot], gated[:], f32(w_out[0][:, slot]), ALU.subtract).then_inc(w_ready, 1)

            weights(0, 0, 1)

            def times_up(i, u):
                n = i * UNITS_ROUND + u
                dve.wait_ge(silu_ready, n + 1)
                dve.wait_ge(filled, n + 1)
                nc.vector.tensor_tensor(both[:, u % R], silu[:, u % R], ps_u[:, u % FB], ALU.mult).then_inc(both_ready, 1)

            def times_weight(i, u):
                n = i * UNITS_ROUND + u
                dve.wait_ge(both_ready, n + 1)
                nc.vector.tensor_tensor(prod[:, u % R], both[:, u % R], ps_c[:, u % FB], ALU.mult).then_inc(prod_ready, 1)

            def rest(i, u):
                n = i * UNITS_ROUND + u
                dve.wait_ge(hi_ready, n + 1)
                nc.vector.tensor_tensor(split[1][:, u % R], prod[:, u % R], f32(split[0][:, u % R]), ALU.subtract).then_inc(t_ready, 1)

            def collect(i, u):
                s, b, c = round_units[u]
                if c == CHUNKS1 - 1:
                    n = i * UNITS_ROUND + u
                    dve.wait_ge(second_done, n + 1 + DONE)
                    xs = x[:, b * TPB:(b + 1) * TPB]
                    nc.vector.tensor_tensor(xs, xs, ps_y[:], ALU.add).then_inc(y_read, 1)

            pipeline(dve, ROUNDS, UNITS_ROUND, [(1, times_up), (0, rest), (1, times_weight), (0, collect),
                                                (0, lambda i, u: at_next_pair(i, u, weights))])


def store_phase(nc, x, out):
    with ExitStack() as ctx:
        m = Memory(nc, ctx, "store")
        stored = m.sem("stored")
        block = ctx.enter_context(nc.Block())

        @block.sync
        def _(sp):
            sp.dma_start(out.rearrange("a (t p) d -> p (a t) d", p=P), x[:]).then_inc(stored, 16)
            sp.wait_ge(stored, 16)


def adaln_program(nc, a, out, stop=4):
    with ExitStack() as ctx:
        m = Memory(nc, ctx, "all")
        cw0 = nc.dram_tensor("cw0", (E0 // GROUP0, 2 * GROUP0, T), F16, kind="Internal").ap()
        x = m.sb("x", [P, NT, D])
        ident = m.sb("ident", [P, P])
        ident_bf = m.sb("ident_bf", [P, P], BF16)
        ident_h = m.sb("ident_h", [P, P], F16)
        mask_q = m.sb("mask_q", [P, P], BF16)
        mask_t = m.sb("mask_t", [P, P], BF16)
        coef = m.sb("coef", [P, 2, 8])
        gate = m.sb("gate", [P, 2, 2, D])
        h_hi = m.sb("h_hi", [P, KC, T], F32R)
        h_lo = m.sb("h_lo", [P, KC, T], F32R)
        setup_phase(nc, a["x"], [a["c0"], a["c1"]], [a["wmod0"], a["wmod1"]], x, ident, ident_bf, ident_h, mask_q, mask_t, coef, gate)
        norm_phase(nc, "n0", x, ident, coef[:, 0, 0:4], h_hi, h_lo)
        attention0_phase(nc, a["w_even"], a["w_odd"], x, h_hi, h_lo, ident, ident_bf, ident_h, mask_q, mask_t, gate[:, 0, 0])
        if stop >= 2:
            norm_phase(nc, "n1", x, ident, coef[:, 0, 4:8], h_hi, h_lo)
            routing_phase(nc, "r0", a["gate_w0"], a["gate_bias0"], cw0.rearrange("g r t -> (g r) t"), h_hi, h_lo, ident_h,
                          E0, 4, 2, 8, 2.5, 0)
            ffn0_phase(nc, a["f0_in"], a["f0_out"], a["f0_experts"], cw0, x, h_hi, h_lo, gate[:, 0, 1])
        if stop >= 3:
            qk1 = nc.dram_tensor("qk1", (2, 2, D, T), F16, kind="Internal").ap()
            norm_phase(nc, "n2", x, ident, coef[:, 1, 0:4], h_hi, h_lo)
            attention1_phase(nc, a["w_qkv1"], a["wo1"], a["bo1"], qk1, x, h_hi, h_lo, ident, ident_bf, mask_q, mask_t, gate[:, 1, 0])
        if stop >= 4:
            cw1 = nc.dram_tensor("cw1", (PAIRS1, 4, T), F16, kind="Internal").ap()
            norm_phase(nc, "n3", x, ident, coef[:, 1, 4:8], h_hi, h_lo)
            routing_phase(nc, "r1", a["gate_w1"], a["gate_bias1"], cw1.rearrange("g r t -> (g r) t"), h_hi, h_lo, ident_h,
                          E1, 4, 1, 4, 1.0, ALWAYS1)
            ffn1_block(nc, a["f1_pairs"], cw1, x, h_hi, h_lo, gate[:, 1, 1])
        store_phase(nc, x, out)



def host_layout(i):
    import numpy as np

    heads = HEADS0
    qk = np.stack([i["L0_attn_W_Q"], i["L0_attn_W_K"]])
    qk = qk.reshape(2, heads, DH0, KC, P).transpose(1, 4, 3, 0, 2).reshape(heads, P, KC * 2 * DH0)
    v = i["L0_attn_W_V"].reshape(heads // 2, 2, DH0, KC, P).transpose(0, 4, 3, 1, 2).reshape(heads // 2, P, KC * 2 * DH0)
    wo = i["L0_attn_W_O"].transpose(0, 2, 1)
    w_even = np.zeros((heads // 2 + 1, P, 768), np.float32)
    w_odd = np.zeros((heads // 2 + 2, P, 1280), np.float32)
    for j in range(heads // 2):
        w_even[j, :, 0:512], w_even[j, :, 512:768] = qk[2 * j + 1], wo[2 * j]
        w_odd[j, :, 0:512], w_odd[j, :, 512:1024] = qk[2 * j], v[j]
        w_odd[j + 1, :, 1024:1280] = wo[2 * j + 1]
    out = {"x": i["L0_attn_x"], "w_even": w_even, "w_odd": w_odd}
    for layer in range(2):
        out[f"c{layer}"] = i[f"L{layer}_c"].reshape(KC, P).T
        out[f"wmod{layer}"] = i[f"L{layer}_wmod"]

    def by_rows(a):
        return a.reshape(-1, P, a.shape[1]).transpose(1, 0, 2).reshape(P, -1)

    for layer, experts in enumerate((E0, 16)):
        out[f"gate_w{layer}"] = i[f"L{layer}_ffn_gate_w"].reshape(experts, KC, P).transpose(2, 1, 0)
    out["gate_bias0"] = np.broadcast_to(i["L0_ffn_gate_bias"], (P, E0))
    out["f0_in"] = np.concatenate([by_rows(i["L0_ffn_fc1_w"].T), by_rows(i["L0_ffn_shared_up_w"].T)], axis=1)
    out["f0_out"] = np.concatenate([i["L0_ffn_fc2_w"].T, by_rows(i["L0_ffn_shared_down_w"].T)], axis=1)
    both = np.stack([i["L0_ffn_w1"].transpose(2, 0, 1), i["L0_ffn_w2"].transpose(2, 0, 1)], axis=2)
    out["f0_experts"] = both.reshape(P, E0 // GROUP0, GROUP0 * 2 * P).transpose(1, 0, 2)
    qkv = np.stack([i["L1_attn_Wq"], i["L1_attn_Wk"], i["L1_attn_Wv"]])
    out["w_qkv1"] = qkv.reshape(3, KC, P, D).transpose(2, 1, 0, 3).reshape(P, -1)
    out["wo1"] = by_rows(i["L1_attn_Wo"])
    out["bo1"] = np.broadcast_to(i["L1_attn_bo"], (P, D))
    out["gate_bias1"] = np.broadcast_to(i["L1_ffn_expert_bias"], (P, E1))

    def shared_halves(a):
        return a.reshape(a.shape[0], ALWAYS1, INNER1).transpose(1, 0, 2)

    def in_chunks(a):
        a = a.reshape(PAIRS1, 2, *a.shape[1:])
        chunks = np.zeros((PAIRS1, *a.shape[2:-1], CHUNKS1, P), np.float32)
        for e in range(2):
            chunks[..., e, :] = a[:, e, ..., :P]
            chunks[..., 2, e * P // 2:e * P // 2 + TAIL1] = a[:, e, ..., P:]
        return chunks

    up = [in_chunks(np.concatenate([i[f"L1_ffn_w{n}"], shared_halves(i[f"L1_ffn_sw{n}"])])) for n in (1, 3)]
    up = np.stack([u.reshape(PAIRS1, KC, P, CHUNKS1, P) for u in up], axis=1)
    down = np.concatenate([i["L1_ffn_w2"], i["L1_ffn_sw2"].reshape(ALWAYS1, INNER1, D)])
    down = in_chunks(down.transpose(0, 2, 1))
    out["f1_pairs"] = np.concatenate([up.transpose(0, 3, 1, 2, 4, 5).reshape(PAIRS1, P, -1),
                                      down.transpose(0, 3, 2, 1).reshape(PAIRS1, P, -1)], axis=2)
    return {k: np.ascontiguousarray(v) for k, v in out.items()}


def kernel(**inputs):
    import numpy as np
    import concourse.bacc as bacc
    from concourse.bass_utils import run_bass_kernel_spmd

    nc = bacc.Bacc("TRN2", target_bir_lowering=False, num_devices=1)
    arrays = host_layout({k: np.asarray(v) for k, v in inputs.items()})
    aps = {k: nc.dram_tensor(f"in_{k}", v.shape, F32, kind="ExternalInput").ap() for k, v in arrays.items()}
    out = nc.dram_tensor("out", (1, T, D), F32, kind="ExternalOutput").ap()
    adaln_program(nc, aps, out)
    r = run_bass_kernel_spmd(nc, [{f"in_{k}": v for k, v in arrays.items()}], core_ids=[0])
    return r.results[0]["out"]
```

```python
from contextlib import ExitStack

from concourse import mybir
from concourse.alu_op_type import AluOpType as ALU

ACT = mybir.ActivationFunctionType
AX_X = mybir.AxisListType.X
F32 = mybir.dt.float32
F32R = mybir.dt.float32r
F16 = mybir.dt.float16
BF16 = mybir.dt.bfloat16

P = 128
T = 2048
D = 256
KC = D // P
NT = T // P
QB = 512
NB = T // QB
TPB = QB // P
EPS = 1e-5
MASKED = -1e30
LOWEST = -3e38


def f32(ap):
    return ap.bitcast(F32)


class Memory:

    def __init__(self, nc, ctx, prefix, reuse=False):
        self.nc, self.ctx, self.prefix, self.sems = nc, ctx, prefix, [] if reuse else None
        if reuse:
            ctx.callback(self.clear)

    def sb(self, name, shape, dt=F32):
        return self.ctx.enter_context(self.nc.sbuf_tensor(f"{self.prefix}_{name}", shape, dt))

    def ps(self, name, shape, dt=F32):
        return self.ctx.enter_context(self.nc.psum_tensor(f"{self.prefix}_{name}", shape, dt))

    def sem(self, name):
        if self.sems is None:
            return self.ctx.enter_context(self.nc.semaphore(f"{self.prefix}_{name}"))
        self.sems.append(self.nc.alloc_semaphore(name=f"{self.prefix}_{name}"))
        return self.sems[-1]

    def clear(self):
        self.nc.clear_and_free_semaphores(self.sems)
        self.nc.all_engine_barrier()



def setup_phase(nc, x_dram, c_dram, wmod_dram, x, ident, ident_bf, ident_h, mask_q, mask_t, coef, gate, stats):
    with ExitStack() as ctx:
        m = Memory(nc, ctx, "set")
        c_col = m.sb("c_col", [P, 2, KC])
        sig = m.sb("sig", [P, 2, KC])
        silu = m.sb("silu", [P, 2, KC])
        silu_bc = m.sb("silu_bc", [P, 2, KC, P])
        wmod = m.sb("wmod", [P, 2, KC, 6 * D])
        sign = m.sb("sign", [P, 2, 2, D])
        size = m.sb("size", [P, 2, 2, D])
        ps_col = m.ps("ps_col", [P, 2, 512])
        ps_gate = m.ps("ps_gate", [P, 2, 2, D])
        c_loaded, made = m.sem("c_loaded"), m.sem("made")
        w_loaded = [m.sem(f"w_loaded{layer}") for layer in range(2)]
        x_loaded = [m.sem(f"x_loaded{b}") for b in range(NB)]
        sig_ready, silu_ready = m.sem("sig_ready"), m.sem("silu_ready")
        cols_ready, gates_ready, dve_done = m.sem("cols_ready"), m.sem("gates_ready"), m.sem("dve_done")
        block = ctx.enter_context(nc.Block())

        @block.sync
        def _(sp):
            for layer in range(2):
                sp.dma_start(c_col[:, layer], c_dram[layer]).then_inc(c_loaded, 16)

            def load_wmod(layer):
                sp.dma_start(wmod[:, layer], wmod_dram[layer].rearrange("(k p) n -> p k n", p=P)).then_inc(w_loaded[layer], 16)

            load_wmod(0)
            xt = x_dram.rearrange("a (t p) d -> p (a t) d", p=P)
            for b in range(NB):
                if b == NB // 2:
                    load_wmod(1)
                sp.dma_start(x[:, b * TPB:(b + 1) * TPB], xt[:, b * TPB:(b + 1) * TPB]).then_inc(x_loaded[b], 16)

        @block.gpsimd
        def _(pool):
            nc.gpsimd.memset(ident[:], 0.0).then_inc(made, 1)
            nc.gpsimd.memset(mask_q[:], 0.0).then_inc(made, 1)
            nc.gpsimd.memset(mask_t[:], 0.0).then_inc(made, 1)
            pool.wait_ge(made, 3)
            nc.gpsimd.affine_select(out=ident[:], in_=ident[:], compare_op=ALU.not_equal, fill=1.0, base=0,
                                    pattern=[[-1, P]], channel_multiplier=1).then_inc(made, 1)
            nc.gpsimd.affine_select(out=mask_q[:], in_=mask_q[:], compare_op=ALU.is_ge, fill=MASKED, base=0,
                                    pattern=[[-1, P]], channel_multiplier=1).then_inc(made, 1)
            nc.gpsimd.affine_select(out=mask_t[:], in_=mask_t[:], compare_op=ALU.is_ge, fill=MASKED, base=0,
                                    pattern=[[1, P]], channel_multiplier=-1).then_inc(made, 1)

        @block.scalar
        def _(act):
            act.wait_ge(c_loaded, 32)
            nc.scalar.activation(sig[:], c_col[:], ACT.Sigmoid).then_inc(sig_ready, 1)

        @block.vector
        def _(dve):
            dve.wait_ge(made, 6)
            nc.vector.tensor_copy(ident_bf[:], ident[:]).then_inc(dve_done, 1)
            nc.vector.tensor_copy(ident_h[:], ident[:]).then_inc(dve_done, 1)
            dve.wait_ge(sig_ready, 1)
            nc.vector.tensor_tensor(silu[:], c_col[:], sig[:], ALU.mult).then_inc(silu_ready, 1)
            dve.wait_ge(silu_ready, 1)
            nc.vector.tensor_copy(silu_bc[:], silu[:].unsqueeze(3).broadcast_to([P, 2, KC, P])).then_inc(silu_ready, 1)
            for b in range(NB):
                dve.wait_ge(x_loaded[b], 16)
                for tile in range(b * TPB, (b + 1) * TPB):
                    nc.vector.bn_stats(stats[:, tile], x[:, tile])
            for layer in range(2):
                done = 2 + 8 * layer
                dve.wait_ge(cols_ready, layer + 1)
                nc.vector.tensor_copy(coef[:, layer], ps_col[:, layer, 0:8]).then_inc(dve_done, 1)
                dve.wait_ge(dve_done, done + 1)
                for k in range(2):
                    c = coef[:, layer, 4 * k + 2:4 * k + 4]
                    nc.vector.tensor_scalar(c, c, 1.0, None, ALU.add).then_inc(dve_done, 1)
                dve.wait_ge(gates_ready, layer + 1)
                g, size_g, sign_g = ps_gate[:, layer], size[:, layer], sign[:, layer]
                nc.vector.tensor_scalar(sign_g, g, 0.0, 2.0, ALU.is_ge, ALU.mult).then_inc(dve_done, 1)
                nc.vector.tensor_scalar(size_g, g, -1.0, None, ALU.mult).then_inc(dve_done, 1)
                dve.wait_ge(dve_done, done + 5)
                nc.vector.tensor_tensor(size_g, size_g, g, ALU.max).then_inc(dve_done, 1)
                dve.wait_ge(dve_done, done + 6)
                nc.vector.tensor_scalar(size_g, size_g, 0.25, None, ALU.max).then_inc(dve_done, 1)
                dve.wait_ge(dve_done, done + 7)
                nc.vector.scalar_tensor_tensor(gate[:, layer], sign_g, -1.0, size_g, ALU.add, ALU.mult).then_inc(dve_done, 1)

        @block.tensor
        def _(pe):
            chunk = [0, 1, 2, 3, 6, 7, 8, 9]
            pe.wait_ge(silu_ready, 2)
            for layer in range(2):
                pe.wait_ge(w_loaded[layer], 16)
                for j, c in enumerate(chunk):
                    for k in range(KC):
                        last = nc.tensor.matmul(ps_col[:, layer, j:j + 1], wmod[:, layer, k, c * P:(c + 1) * P],
                                                silu[:, layer, k:k + 1], start=(k == 0), stop=(k == KC - 1))
                last.then_inc(cols_ready, 1)
                for g in range(2):
                    for k in range(KC):
                        last = nc.tensor.matmul(ps_gate[:, layer, g], silu_bc[:, layer, k],
                                                wmod[:, layer, k, (2 + 3 * g) * D:(3 + 3 * g) * D],
                                                start=(k == 0), stop=(k == KC - 1))
                last.then_inc(gates_ready, 1)



class Beside:

    def __init__(self, loads=(), gated=(), splits=()):
        self.loads, self.gated, self.splits = loads, gated, splits

    def open(self, nc, m):
        self.nc = nc
        self.loaded, self.is_gated, self.hi_ready = m.sem("w_loaded"), m.sem("w_gated"), m.sem("w_hi_ready")

    def sync(self, sp):
        for to, dram in self.loads:
            sp.dma_start(to, dram).then_inc(self.loaded, 16)

    def gpsimd(self, pool):
        if self.loads:
            pool.wait_ge(self.loaded, 16 * len(self.loads))
        for to, w, gate in self.gated:
            self.nc.gpsimd.tensor_tensor(to, w, gate, ALU.mult).then_inc(self.is_gated, 1)
        if self.gated:
            pool.wait_ge(self.is_gated, len(self.gated))
        for hi, _, w in self.splits:
            self.nc.gpsimd.tensor_copy(hi, w).then_inc(self.hi_ready, 1)
        for n, (hi, lo, w) in enumerate(self.splits):
            pool.wait_ge(self.hi_ready, n + 1)
            self.nc.gpsimd.tensor_tensor(lo, w, f32(hi), ALU.subtract)


def norm_phase(nc, name, x, ident, shift_scale, h_hi, h_lo, beside, stats):
    with ExitStack() as ctx:
        m = Memory(nc, ctx, name)
        mv = m.sb("mv", [P, NT, 2])
        std = m.sb("std", [P, NT])
        rstd = m.sb("rstd", [P, NT])
        xn = m.sb("xn", [P, NT, D])
        h32 = m.sb("h32", [P, 2, QB])
        ps = m.ps("ps", [P, 4, QB])
        stat_done, std_ready, xn_ready = m.sem("stat_done"), m.sem("std_ready"), m.sem("xn_ready")
        turned, h32_ready, hi_ready, lo_ready = m.sem("turned"), m.sem("h32_ready"), m.sem("hi_ready"), m.sem("lo_ready")
        beside.open(nc, m)
        block = ctx.enter_context(nc.Block())
        units = [(b, k) for b in range(NB) for k in range(KC)]

        @block.sync
        def _(sp):
            beside.sync(sp)

        @block.gpsimd
        def _(pool):
            beside.gpsimd(pool)

        @block.vector
        def _(dve):
            for t in range(NT):
                nc.vector.bn_aggr(mv[:, t], stats[:, t]).then_inc(stat_done, 1)
            dve.wait_ge(stat_done, NT)
            nc.vector.tensor_scalar(rstd[:], mv[:, :, 1], EPS, None, ALU.add).then_inc(stat_done, 1)
            dve.wait_ge(std_ready, 1)
            nc.vector.reciprocal(rstd[:], std[:]).then_inc(stat_done, 1)
            dve.wait_ge(stat_done, NT + 2)

            def normalize(b):
                for t in range(b * TPB, (b + 1) * TPB):
                    nc.vector.tensor_scalar(xn[:, t], x[:, t], mv[:, t, 0:1], rstd[:, t:t + 1],
                                            ALU.subtract, ALU.mult).then_inc(xn_ready, 1)

            normalize(0)
            for n, (b, k) in enumerate(units):
                if k == 0 and b + 1 < NB:
                    normalize(b + 1)
                dve.wait_ge(hi_ready, n + 1)
                nc.vector.tensor_tensor(h_lo[:, k, b * QB:(b + 1) * QB], h32[:, n % 2],
                                        f32(h_hi[:, k, b * QB:(b + 1) * QB]), ALU.subtract).then_inc(lo_ready, 1)

        @block.tensor
        def _(pe):
            for n, (b, k) in enumerate(units):
                pe.wait_ge(xn_ready, (b + 1) * TPB)
                if n >= 4:
                    pe.wait_ge(h32_ready, n - 3)
                for j in range(TPB):
                    last = nc.tensor.transpose(ps[:, n % 4, j * P:(j + 1) * P],
                                               xn[:, b * TPB + j, k * P:(k + 1) * P], ident[:])
                last.then_inc(turned, 1)

        @block.scalar
        def _(act):
            act.wait_ge(stat_done, NT + 1)
            nc.scalar.activation(std[:], rstd[:], ACT.Sqrt).then_inc(std_ready, 1)
            for n, (b, k) in enumerate(units):
                act.wait_ge(turned, n + 1)
                if n >= 2:
                    act.wait_ge(lo_ready, n - 1)
                nc.scalar.activation(h32[:, n % 2], ps[:, n % 4], ACT.Identity,
                                     bias=shift_scale[:, k:k + 1], scale=shift_scale[:, 2 + k:3 + k]).then_inc(h32_ready, 1)
                act.wait_ge(h32_ready, n + 1)
                nc.scalar.activation(h_hi[:, k, b * QB:(b + 1) * QB], h32[:, n % 2], ACT.Copy).then_inc(hi_ready, 1)



HEADS0 = 16
DH0 = 128
WO_SCALE = 64.0
PV_LAG0 = 4
PREP_UNITS0, SPLIT_UNIT0 = 34, 14
UNITS = [(qb, kt) for qb in range(NB) for kt in range(TPB * (qb + 1))]
MAXES = [(qt, kb) for qt in range(NT) for kb in range(qt // TPB + 1)]


def first_col(qb, kt):
    return P * max(0, kt - TPB * qb)


def attention0_steps():
    def prep(h):
        items = [("QK", h, which, b) for b in range(NB) for which in "KQ"]
        if h % 2 == 0:
            items += [("V", h, tp) for tp in range(NT // 2)]
        return items + [("MAX", h, qt, kb) for qt, kb in MAXES]

    def cost(item):
        return 0.8 if item[0] == "MAX" else 1.3

    start = [("LOADW", 0), ("LOADW", 1), ("SPLIT", 0), ("LOADW", 2)]
    start += prep(0) + [("COMBINE", 0)] + [("BCAST", 0, b) for b in range(NB)]
    periods = []
    late = []
    for h in range(HEADS0):
        steps = []

        def tick():
            nonlocal late
            due = [s for n, s in late if n == 0]
            late = [(n - 1, s) for n, s in late if n > 0]
            steps.extend(due)

        ahead = prep(h + 1) if h + 1 < HEADS0 else []
        whole = sum(map(cost, ahead))
        spent = 0.0
        for u, (qb, kt) in enumerate(UNITS):
            steps += [("S", h, u), ("SUB", h, u)]
            while ahead and spent < whole * (u + 1) / PREP_UNITS0:
                spent += cost(ahead[0])
                steps.append(ahead.pop(0))
            if h + 1 < HEADS0:
                if u == len(UNITS) - NB - 1:
                    steps.append(("COMBINE", h + 1))
                if u >= len(UNITS) - NB:
                    steps.append(("BCAST", h + 1, u - (len(UNITS) - NB)))
                if u == SPLIT_UNIT0:
                    steps.append(("SPLIT", h + 1))
                    steps.append(("LOADW", h + 3))
            late += [(0, ("EXP", h, u)), (0, ("LO", h, u))]
            tick()
            late.append((PV_LAG0 + (kt == 0), ("PV", h, u)))
            if kt == TPB * (qb + 1) - 1:
                late += [(PV_LAG0, ("ZNORM", h, qb)), (PV_LAG0 + 1, ("ZLO", h, qb)), (PV_LAG0 + 3, ("ZTURN", h, qb)),
                         (PV_LAG0 + 5, ("WO", h, qb, 0)), (PV_LAG0 + 5, ("WO", h, qb, 1))]
            if h % 2 == 0 and u == 4:
                steps.append(("VCOPY", h + 1))
        periods.append(steps)
    tail = []
    while late:
        tail += [s for n, s in late if n == 0]
        late = [(n - 1, s) for n, s in late if n > 0]
    return start, periods, tail


STREAMS = {"S": "S", "QK": "AUX", "V": "AUX", "MAX": "AUX", "WO": "AUX", "ZTURN": "T", "BCAST": "T",
           "ZNORM": "Z", "SPLIT": "W", "COMBINE": "C", "VCOPY": "VC"}
HI_STREAM = {"QK": "HI", "V": "HI"}


def number_steps(steps, streams):
    place, length = {}, {}
    for s in steps:
        if s[0] in streams:
            stream = streams[s[0]]
            place[s] = length.get(stream, 0)
            length[stream] = place[s] + 1
    return place, length


class Attention0Weights:

    def __init__(self, nc, ctx):
        m = Memory(nc, ctx, "wa")
        self.stage = [m.sb("stage_even", [P, 768]), m.sb("stage_odd", [P, 1280])]
        self.qk_hi = [m.sb(f"wqk_hi{i}", [P, KC, 2, P], F32R) for i in range(2)]
        self.qk_lo = [m.sb(f"wqk_lo{i}", [P, KC, 2, P], F32R) for i in range(2)]
        self.v_hi, self.v_lo = m.sb("wv_hi", [P, KC, 2 * P], F32R), m.sb("wv_lo", [P, KC, 2 * P], F32R)

    def beside(self, w_odd):
        stage = self.stage[1]
        qk = [w[1][:].rearrange("p k c n -> p (k c n)") for w in (self.qk_hi, self.qk_lo)]
        v = [w[:].rearrange("p k n -> p (k n)") for w in (self.v_hi, self.v_lo)]
        return Beside([(stage[:], w_odd[0])], splits=[(*qk, stage[:, 0:512]), (*v, stage[:, 512:1024])])


def attention0_phase(nc, w, w_even, w_odd, x, h_hi, h_lo, ident_bf, ident_h, mask_q, mask_t, gate_row, stats):
    start, periods, tail = attention0_steps()
    place, _ = number_steps(start + sum(periods, []) + tail, STREAMS)
    hi_place, _ = number_steps(start + sum(periods, []), HI_STREAM)
    one_round = number_steps(periods[1] + periods[2], STREAMS)[1] | number_steps(periods[1] + periods[2], HI_STREAM)[1]
    for a in (1, 2):
        for h in range(a, HEADS0 - 1, 2):
            assert [(s[0], s[1] - h + a, *s[2:]) for s in periods[h]] == periods[a]
    scale = DH0 ** -0.5
    SB, AB, PR, EB, SR = 2, 3, 8, 4, 4
    assert one_round["AUX"] % AB == 0 and len(UNITS) % PR == 0

    with ExitStack() as ctx:
        m = Memory(nc, ctx, "a0", reuse=True)
        stage, wqk_hi, wqk_lo, wv_hi, wv_lo = w.stage, w.qk_hi, w.qk_lo, w.v_hi, w.v_lo
        wo_gated = m.sb("wo_gated", [P, D])
        wo_hi = [m.sb(f"wo_hi{i}", [P, D], F16) for i in range(2)]
        wo_lo = [m.sb(f"wo_lo{i}", [P, D], F16) for i in range(2)]
        gate64 = m.sb("gate64", [P, D])
        q_hi, q_lo = m.sb("q_hi", [P, 2, T], F16), m.sb("q_lo", [P, 2, T], F16)
        k_hi, k_lo = m.sb("k_hi", [P, 2, T], F16), m.sb("k_lo", [P, 2, T], F16)
        EVEN, ODD, NEXT_ODD = range(3)
        v_hi = [m.sb(f"v_hi{i}", [P, NT, P + 2], F16) for i in range(3)]
        v_lo = [m.sb(f"v_lo{i}", [P, NT, P], F16) for i in range(3)]
        partial = m.sb("partial", [P, NT, NB])
        neg_max = m.sb("neg_max", [P, NT], F16)
        neg_rows = m.sb("neg_rows", [P, 2, T], F16)
        s32 = m.sb("s32", [P, SR, QB])
        p32 = m.sb("p32", [P, EB, QB])
        p_hi, p_lo = m.sb("p_hi", [P, PR, QB], F16), m.sb("p_lo", [P, PR, QB], F16)
        rden = m.sb("rden", [P, 2, 2])
        zn = m.sb("zn", [P, TPB, P])
        z_hi, z_lo = m.sb("z_hi", [P, TPB, P], F16), m.sb("z_lo", [P, TPB, P], F16)
        z_t = m.sb("z_t", [P, 2, TPB, P], F16)
        ps_s = m.ps("ps_s", [P, SB, QB])
        ps_z = m.ps("ps_z", [P, 2, 2, 256])
        ps_t = m.ps("ps_t", [P, QB])
        ps_aux = m.ps("ps_aux", [P, AB, QB])

        const_ready = m.sem("const_ready")
        w_loaded = [m.sem("w_loaded_even"), m.sem("w_loaded_odd")]
        gated, w_ready = m.sem("gated"), m.sem("w_ready")
        w_hi_ready = [m.sem("w_hi_ready_even"), m.sem("w_hi_ready_odd")]
        s_filled, s_read, s_exped, p_lo_ready = m.sem("s_filled"), m.sem("s_read"), m.sem("s_exped"), m.sem("p_lo_ready")
        pv_done = m.sem("pv_done")
        aux_filled, aux_hi, aux_free = m.sem("aux_filled"), m.sem("aux_hi"), m.sem("aux_free")
        max_ready = m.sem("max_ready")
        t_filled, t_free = m.sem("t_filled"), m.sem("t_free")
        rden_ready, z_free, z_hi_ready, z_lo_ready = m.sem("rden_ready"), m.sem("z_free"), m.sem("z_hi_ready"), m.sem("z_lo_ready")
        v_copied = m.sem("v_copied")
        block = ctx.enter_context(nc.Block())

        def whole_program(eng, step):
            def in_line(n, stream):
                return n

            for s in start + periods[0]:
                step(s, in_line, 0)
            with eng.Fori(0, (HEADS0 - 2) // 2) as i:
                for s in periods[1] + periods[2]:
                    step(s, lambda n, stream: n + i * one_round[stream], i)
            for s in periods[HEADS0 - 1] + tail:
                step(s, in_line, 0)

        def weight_set(period):
            return (1, (period + 1) // 2) if period % 2 else (0, period // 2)

        def turned_before(h, qb):
            if (h, qb) == (0, 0):
                return 1
            hb, qbb = (h, qb - 1) if qb else (h - 1, NB - 1)
            return place["ZTURN", hb, qbb] + 1

        def pv(h, u):
            return place["S", h, u]

        @block.sync
        def _(sp):
            def step(s, at, i):
                kind, h = s[0], s[1]
                if kind == "LOADW":
                    parity, j = weight_set(h)
                    if h > 1:
                        sp.wait_ge(w_ready, at(place["SPLIT", h - 2], "W") + 1)
                    src = w_odd if parity else w_even
                    sp.dma_start(stage[parity][:], src[i + j]).then_inc(w_loaded[parity], 16)

            whole_program(sp, step)
            for parity in range(2):
                sp.wait_ge(w_loaded[parity], 16 * (HEADS0 // 2 + 1))

        @block.gpsimd
        def _(pool):
            pool.sem_inc(p_lo_ready, EB)
            for i in range(3):
                nc.gpsimd.memset(v_hi[i][:, :, P:P + 2], 1.0).then_inc(const_ready, 1)
            nc.gpsimd.memset(partial[:], LOWEST).then_inc(const_ready, 1)
            nc.gpsimd.tensor_scalar(gate64[:], gate_row, WO_SCALE, None, ALU.mult).then_inc(gated, 1)
            pool.wait_ge(gated, 1)

            def step(s, at, i):
                kind, h = s[0], s[1]
                if kind == "SPLIT":
                    parity, j = weight_set(h)
                    n = at(place[s], "W")
                    pool.wait_ge(w_loaded[parity], 16 * (i + j + 1 - parity))
                    w = stage[parity]
                    if h > 0:
                        pool.wait_ge(w_ready, n)
                    nc.gpsimd.tensor_tensor(wo_gated[:], w[:, -D:], gate64[:], ALU.mult).then_inc(gated, 1)
                    pool.wait_ge(w_hi_ready[parity], (2 + parity) * (i + j + 1 - parity))
                    nc.gpsimd.tensor_tensor(wqk_lo[parity][:].rearrange("p k c n -> p (k c n)"), w[:, 0:512],
                                            f32(wqk_hi[parity][:]).rearrange("p k c n -> p (k c n)"), ALU.subtract)
                    if parity:
                        nc.gpsimd.tensor_tensor(wv_lo[:].rearrange("p k n -> p (k n)"), w[:, 512:1024],
                                                f32(wv_hi[:]).rearrange("p k n -> p (k n)"), ALU.subtract)
                    nc.gpsimd.tensor_tensor(wo_lo[parity][:], wo_gated[:], wo_hi[parity][:], ALU.subtract).then_inc(w_ready, 1)

                elif kind == "LO":
                    u = s[2]
                    n = at(place["S", h, u], "S")
                    c = first_col(*UNITS[u])
                    pool.wait_ge(s_exped, n + 1 + SR)
                    nc.gpsimd.tensor_tensor(p_lo[:, u % PR, c:QB], p32[:, u % EB, c:QB], p_hi[:, u % PR, c:QB], ALU.subtract).then_inc(p_lo_ready, 1)

            whole_program(pool, step)

        @block.tensor
        def _(pe):
            pe.wait_ge(const_ready, 4)
            pe.sem_inc(pv_done, PR)

            def step(s, at, i):
                kind, h = s[0], s[1]
                if kind in ("QK", "V", "MAX", "WO"):
                    n = place[s]
                    pe.wait_ge(aux_free, at(n, "AUX") + 1)
                    bank = ps_aux[:, n % AB]
                    par = (h + 1) % 2
                if kind == "QK":
                    which, b = s[2:]
                    if b == 0 and h > 0:
                        pe.wait_ge(w_ready, at(place["SPLIT", h - 1], "W") + 1)
                    col = "QK".index(which)
                    tok = slice(b * QB, (b + 1) * QB)
                    for k in range(KC):
                        for w, act in ((wqk_hi, h_hi), (wqk_hi, h_lo), (wqk_lo, h_hi)):
                            last = nc.tensor.matmul(bank, w[par][:, k, col], act[:, k, tok],
                                                    start=(k == 0 and w is wqk_hi and act is h_hi),
                                                    stop=(k == KC - 1 and w is wqk_lo))
                    last.then_inc(aux_filled, 1)
                elif kind == "V":
                    for j in range(2):
                        tok = slice((2 * s[2] + j) * P, (2 * s[2] + j + 1) * P)
                        for k in range(KC):
                            for act, w in ((h_hi, wv_hi), (h_hi, wv_lo), (h_lo, wv_hi)):
                                last = nc.tensor.matmul(bank[:, j * 256:(j + 1) * 256], act[:, k, tok], w[:, k],
                                                        start=(k == 0 and act is h_hi and w is wv_hi),
                                                        stop=(k == KC - 1 and act is h_lo))
                    last.then_inc(aux_filled, 1)
                elif kind == "MAX":
                    qt, kb = s[2:]
                    if kb == 0:
                        pe.wait_ge(aux_hi, at(hi_place["QK", h, "Q", qt // TPB], "HI") + 1)
                    diagonal = kb == qt // TPB
                    n = min(QB, (qt + 1) * P - kb * QB)
                    nc_last = nc.tensor.matmul(bank[:, 0:n], q_hi[:, h % 2, qt * P:(qt + 1) * P],
                                               k_hi[:, h % 2, kb * QB:kb * QB + n], start=True, stop=not diagonal)
                    if diagonal:
                        nc_last = nc.tensor.matmul(bank[:, n - P:n], ident_bf[:], mask_q[:], start=False, stop=True)
                    nc_last.then_inc(aux_filled, 1)
                elif kind == "WO":
                    qb, pair = s[2:]
                    pe.wait_ge(t_free, at(place["ZTURN", h, qb], "T") + 2)
                    for j in range(2):
                        t = 2 * pair + j
                        for a, w in ((0, wo_hi), (0, wo_lo), (1, wo_hi)):
                            last = nc.tensor.matmul(bank[:, j * D:(j + 1) * D], z_t[:, a, t], w[h % 2][:],
                                                    start=(a == 0 and w is wo_hi), stop=(a == 1))
                    last.then_inc(aux_filled, 1)
                elif kind == "S":
                    u = s[2]
                    qb, kt = UNITS[u]
                    if u == 0:
                        pe.wait_ge(aux_free, at(place["MAX", h, NT - 1, NB - 1], "AUX") + 1 + AB)
                        if h % 2:
                            pe.wait_ge(v_copied, 2 * (at(place["VCOPY", h], "VC") + 1))
                    pe.wait_ge(s_read, at(place[s], "S") + 1)
                    c = first_col(qb, kt)
                    out = ps_s[:, u % SB, c:QB]
                    keys = slice(kt * P, (kt + 1) * P)
                    q = slice(qb * QB + c, (qb + 1) * QB)
                    nc.tensor.matmul(out, k_hi[:, h % 2, keys], q_hi[:, h % 2, q], start=True, stop=False)
                    nc.tensor.matmul(out, k_hi[:, h % 2, keys], q_lo[:, h % 2, q], start=False, stop=False)
                    diagonal = kt >= TPB * qb
                    last = nc.tensor.matmul(out, k_lo[:, h % 2, keys], q_hi[:, h % 2, q], start=False, stop=not diagonal)
                    if diagonal:
                        last = nc.tensor.matmul(ps_s[:, u % SB, c:c + P], ident_bf[:], mask_t[:], start=False, stop=True)
                    last.then_inc(s_filled, 1)
                elif kind == "PV":
                    u = s[2]
                    qb, kt = UNITS[u]
                    if kt == 0:
                        pe.wait_ge(z_free, at(place["ZNORM", h, qb], "Z") + 1)
                    pe.wait_ge(p_lo_ready, at(pv(h, u), "S") + 1 + EB)
                    v = ODD if h % 2 else EVEN
                    for t in range(first_col(qb, kt) // P, TPB):
                        q = slice(t * P, (t + 1) * P)
                        end = t % 2 == 1 and kt == TPB * qb + t
                        z = ps_z[:, t // 2, t % 2]
                        nc.tensor.matmul(z[:, 0:P + 1], p_hi[:, u % PR, q], v_hi[v][:, kt, 0:P + 1], start=(kt == 0 and t % 2 == 0), stop=False)
                        nc.tensor.matmul(z[:, 0:P], p_hi[:, u % PR, q], v_lo[v][:, kt], start=False, stop=False)
                        last = nc.tensor.matmul(z[:, 0:P + 1], p_lo[:, u % PR, q], v_hi[v][:, kt, 0:P + 1], start=False, stop=end)
                    last.then_inc(pv_done, 1)
                elif kind == "ZTURN":
                    qb = s[2]
                    pe.wait_ge(t_free, at(place[s], "T") + 1)
                    pe.wait_ge(z_lo_ready, at(place["ZNORM", h, qb], "Z") + 1)
                    pt = ps_t[:].bitcast(F16).rearrange("p (a t n) -> p a t n", a=2, t=TPB)
                    for a, z in enumerate((z_hi, z_lo)):
                        for t in range(TPB):
                            last = nc.tensor.transpose(pt[:, a, t], z[:, t], ident_h[:])
                    last.then_inc(t_filled, 1)
                elif kind == "BCAST":
                    pe.wait_ge(t_free, at(place[s], "T") + 1)
                    pe.wait_ge(max_ready, at(place["COMBINE", h], "C") + 1)
                    for t in range(TPB):
                        column = neg_max[:, s[2] * TPB + t:s[2] * TPB + t + 1].broadcast_to([P, P])
                        last = nc.tensor.matmul(ps_t[:, t * P:(t + 1) * P], column, ident_h[:], start=(t == 0), stop=(t == TPB - 1))
                    last.then_inc(t_filled, 1)

            whole_program(pe, step)

        @block.scalar
        def _(act):
            act.sem_inc(s_exped, SR)
            act.sem_inc(t_free, 1)

            def step(s, at, i):
                kind, h = s[0], s[1]
                if kind == "SPLIT":
                    parity, j = weight_set(h)
                    act.wait_ge(w_loaded[parity], 16 * (i + j + 1 - parity))
                    w = stage[parity]
                    if h >= 2:
                        act.wait_ge(aux_filled, at(place["WO", h - 2, NB - 1, 1], "AUX") + 1)
                    elif h == 1:
                        act.wait_ge(aux_filled, place["V", 0, NT // 2 - 1] + 1)
                    nc.scalar.activation(wqk_hi[parity][:].rearrange("p k c n -> p (k c n)"), w[:, 0:512], ACT.Copy).then_inc(w_hi_ready[parity], 1)
                    if parity:
                        nc.scalar.activation(wv_hi[:].rearrange("p k n -> p (k n)"), w[:, 512:1024], ACT.Copy).then_inc(w_hi_ready[parity], 1)
                    act.wait_ge(gated, at(place[s], "W") + 2)
                    nc.scalar.activation(wo_hi[parity][:], wo_gated[:], ACT.Copy).then_inc(w_hi_ready[parity], 1)
                elif kind == "QK":
                    which, b = s[2:]
                    n = place[s]
                    act.wait_ge(aux_filled, at(n, "AUX") + 1)
                    out = (q_hi if which == "Q" else k_hi)[:, h % 2, b * QB:(b + 1) * QB]
                    nc.scalar.activation(out, ps_aux[:, n % AB], ACT.Copy).then_inc(aux_hi, 1)
                elif kind == "V":
                    n = place[s]
                    act.wait_ge(aux_filled, at(n, "AUX") + 1)
                    src = ps_aux[:, n % AB].rearrange("p (t h e) -> p t h e", t=2, h=2)
                    t = slice(2 * s[2], 2 * s[2] + 2)
                    nc.scalar.activation(v_hi[EVEN][:, t, 0:P], src[:, :, 0], ACT.Copy)
                    if s[2] == 0 and h >= 2:
                        act.wait_ge(v_copied, 2 * at(place["VCOPY", h - 1], "VC") + 2)
                    nc.scalar.activation(v_hi[NEXT_ODD][:, t, 0:P], src[:, :, 1], ACT.Copy).then_inc(aux_hi, 1)
                elif kind == "EXP":
                    u = s[2]
                    c = first_col(*UNITS[u])
                    n = at(place["S", h, u], "S")
                    act.wait_ge(s_read, n + 1 + SB)
                    act.wait_ge(p_lo_ready, n + 1)
                    act.wait_ge(pv_done, n + 1)
                    nc.scalar.activation(p32[:, u % EB, c:QB], s32[:, u % SR, c:QB], ACT.Exp, scale=scale)
                    nc.scalar.activation(p_hi[:, u % PR, c:QB], s32[:, u % SR, c:QB], ACT.Exp, scale=scale).then_inc(s_exped, 1)
                elif kind == "ZLO":
                    n = at(place["ZNORM", h, s[2]], "Z")
                    act.wait_ge(z_free, n + 2)
                    act.wait_ge(t_filled, at(turned_before(h, s[2]), "T"))
                    nc.scalar.activation(z_hi[:], zn[:], ACT.Copy).then_inc(z_hi_ready, 1)
                elif kind == "ZTURN":
                    n = at(place[s], "T")
                    act.wait_ge(t_filled, n + 1)
                    if (h, s[2]) != (0, 0):
                        hb, qbb = (h, s[2] - 1) if s[2] else (h - 1, NB - 1)
                        act.wait_ge(aux_filled, at(place["WO", hb, qbb, 1], "AUX") + 1)
                    nc.scalar.activation(z_t[:].rearrange("p a t n -> p (a t n)"), ps_t[:].bitcast(F16), ACT.Copy).then_inc(t_free, 1)
                elif kind == "BCAST":
                    act.wait_ge(t_filled, at(place[s], "T") + 1)
                    nc.scalar.activation(neg_rows[:, h % 2, s[2] * QB:(s[2] + 1) * QB], ps_t[:], ACT.Copy).then_inc(t_free, 1)

            whole_program(act, step)

        @block.vector
        def _(dve):
            dve.sem_inc(aux_free, AB)
            dve.sem_inc(z_free, 1)
            dve.sem_inc(s_read, SB)
            dve.wait_ge(const_ready, 4)

            def step(s, at, i):
                kind, h = s[0], s[1]
                if kind == "QK":
                    which, b = s[2:]
                    n = place[s]
                    dve.wait_ge(aux_hi, at(hi_place[s], "HI") + 1)
                    hi, lo = (q_hi, q_lo) if which == "Q" else (k_hi, k_lo)
                    tok = slice(b * QB, (b + 1) * QB)
                    nc.vector.tensor_tensor(lo[:, h % 2, tok], ps_aux[:, n % AB], hi[:, h % 2, tok], ALU.subtract).then_inc(aux_free, 1)
                elif kind == "V":
                    n = place[s]
                    dve.wait_ge(aux_hi, at(hi_place[s], "HI") + 1)
                    src = ps_aux[:, n % AB].rearrange("p (t h e) -> p t h e", t=2, h=2)
                    t = slice(2 * s[2], 2 * s[2] + 2)
                    nc.vector.tensor_tensor(v_lo[EVEN][:, t], src[:, :, 0], v_hi[EVEN][:, t, 0:P], ALU.subtract)
                    nc.vector.tensor_tensor(v_lo[NEXT_ODD][:, t], src[:, :, 1], v_hi[NEXT_ODD][:, t, 0:P], ALU.subtract).then_inc(aux_free, 1)
                elif kind == "MAX":
                    qt, kb = s[2:]
                    n = place[s]
                    dve.wait_ge(aux_filled, at(n, "AUX") + 1)
                    if (qt, kb) == (0, 0) and h > 0:
                        dve.wait_ge(max_ready, at(place["COMBINE", h], "C"))
                    cols = min(QB, (qt + 1) * P - kb * QB)
                    nc.vector.tensor_reduce(partial[:, qt, kb:kb + 1], ps_aux[:, n % AB, 0:cols], AX_X, ALU.max).then_inc(aux_free, 1)
                elif kind == "COMBINE":
                    n = at(place[s], "C")
                    dve.wait_ge(aux_free, at(place["MAX", h, NT - 1, NB - 1], "AUX") + 1 + AB)
                    if h > 0:
                        dve.wait_ge(t_filled, at(place["BCAST", h - 1, NB - 1], "T") + 1)
                    nc.vector.tensor_reduce(neg_max[:], partial[:], AX_X, ALU.max, negate=True).then_inc(max_ready, 1)
                elif kind == "WO":
                    qb, pair = s[2:]
                    n = place[s]
                    dve.wait_ge(aux_filled, at(n, "AUX") + 1)
                    xs = x[:, qb * TPB + 2 * pair:qb * TPB + 2 * pair + 2].rearrange("p t d -> p (t d)")
                    nc.vector.scalar_tensor_tensor(xs, ps_aux[:, n % AB], 1.0 / WO_SCALE, xs, ALU.mult, ALU.add).then_inc(aux_free, 1)
                    if h == HEADS0 - 1:
                        dve.wait_ge(aux_free, n + 1 + AB)
                        for t in range(qb * TPB + 2 * pair, qb * TPB + 2 * pair + 2):
                            nc.vector.bn_stats(stats[:, t], x[:, t])
                elif kind == "SUB":
                    u = s[2]
                    qb, kt = UNITS[u]
                    n = at(place["S", h, u], "S")
                    c = first_col(qb, kt)
                    if u == 0:
                        dve.wait_ge(t_free, at(place["BCAST", h, NB - 1], "T") + 2)
                    dve.wait_ge(s_filled, n + 1)
                    dve.wait_ge(s_exped, n + 1)
                    nc.vector.tensor_tensor(s32[:, u % SR, c:QB], ps_s[:, u % SB, c:QB],
                                            neg_rows[:, h % 2, qb * QB + c:(qb + 1) * QB], ALU.add).then_inc(s_read, 1)
                elif kind == "ZNORM":
                    qb = s[2]
                    n = at(place[s], "Z")
                    dve.wait_ge(pv_done, at(pv(h, UNITS.index((qb, TPB * (qb + 1) - 1))), "S") + 1 + PR)
                    if (h, qb) != (0, 0):
                        dve.wait_ge(z_lo_ready, n)
                    nc.vector.reciprocal(rden[:], ps_z[:, :, :, P]).then_inc(rden_ready, 1)
                    dve.wait_ge(rden_ready, n + 1)
                    nc.vector.tensor_tensor(zn[:].rearrange("p (a b) n -> p a b n", a=2), ps_z[:, :, :, 0:P],
                                            rden[:].unsqueeze(3).broadcast_to([P, 2, 2, P]), ALU.mult).then_inc(z_free, 1)
                elif kind == "ZLO":
                    n = at(place["ZNORM", h, s[2]], "Z")
                    dve.wait_ge(z_hi_ready, n + 1)
                    nc.vector.tensor_tensor(z_lo[:], zn[:], z_hi[:], ALU.subtract).then_inc(z_lo_ready, 1)

                elif kind == "VCOPY":
                    dve.wait_ge(aux_free, at(place["V", h - 1, NT // 2 - 1], "AUX") + 1 + AB)
                    if h > 2:
                        dve.wait_ge(pv_done, at(pv(h - 2, len(UNITS) - 1), "S") + 1 + PR)
                    nc.vector.tensor_copy(v_hi[ODD][:, :, 0:P], v_hi[NEXT_ODD][:, :, 0:P]).then_inc(v_copied, 1)
                    nc.vector.tensor_copy(v_lo[ODD][:], v_lo[NEXT_ODD][:]).then_inc(v_copied, 1)

            whole_program(dve, step)



def routing_phase(nc, name, gw, bias, cw_dram, h_hi, h_lo, ident_h, experts, groups, group_best,
                  top_k, route_scale, always, beside):
    E, G, A = experts, groups, always
    per = E // G
    with ExitStack() as ctx:
        m = Memory(nc, ctx, name)
        gw_x = m.sb("gw_x", [P, KC, 2 * P], F32R)
        gw_zero = m.sb("gw_zero", [P, KC, 2 * P])
        logit = m.sb("logit", [P, NT, E])
        score = m.sb("score", [P, NT, E])
        biased = m.sb("biased", [P, NT, E])
        best = m.sb("best", [P, NT, G, 8])
        gscore = m.sb("gscore", [P, NT, G])
        ahead = m.sb("ahead", [P, NT, G, G])
        chosen_g = m.sb("chosen_g", [P, NT, G])
        penalty = m.sb("penalty", [P, NT, G])
        top = m.sb("top", [P, NT, 8])
        above = m.sb("above", [P, NT, E])
        equal = m.sb("equal", [P, NT, E])
        carry = m.sb("carry", [P, NT, E])
        order = m.sb("order", [P, NT, E])
        room = m.sb("room", [P, NT])
        weight = m.sb("weight", [P, NT, E])
        total = m.sb("total", [P, NT])
        parts = m.sb("parts", [P, NT, E + A, 2], F16)
        rows = m.sb("rows", [2 * (E + A), T], F16)
        ps = m.ps("ps", [P, 4, 2, 256])
        ps_r = m.ps("ps_r", [P, 2, 1024], F16)
        step_done = m.sem("step_done")
        gw_ready, filled, first_read, freed = m.sem("gw_ready"), m.sem("filled"), m.sem("first_read"), m.sem("freed")
        scored, parts_ready, turned, rows_ready, stored = (m.sem("scored"), m.sem("parts_ready"), m.sem("turned"),
                                                           m.sem("rows_ready"), m.sem("stored"))
        hi_done = m.sem("hi_done")
        beside.open(nc, m)
        block = ctx.enter_context(nc.Block())

        @block.gpsimd
        def _(pool):
            beside.gpsimd(pool)

        @block.sync
        def _(sp):
            beside.sync(sp)
            sp.wait_ge(rows_ready, 2)
            sp.dma_start(cw_dram, rows[:]).then_inc(stored, 16)
            sp.wait_ge(stored, 16)

        @block.tensor
        def _(pe):
            pe.wait_ge(gw_ready, 1)
            for n in range(NT // 2):
                if n >= 4:
                    pe.wait_ge(freed, n - 3)
                for j in range(2):
                    tok = slice((2 * n + j) * P, (2 * n + j + 1) * P)
                    for k in range(KC):
                        for h in (h_hi, h_lo):
                            last = nc.tensor.matmul(ps[:, n % 4, j], h[:, k, tok], gw_x[:, k],
                                                    start=(k == 0 and h is h_hi), stop=(k == KC - 1 and h is h_lo))
                last.then_inc(filled, 1)
            pe.wait_ge(parts_ready, 1)
            for t in range(NT):
                last = nc.tensor.transpose(ps_r[0:2 * (E + A), t // 8, (t % 8) * P:(t % 8 + 1) * P],
                                           parts[:, t].rearrange("p e a -> p (e a)"), ident_h[:])
                if t % 8 == 7:
                    last.then_inc(turned, 1)

        @block.scalar
        def _(act):
            act.wait_ge(step_done, 1)
            nc.scalar.activation(gw_x[:], gw_zero[:], ACT.Copy).then_inc(hi_done, 1)
            act.wait_ge(hi_done, 1)
            nc.scalar.activation(gw_x[:, :, 0:E], gw[:], ACT.Copy).then_inc(hi_done, 1)
            for n in range(NT // 2):
                act.wait_ge(filled, n + 1)
                nc.scalar.activation(logit[:, 2 * n:2 * n + 2], ps[:, n % 4, :, 0:E], ACT.Copy).then_inc(first_read, 1)
            act.wait_ge(freed, NT // 2)
            nc.scalar.activation(score[:], logit[:], ACT.Sigmoid).then_inc(scored, 1)
            for half in range(2):
                act.wait_ge(turned, half + 1)
                nc.scalar.activation(rows[:, half * 1024:(half + 1) * 1024], ps_r[0:2 * (E + A), half], ACT.Copy).then_inc(rows_ready, 1)

        @block.vector
        def _(dve):
            done = [0]

            def chain(instruction):
                done[0] += 1
                instruction.then_inc(step_done, 1)
                dve.wait_ge(step_done, done[0])

            def over_experts(ap):
                return ap.unsqueeze(3).broadcast_to([P, NT, G, per])

            def grouped(tile):
                return tile[:].rearrange("p t (g e) -> p t g e", g=G)

            chain(nc.vector.memset(gw_zero[:], 0.0))
            dve.wait_ge(hi_done, 2)
            nc.vector.tensor_tensor(gw_x[:, :, E:2 * E], gw[:], f32(gw_x[:, :, 0:E]), ALU.subtract).then_inc(gw_ready, 1)
            for n in range(NT // 2):
                dve.wait_ge(first_read, n + 1)
                out = logit[:, 2 * n:2 * n + 2]
                nc.vector.tensor_tensor(out, ps[:, n % 4, :, E:2 * E], out, ALU.add).then_inc(freed, 1)
            nc.vector.memset(ahead[:], 0.0)
            nc.vector.memset(carry[:], 1.0)
            chain(nc.vector.memset(parts[:], 0.0))
            nc.vector.memset(carry[:, :, 0:1], 0.0)
            if A:
                nc.vector.memset(parts[:, :, E:, 0:1], 1.0)
            dve.wait_ge(scored, 1)
            chain(nc.vector.tensor_tensor(biased[:], score[:], bias[:].unsqueeze(1).broadcast_to([P, NT, E]), ALU.add))
            if group_best == 2:
                for t in range(NT):
                    for g in range(G):
                        last = nc.vector.max(best[:, t, g], biased[:, t, g * per:(g + 1) * per])
                chain(last)
                chain(nc.vector.tensor_tensor(gscore[:], best[:, :, :, 0], best[:, :, :, 1], ALU.add))
            else:
                chain(nc.vector.tensor_reduce(gscore[:], grouped(biased), AX_X, ALU.max))
            for j in range(G):
                other = gscore[:, :, j:j + 1]
                if j + 1 < G:
                    last = nc.vector.tensor_tensor(ahead[:, :, j + 1:, j], other.broadcast_to([P, NT, G - 1 - j]),
                                                   gscore[:, :, j + 1:], ALU.is_ge)
                if j:
                    last = nc.vector.tensor_tensor(ahead[:, :, 0:j, j], other.broadcast_to([P, NT, j]),
                                                   gscore[:, :, 0:j], ALU.is_gt)
            chain(last)
            chain(nc.vector.tensor_reduce(chosen_g[:], ahead[:], AX_X, ALU.add))
            chain(nc.vector.tensor_scalar(chosen_g[:], chosen_g[:], 2.0, None, ALU.is_lt))
            chain(nc.vector.tensor_scalar(penalty[:], chosen_g[:], 1.0, -LOWEST, ALU.subtract, ALU.mult))
            chain(nc.vector.tensor_tensor(grouped(biased), grouped(biased), over_experts(chosen_g[:]), ALU.mult))
            chain(nc.vector.tensor_tensor(grouped(biased), grouped(biased), over_experts(penalty[:]), ALU.add))
            for t in range(NT):
                last = nc.vector.max(top[:, t], biased[:, t])
            chain(last)
            least = top[:, :, top_k - 1:top_k].broadcast_to([P, NT, E])
            nc.vector.tensor_tensor(above[:], biased[:], least, ALU.is_gt)
            chain(nc.vector.tensor_tensor(equal[:], biased[:], least, ALU.is_equal))
            nc.vector.tensor_reduce(room[:], above[:], AX_X, ALU.add)
            chain(nc.vector.tensor_tensor_scan(order[:].rearrange("p t e -> p (t e)"), carry[:].rearrange("p t e -> p (t e)"),
                                               equal[:].rearrange("p t e -> p (t e)"), 0.0, ALU.mult, ALU.add))
            chain(nc.vector.tensor_scalar(room[:], room[:], -1.0, float(top_k), ALU.mult, ALU.add))
            chain(nc.vector.tensor_tensor(order[:], order[:], room[:].unsqueeze(2).broadcast_to([P, NT, E]), ALU.is_le))
            chain(nc.vector.tensor_tensor(equal[:], equal[:], order[:], ALU.mult))
            chain(nc.vector.tensor_tensor(above[:], above[:], equal[:], ALU.add))
            chain(nc.vector.tensor_tensor(weight[:], above[:], score[:], ALU.mult))
            chain(nc.vector.tensor_reduce(total[:], weight[:], AX_X, ALU.add))
            chain(nc.vector.reciprocal(room[:], total[:]))
            chain(nc.vector.scalar_tensor_tensor(weight[:], weight[:], route_scale,
                                                 room[:].unsqueeze(2).broadcast_to([P, NT, E]), ALU.mult, ALU.mult))
            chain(nc.vector.tensor_copy(parts[:, :, 0:E, 0], weight[:]))
            nc.vector.tensor_tensor(parts[:, :, 0:E, 1], weight[:], parts[:, :, 0:E, 0], ALU.subtract).then_inc(parts_ready, 1)



THREE = ((0, 0), (0, 1), (1, 0))


def pipeline(eng, rounds, units, stages):
    deepest = max(lead for lead, _ in stages)

    def run(i, u, last):
        for lead, step in stages:
            v = u + lead
            if 0 <= v < units:
                step(i, v)
            elif v >= units and not last:
                step(i + 1, v - units)

    for u in range(-deepest, 0):
        run(0, u, False)
    if rounds > 1:
        with eng.Fori(0, rounds - 1) as i:
            for u in range(units):
                run(i, u, False)
    for u in range(units):
        run(rounds - 1, u, True)

E0, GROUP0 = 32, 4
SHARED0 = 4


class Ffn0Weights:

    def __init__(self, nc, ctx):
        m = Memory(nc, ctx, "w0")
        self.gate_w, self.bias = m.sb("gate_w", [P, KC, E0]), m.sb("bias", [P, E0])
        fc1_cols, width = KC * P, KC * P + KC * SHARED0 * P
        self.w32, self.w_hi, self.w_lo = m.sb("w32", [P, width]), m.sb("w_hi", [P, width], F32R), m.sb("w_lo", [P, width], F32R)
        self.fc1 = [w[:, 0:fc1_cols].rearrange("p (k n) -> p k n", k=KC) for w in (self.w_hi, self.w_lo)]
        self.up = [w[:, fc1_cols:].rearrange("p (k n) -> p k n", k=KC) for w in (self.w_hi, self.w_lo)]
        self.out32 = m.sb("out32", [P, 1 + SHARED0, D])
        self.out_w = [m.sb("out_hi", [P, 1 + SHARED0, D], F32R), m.sb("out_lo", [P, 1 + SHARED0, D], F32R)]
        self.stage = m.sb("stage", [P, 2, GROUP0, 2, P])
        self.experts = [m.sb("we_hi", [P, 2, GROUP0, 2, P], F32R), m.sb("we_lo", [P, 2, GROUP0, 2, P], F32R)]

    def beside_norm(self, a):
        return Beside([(self.gate_w[:], a["gate_w0"]), (self.bias[:], a["gate_bias0"]), (self.w32[:], a["f0_in"])],
                      splits=[(self.w_hi[:], self.w_lo[:], self.w32[:])])

    def beside_routing(self, a, gate_row):
        first = self.stage[:, 0].rearrange("p e c n -> p (e c n)")
        hi, lo = [w[:, 0].rearrange("p e c n -> p (e c n)") for w in self.experts]
        return Beside([(self.out32[:].rearrange("p c n -> p (c n)"), a["f0_out"]), (first, a["f0_experts"][0])],
                      gated=[(self.out32[:], self.out32[:], gate_row.unsqueeze(1).broadcast_to([P, 1 + SHARED0, D]))],
                      splits=[(hi, lo, first), (self.out_w[0][:], self.out_w[1][:], self.out32[:])])


def ffn0_phase(nc, w, w_exp_dram, cw_dram, x, h_hi, h_lo, stats):
    with ExitStack() as outer:
        y_acc = Memory(nc, outer, "f0").sb("y_acc", [P, T])
        experts0_block(nc, w.fc1, w.stage, w.experts, w_exp_dram, cw_dram, h_hi, h_lo, y_acc)
        output0_block(nc, w.out_w, w.up, y_acc, x, h_hi, h_lo, stats)


def experts0_block(nc, fc1, stage, we, w_exp_dram, cw_dram, h_hi, h_lo, y_acc):
    ROUNDS = E0 // GROUP0 // 2
    UNITS_ROUND = 2 * NB * GROUP0
    GROUP_UNITS = NB * GROUP0
    RR, TR = 4, 4
    HB, CB, YB = 4, 2, 2
    round_units = [(half, b, e) for half in range(2) for b in range(NB) for e in range(GROUP0)]
    with ExitStack() as ctx:
        m = Memory(nc, ctx, "f0e")
        lat = [m.sb("lat_hi", [P, T], F32R), m.sb("lat_lo", [P, T], F32R)]
        crow = m.sb("crow", [2 * GROUP0, 2, T], F16)
        pick = m.sb("pick", [2 * GROUP0, GROUP0, P], F16)
        relu = m.sb("relu", [P, RR, QB])
        scaled = m.sb("scaled", [P, RR, QB])
        prod = m.sb("prod", [P, RR, QB])
        split = [m.sb("t_hi", [P, TR, QB], F32R), m.sb("t_lo", [P, TR, QB], F32R)]
        ps_h, ps_c, ps_y = m.ps("ps_h", [P, HB, QB]), m.ps("ps_c", [P, CB, QB]), m.ps("ps_y", [P, YB, QB])
        lat_filled, lat_hi_ready, lat_ready = m.sem("lat_filled"), m.sem("lat_hi_ready"), m.sem("lat_ready")
        zeroed, picked = m.sem("zeroed"), m.sem("picked")
        e_loaded, c_loaded = [[m.sem(f"{what}_loaded{half}") for half in range(2)] for what in "ec"]
        e_hi, e_ready = m.sem("e_hi"), m.sem("e_ready")
        h_filled, c_filled, relu_ready = m.sem("h_filled"), m.sem("c_filled"), m.sem("relu_ready")
        scaled_ready, prod_ready, t_hi_ready, t_ready = m.sem("scaled_ready"), m.sem("prod_ready"), m.sem("t_hi_ready"), m.sem("t_ready")
        second_done, y_free = m.sem("second_done"), m.sem("y_free")
        block = ctx.enter_context(nc.Block())

        @block.sync
        def _(sp):
            def load(group, half):
                sp.dma_start(crow[:, half], cw_dram[group]).then_inc(c_loaded[half], 16)
                sp.dma_start(stage[:, half].rearrange("p e c n -> p (e c n)"), w_exp_dram[group]).then_inc(e_loaded[half], 16)

            sp.dma_start(crow[:, 0], cw_dram[0]).then_inc(c_loaded[0], 16)
            load(1, 1)
            with sp.Fori(0, ROUNDS - 1) as i:
                for half in range(2):
                    sp.wait_ge(c_filled, (2 * i + half + 1) * GROUP_UNITS)
                    load(2 * i + half + 2, half)
            for half in range(2):
                sp.wait_ge(e_loaded[half], 16 * (ROUNDS - 1 + half))
                sp.wait_ge(c_loaded[half], 16 * ROUNDS)

        @block.gpsimd
        def _(pool):
            pool.sem_inc(prod_ready, RR)
            nc.gpsimd.memset(pick[:], 1.0).then_inc(zeroed, 1)
            pool.wait_ge(zeroed, 1)
            for e in range(GROUP0):
                nc.gpsimd.affine_select(out=pick[:, e], in_=pick[:, e], compare_op=ALU.is_ge, fill=0.0, base=-2 * e,
                                        pattern=[[0, P]], channel_multiplier=1).then_inc(zeroed, 1)
            pool.wait_ge(zeroed, 1 + GROUP0)
            for e in range(GROUP0):
                nc.gpsimd.affine_select(out=pick[:, e], in_=pick[:, e], compare_op=ALU.is_ge, fill=0.0, base=2 * e + 1,
                                        pattern=[[0, P]], channel_multiplier=-1).then_inc(picked, 1)

            def square(i, u):
                n = i * UNITS_ROUND + u
                pool.wait_ge(t_ready, n + 1)
                pool.wait_ge(scaled_ready, n + 1 + CB)
                nc.gpsimd.tensor_tensor(prod[:, u % RR], scaled[:, u % RR], relu[:, u % RR], ALU.mult).then_inc(prod_ready, 1)

            pipeline(pool, ROUNDS, UNITS_ROUND, [(0, square)])

        @block.tensor
        def _(pe):
            pe.sem_inc(second_done, TR)
            for b in range(NB):
                tok = slice(b * QB, (b + 1) * QB)
                for k in range(KC):
                    for wi, hi in THREE:
                        last = nc.tensor.matmul(ps_h[:, b], fc1[wi][:, k], (h_hi, h_lo)[hi][:, k, tok],
                                                start=(k == 0 and (wi, hi) == (0, 0)), stop=(k == KC - 1 and (wi, hi) == (1, 0)))
                last.then_inc(lat_filled, 1)
            pe.wait_ge(lat_ready, NB)
            pe.wait_ge(picked, GROUP0)

            def first(i, u):
                half, b, e = round_units[u]
                n = i * UNITS_ROUND + u
                if (b, e) == (0, 0):
                    pe.wait_ge(e_ready, 2 * i + half + 1)
                tok = slice(b * QB, (b + 1) * QB)
                pe.wait_ge(relu_ready, n + 1)
                for wi, li in THREE:
                    last = nc.tensor.matmul(ps_h[:, u % HB], we[wi][:, half, e, 0], lat[li][:, tok],
                                            start=(wi, li) == (0, 0), stop=(wi, li) == (1, 0))
                last.then_inc(h_filled, 1)
                if (b, e) == (0, 0):
                    pe.wait_ge(c_loaded[half], 16 * (i + 1))
                pe.wait_ge(scaled_ready, n + 1)
                nc.tensor.matmul(ps_c[:, u % CB], pick[:, e], crow[:, half, tok], start=True, stop=True).then_inc(c_filled, 1)

            def second(i, u):
                half, b, e = round_units[u]
                n = i * UNITS_ROUND + u
                if e == 0:
                    pe.wait_ge(y_free, i * (UNITS_ROUND // GROUP0) + u // GROUP0 + 1)
                pe.wait_ge(t_ready, n + 1 + RR)
                for wi, ti in THREE:
                    last = nc.tensor.matmul(ps_y[:, b % YB], we[wi][:, half, e, 1], split[ti][:, u % TR],
                                            start=(e == 0 and (wi, ti) == (0, 0)), stop=(e == GROUP0 - 1 and (wi, ti) == (1, 0)))
                last.then_inc(second_done, 1)

            pipeline(pe, ROUNDS, UNITS_ROUND, [(4, first), (0, second)])

        @block.scalar
        def _(act):
            act.sem_inc(relu_ready, HB)
            for b in range(NB):
                act.wait_ge(lat_filled, b + 1)
                nc.scalar.activation(lat[0][:, b * QB:(b + 1) * QB], ps_h[:, b], ACT.Copy).then_inc(lat_hi_ready, 1)

            def split_weights(group, half, i):
                act.wait_ge(e_loaded[half], 16 * (i + half))
                if half or not isinstance(group, int):
                    act.wait_ge(second_done, (group - 1) * GROUP_UNITS + TR)
                nc.scalar.activation(we[0][:, half], stage[:, half], ACT.Copy).then_inc(e_hi, 1)

            def weights(i, u):
                if u % GROUP_UNITS == 6 and not (u > GROUP_UNITS and isinstance(i, int) and i == ROUNDS - 1):
                    g = u // GROUP_UNITS
                    split_weights(2 * i + g + 1, 1 - g, i + g)

            def rectify(i, u):
                n = i * UNITS_ROUND + u
                act.wait_ge(h_filled, n + 1)
                act.wait_ge(prod_ready, n + 1)
                nc.scalar.activation(relu[:, u % RR], ps_h[:, u % HB], ACT.Relu).then_inc(relu_ready, 1)

            def leading(i, u):
                n = i * UNITS_ROUND + u
                act.wait_ge(prod_ready, n + 1 + RR)
                act.wait_ge(second_done, n + 1)
                nc.scalar.activation(split[0][:, u % TR], prod[:, u % RR], ACT.Copy).then_inc(t_hi_ready, 1)

            pipeline(act, ROUNDS, UNITS_ROUND, [(3, rectify), (1, leading), (0, weights)])

        @block.vector
        def _(dve):
            dve.sem_inc(e_ready, 1)
            dve.sem_inc(scaled_ready, CB)
            dve.sem_inc(t_ready, RR)
            dve.sem_inc(y_free, YB)
            nc.vector.memset(y_acc[:], 0.0)
            for b in range(NB):
                dve.wait_ge(lat_hi_ready, b + 1)
                tok = slice(b * QB, (b + 1) * QB)
                nc.vector.tensor_tensor(lat[1][:, tok], ps_h[:, b], f32(lat[0][:, tok]), ALU.subtract).then_inc(lat_ready, 1)

            def split_weights(group, half, i):
                dve.wait_ge(e_hi, group)
                nc.vector.tensor_tensor(we[1][:, half], stage[:, half], f32(we[0][:, half]), ALU.subtract).then_inc(e_ready, 1)

            def weights(i, u):
                if u % GROUP_UNITS == 6 and not (u > GROUP_UNITS and isinstance(i, int) and i == ROUNDS - 1):
                    g = u // GROUP_UNITS
                    split_weights(2 * i + g + 1, 1 - g, i + g)

            def scale(i, u):
                n = i * UNITS_ROUND + u
                dve.wait_ge(c_filled, n + 1)
                dve.wait_ge(relu_ready, n + 1 + HB)
                dve.wait_ge(prod_ready, n + 1)
                nc.vector.tensor_tensor(scaled[:, u % RR], ps_c[:, u % CB], relu[:, u % RR], ALU.mult).then_inc(scaled_ready, 1)

            def rest(i, u):
                n = i * UNITS_ROUND + u
                dve.wait_ge(t_hi_ready, n + 1)
                nc.vector.tensor_tensor(split[1][:, u % TR], prod[:, u % RR], f32(split[0][:, u % TR]), ALU.subtract).then_inc(t_ready, 1)

            def collect(i, u):
                half, b, e = round_units[u]
                if e == GROUP0 - 1:
                    dve.wait_ge(second_done, i * UNITS_ROUND + u + 1 + TR)
                    tok = slice(b * QB, (b + 1) * QB)
                    nc.vector.tensor_tensor(y_acc[:, tok], y_acc[:, tok], ps_y[:, b % YB], ALU.add).then_inc(y_free, 1)

            pipeline(dve, ROUNDS, UNITS_ROUND, [(3, scale), (1, rest), (0, collect), (0, weights)])


def output0_block(nc, out_w, up, y_acc, x, h_hi, h_lo, stats):
    with ExitStack() as ctx:
        m = Memory(nc, ctx, "f0o")
        y = [m.sb("y_hi", [P, T], F32R), m.sb("y_lo", [P, T], F32R)]
        relu = m.sb("relu", [P, 4, QB])
        prod = m.sb("prod", [P, 4, QB])
        inner = [m.sb("inner_hi", [P, 2, SHARED0, QB], F32R), m.sb("inner_lo", [P, 2, SHARED0, QB], F32R)]
        UB, OB = 4, 4
        ps_u, ps_o = m.ps("ps_u", [P, UB, QB]), m.ps("ps_o", [P, OB, 2, D])
        y_hi_ready, y_ready = m.sem("y_hi_ready"), m.sem("y_ready")
        u_filled, relu_ready, prod_ready = m.sem("u_filled"), m.sem("relu_ready"), m.sem("prod_ready")
        in_hi_ready, in_ready, o_filled, o_free = m.sem("in_hi_ready"), m.sem("in_ready"), m.sem("o_filled"), m.sem("o_free")
        block = ctx.enter_context(nc.Block())
        units = [(b, c) for b in range(NB) for c in range(SHARED0)]

        @block.tensor
        def _(pe):
            def up_block(b):
                for c in range(SHARED0):
                    n = b * SHARED0 + c
                    if n >= UB:
                        pe.wait_ge(relu_ready, n - UB + 1)
                    for k in range(KC):
                        for wi, hi in THREE:
                            last = nc.tensor.matmul(ps_u[:, n % UB], up[wi][:, k, c * P:(c + 1) * P],
                                                    (h_hi, h_lo)[hi][:, k, b * QB:(b + 1) * QB],
                                                    start=(k == 0 and (wi, hi) == (0, 0)), stop=(k == KC - 1 and (wi, hi) == (1, 0)))
                    last.then_inc(u_filled, 1)

            def out_block(b):
                for pair in range(TPB // 2):
                    n = b * (TPB // 2) + pair
                    if n >= OB:
                        pe.wait_ge(o_free, n - OB + 1)
                    for j in range(2):
                        t = 2 * pair + j
                        for c in range(SHARED0 + 1):
                            for ai, wi in THREE:
                                a = y[ai][:, (b * TPB + t) * P:(b * TPB + t + 1) * P] if c == 0 else inner[ai][:, b % 2, c - 1, t * P:(t + 1) * P]
                                last = nc.tensor.matmul(ps_o[:, n % OB, j], a, out_w[wi][:, c],
                                                        start=(c == 0 and (ai, wi) == (0, 0)), stop=(c == SHARED0 and (ai, wi) == (1, 0)))
                    last.then_inc(o_filled, 1)

            up_block(0)
            for b in range(NB):
                if b + 1 < NB:
                    up_block(b + 1)
                pe.wait_ge(in_ready, (b + 1) * SHARED0)
                pe.wait_ge(y_ready, b + 1)
                out_block(b)

        @block.gpsimd
        def _(pool):
            for n in range(len(units)):
                pool.wait_ge(relu_ready, n + 1)
                if n >= 4:
                    pool.wait_ge(in_ready, n - 3)
                nc.gpsimd.tensor_tensor(prod[:, n % 4], relu[:, n % 4], relu[:, n % 4], ALU.mult).then_inc(prod_ready, 1)

        @block.scalar
        def _(act):
            for b in range(NB):
                nc.scalar.activation(y[0][:, b * QB:(b + 1) * QB], y_acc[:, b * QB:(b + 1) * QB], ACT.Copy).then_inc(y_hi_ready, 1)

            def leading(n):
                b, c = units[n]
                act.wait_ge(prod_ready, n + 1)
                if b >= 2:
                    act.wait_ge(o_filled, (b - 1) * (TPB // 2))
                nc.scalar.activation(inner[0][:, b % 2, c], prod[:, n % 4], ACT.Copy).then_inc(in_hi_ready, 1)

            for n in range(len(units)):
                act.wait_ge(u_filled, n + 1)
                if n >= 4:
                    act.wait_ge(prod_ready, n - 3)
                nc.scalar.activation(relu[:, n % 4], ps_u[:, n % UB], ACT.Relu).then_inc(relu_ready, 1)
                if n >= 2:
                    leading(n - 2)
            leading(len(units) - 2)
            leading(len(units) - 1)

        @block.vector
        def _(dve):
            for b in range(NB):
                dve.wait_ge(y_hi_ready, b + 1)
                tok = slice(b * QB, (b + 1) * QB)
                nc.vector.tensor_tensor(y[1][:, tok], y_acc[:, tok], f32(y[0][:, tok]), ALU.subtract).then_inc(y_ready, 1)

            def collect(b):
                for pair in range(TPB // 2):
                    n = b * (TPB // 2) + pair
                    dve.wait_ge(o_filled, n + 1)
                    xs = x[:, 2 * n:2 * n + 2]
                    nc.vector.tensor_tensor(xs, xs, ps_o[:, n % OB], ALU.add).then_inc(o_free, 1)
                dve.wait_ge(o_free, (b + 1) * (TPB // 2))
                for t in range(b * TPB, (b + 1) * TPB):
                    nc.vector.bn_stats(stats[:, t], x[:, t])

            for n, (b, c) in enumerate(units):
                dve.wait_ge(in_hi_ready, n + 1)
                nc.vector.tensor_tensor(inner[1][:, b % 2, c], prod[:, n % 4], f32(inner[0][:, b % 2, c]), ALU.subtract).then_inc(in_ready, 1)
                if c == SHARED0 - 1 and b >= 1:
                    collect(b - 1)
            collect(NB - 1)



HEADS1 = 16
DH1 = D // HEADS1
STACK = 4 * DH1
VW = 2 * DH1 + 1
WIDE = 2 * QB
WIDE_MAXES = [(qt, w) for qt in range(NT) for w in range(qt * P // WIDE + 1)]


def project1_block(nc, w, qk_dram, v_all, h_hi, h_lo):
    with ExitStack() as ctx:
        m = Memory(nc, ctx, "p1")
        parts = [m.sb("hi", [P, 2, 2, T], F16), m.sb("lo", [P, 2, 2, T], F16)]
        ps = m.ps("ps", [P, 8, QB])
        filled, hi_ready, freed, stored, ones_ready = m.sem("filled"), m.sem("hi_ready"), m.sem("freed"), m.sem("stored"), m.sem("ones_ready")
        block = ctx.enter_context(nc.Block())
        qk = [(c, which, b) for c in range(KC) for which in range(2) for b in range(NB)]
        vs = list(range(NT // 2))

        @block.sync
        def _(sp):
            for n, (c, which) in enumerate((c, which) for c in range(KC) for which in range(2)):
                sp.wait_ge(freed, (n + 1) * NB)
                for a in range(2):
                    sp.dma_start(qk_dram[which, a, c * P:(c + 1) * P], parts[a][:, which, c]).then_inc(stored, 16)
            sp.wait_ge(stored, 16 * 8)

        @block.gpsimd
        def _(pool):
            nc.gpsimd.memset(v_all[:, :, :, VW - 1:VW], 1.0).then_inc(ones_ready, 1)

        @block.tensor
        def _(pe):
            for n, (c, which, b) in enumerate(qk):
                if n >= 8:
                    pe.wait_ge(freed, n - 7)
                for k in range(KC):
                    for wi, hi in THREE:
                        last = nc.tensor.matmul(ps[:, n % 8], w[wi][:, k, which, c * P:(c + 1) * P], (h_hi, h_lo)[hi][:, k, b * QB:(b + 1) * QB],
                                                start=(k == 0 and (wi, hi) == (0, 0)), stop=(k == KC - 1 and (wi, hi) == (1, 0)))
                last.then_inc(filled, 1)
            for pair in vs:
                n = len(qk) + pair
                pe.wait_ge(freed, n - 7)
                for j in range(2):
                    t = 2 * pair + j
                    for k in range(KC):
                        for hi, wi in THREE:
                            last = nc.tensor.matmul(ps[:, n % 8, j * D:(j + 1) * D], (h_hi, h_lo)[hi][:, k, t * P:(t + 1) * P], w[wi][:, k, 2],
                                                    start=(k == 0 and (wi, hi) == (0, 0)), stop=(k == KC - 1 and (hi, wi) == (1, 0)))
                last.then_inc(filled, 1)

        def v_part(pair, a):
            return v_all[:, :, 2 * pair:2 * pair + 2, a * DH1:(a + 1) * DH1].rearrange("p h t d -> p t h d")

        def v_sums(n):
            return ps[:, n % 8].rearrange("p (t h d) -> p t h d", t=2, d=DH1)

        @block.scalar
        def _(act):
            for n, (c, which, b) in enumerate(qk):
                act.wait_ge(filled, n + 1)
                nc.scalar.activation(parts[0][:, which, c, b * QB:(b + 1) * QB], ps[:, n % 8], ACT.Copy).then_inc(hi_ready, 1)
            for pair in vs:
                n = len(qk) + pair
                act.wait_ge(filled, n + 1)
                for j in range(2):
                    last = nc.scalar.activation(v_part(pair, 0)[:, j], v_sums(n)[:, j], ACT.Copy)
                last.then_inc(hi_ready, 1)

        @block.vector
        def _(dve):
            for n, (c, which, b) in enumerate(qk):
                dve.wait_ge(hi_ready, n + 1)
                tok = slice(b * QB, (b + 1) * QB)
                nc.vector.tensor_tensor(parts[1][:, which, c, tok], ps[:, n % 8], parts[0][:, which, c, tok], ALU.subtract).then_inc(freed, 1)
            for pair in vs:
                n = len(qk) + pair
                dve.wait_ge(hi_ready, n + 1)
                for j in range(2):
                    last = nc.vector.tensor_tensor(v_part(pair, 1)[:, j], v_sums(n)[:, j], v_part(pair, 0)[:, j], ALU.subtract)
                last.then_inc(freed, 1)


LO_LAG, PV_LAG = 0, 5
ROUND1 = 3
MAX_UNITS = 0, 35


def wide_keys(qt, w):
    return min(WIDE, (qt + 1) * P - w * WIDE)


def lo_owner(u):
    return int(u % 5 != 0) if MAX_UNITS[0] <= u < MAX_UNITS[1] else u % 2


def hi_by_vector(u):
    return lo_owner(u) == 0


def attention1_steps():
    def prep(h):
        return [("MAX", h, qt, w) for qt, w in WIDE_MAXES]

    def cost(item):
        return P + wide_keys(*item[2:])

    whole = sum(map(cost, prep(0)))
    start = [("LOADQK", 0), ("LOADQK", 1), ("LOADV", 0)] + prep(0) + [("COMBINE", 0), ("MROW", 0)]
    periods, late = [], []
    for h in range(HEADS1):
        steps = []
        more = h + 1 < HEADS1
        ahead = prep(h + 1) if more else []
        for u, (qb, kt) in enumerate(UNITS):
            steps.append(("S", h, u))
            if h + 2 < HEADS1 and u == 3:
                steps.append(("LOADQK", h + 2))
            if more and u == PV_LAG + 3:
                steps.append(("LOADV", h + 1))
            while ahead and sum(map(cost, ahead)) > whole * (MAX_UNITS[1] - 1 - u) / (MAX_UNITS[1] - MAX_UNITS[0]):
                steps.append(ahead.pop(0))
            if more and u == MAX_UNITS[1]:
                steps.append(("COMBINE", h + 1))
            if more and u == MAX_UNITS[1] + 1:
                steps.append(("MROW", h + 1))
            steps += [s for n, s in late if n == 0]
            late = [(n - 1, s) for n, s in late if n > 0]
            if hi_by_vector(u):
                late.append((LO_LAG, ("HIV", h, u)))
            late += [(LO_LAG, (("LOV", "LOG")[lo_owner(u)], h, u)), (PV_LAG, ("PV", h, u))]
            if kt == TPB * (qb + 1) - 1:
                late.append((PV_LAG, ("ZOUT", h, qb)))
        periods.append(steps)
    tail = [s for _, s in sorted(late, key=lambda x: x[0])]
    return start, periods, tail


def attention1_block(nc, qk_dram, v_all, context, ident, ident_bf, mask_q, mask_t):
    start, periods, tail = attention1_steps()
    streams = {"S": "S", "LOV": "LOV", "LOG": "LOG", "HIV": "HIV", "MAX": "AUX", "MROW": "AUX", "ZOUT": "Z", "COMBINE": "C"}
    place, _ = number_steps(start + sum(periods, []) + tail, streams)
    _, one_round = number_steps(sum(periods[1:1 + ROUND1], []), streams)
    looped = (HEADS1 - 2) // ROUND1 * ROUND1
    for a in range(1, ROUND1 + 1):
        for h in range(a, looped + 1, ROUND1):
            assert [(s[0], s[1] - h + a, *s[2:]) for s in periods[h]] == periods[a]
    scale = DH1 ** -0.5
    SB, AB, PR = 2, 2, 8
    qk_heads = qk_dram.rearrange("w a (h d) t -> w a h d t", d=DH1)
    context_heads = context[:].rearrange("p t (h d) -> p h t d", d=DH1)
    with ExitStack() as ctx:
        m = Memory(nc, ctx, "a1", reuse=True)
        q_stack, k_stack = m.sb("q_stack", [P, ROUND1, T], F16), m.sb("k_stack", [P, ROUND1, T], F16)
        zero_row = m.sb("zero_row", [1, T], F16)
        v_head = m.sb("v_head", [P, ROUND1, NT, VW], F16)
        partial = m.sb("partial", [P, NT, T // WIDE])
        neg_max = m.sb("neg_max", [P, NT])
        neg_max_t = m.sb("neg_max_t", [NT, P], F16)
        p32 = m.sb("p32", [P, PR, QB])
        p_hi, p_lo = m.sb("p_hi", [P, PR, QB], F16), m.sb("p_lo", [P, PR, QB], F16)
        z = m.sb("z", [P, TPB, DH1])
        rden = m.sb("rden", [P, TPB])
        ps_s = m.ps("ps_s", [P, SB, QB])
        ps_z = m.ps("ps_z", [P, 2, TPB, P])
        ps_m = m.ps("ps_m", [P, AB, WIDE])
        const_ready = m.sem("const_ready")
        row_loaded = m.sem("row_loaded")
        loaded, v_loaded = [[m.sem(f"{what}_loaded{s}") for s in range(ROUND1)] for what in ("qk", "v")]
        s_filled, s_exped, pv_done = m.sem("s_filled"), m.sem("s_exped"), m.sem("pv_done")
        lo_ready = [m.sem("lo_ready_vector"), m.sem("lo_ready_gpsimd")]
        max_filled, max_read, max_ready = m.sem("max_filled"), m.sem("max_read"), m.sem("max_ready")
        hi_ready, z_read, z_out = m.sem("hi_ready"), m.sem("z_read"), m.sem("z_out")
        block = ctx.enter_context(nc.Block())
        PER_LOAD = 16 * 5

        def whole_program(eng, step):
            def in_line(n, stream):
                return n

            for s in start + periods[0]:
                step(s, in_line, 0)
            with eng.Fori(0, looped // ROUND1) as i:
                for s in sum(periods[1:1 + ROUND1], []):
                    step(s, lambda n, stream: n + i * one_round[stream], i)
            for s in sum(periods[looped + 1:], []) + tail:
                step(s, in_line, 0)

        def rest(eng, unit, s, at):
            h, u = s[1:]
            c = first_col(*UNITS[u])
            eng.wait_ge(s_exped, at(place["S", h, u], "S") + 1 + SB)
            unit.tensor_tensor(p_lo[:, u % PR, c:QB], p32[:, u % PR, c:QB], p_hi[:, u % PR, c:QB],
                               ALU.subtract).then_inc(lo_ready[lo_owner(u)], 1)

        @block.sync
        def _(sp):
            sp.wait_ge(const_ready, 5)

            def step(s, at, i):
                kind, h = s[0], s[1]
                if kind == "LOADQK":
                    slot = h % ROUND1
                    if h >= ROUND1:
                        sp.wait_ge(s_filled, at(place["S", h - ROUND1, len(UNITS) - 1], "S") + 1)
                    head = ROUND1 * i + h
                    for j in range(2):
                        rows = slice(2 * j * DH1, 2 * (j + 1) * DH1)
                        sp.dma_start(q_stack[rows, slot], qk_heads[0, j, head].unsqueeze(0).broadcast_to([2, DH1, T])).then_inc(loaded[slot], 16)
                        sp.dma_start(k_stack[rows, slot], qk_heads[1, :, head]).then_inc(loaded[slot], 16)
                    sp.dma_start(q_stack[STACK:STACK + 1, slot], zero_row[:]).then_inc(loaded[slot], 16)
                elif kind == "LOADV":
                    slot = h % ROUND1
                    if h >= 2:
                        sp.wait_ge(pv_done, at(place["S", h - 2, 0], "S") + 1 + PR)
                    sp.dma_start(v_head[:, slot], v_all[:, ROUND1 * i + h]).then_inc(v_loaded[slot], 16)
                elif kind == "MROW":
                    sp.wait_ge(max_read, at(place[s], "AUX") + 1 + AB)
                    sp.dma_start(q_stack[STACK:STACK + 1, h % ROUND1].rearrange("a (t p) -> a t p", p=P), neg_max_t[:]).then_inc(row_loaded, 16)

            whole_program(sp, step)

        @block.gpsimd
        def _(pool):
            consts = [(q_stack[STACK:], 0.0), (zero_row[:], 0.0), (partial[:], LOWEST), (k_stack[STACK:], 0.0), (k_stack[STACK:STACK + 1], 1.0)]
            for n, (out, value) in enumerate(consts):
                if n:
                    pool.wait_ge(const_ready, n)
                nc.gpsimd.memset(out, value).then_inc(const_ready, 1)

            def step(s, at, i):
                if s[0] == "LOG":
                    rest(pool, nc.gpsimd, s, at)

            whole_program(pool, step)

        @block.tensor
        def _(pe):
            pe.wait_ge(const_ready, 5)
            pe.sem_inc(pv_done, PR)

            def step(s, at, i):
                kind, h = s[0], s[1]
                slot = h % ROUND1
                if kind == "MAX":
                    qt, w = s[2:]
                    n = place[s]
                    if (qt, w) == (0, 0):
                        pe.wait_ge(loaded[slot], PER_LOAD * (i + h // ROUND1 + 1))
                    pe.wait_ge(max_read, at(n, "AUX") + 1)
                    end = wide_keys(qt, w)
                    for c in range(0, end, QB):
                        to = min(c + QB, end)
                        diagonal = w * WIDE + to == (qt + 1) * P
                        last = nc.tensor.matmul(ps_m[:, n % AB, c:to], q_stack[:, slot, qt * P:(qt + 1) * P],
                                                k_stack[:, slot, w * WIDE + c:w * WIDE + to], start=True, stop=not diagonal)
                        if diagonal:
                            last = nc.tensor.matmul(ps_m[:, n % AB, to - P:to], ident_bf[:], mask_q[:], start=False, stop=True)
                    last.then_inc(max_filled, 1)
                elif kind == "MROW":
                    n = place[s]
                    pe.wait_ge(max_read, at(n, "AUX") + 1)
                    pe.wait_ge(max_ready, at(place["COMBINE", h], "C") + 1)
                    nc.tensor.transpose(ps_m[0:NT, n % AB, 0:P], neg_max[:], ident[:]).then_inc(max_filled, 1)
                elif kind == "S":
                    u = s[2]
                    qb, kt = UNITS[u]
                    if u == 0:
                        pe.wait_ge(row_loaded, 16 * (at(place["COMBINE", h], "C") + 1))
                    pe.wait_ge(s_exped, at(place[s], "S") + 1)
                    c = first_col(qb, kt)
                    diagonal = kt >= TPB * qb
                    last = nc.tensor.matmul(ps_s[:, u % SB, c:QB], k_stack[:, slot, kt * P:(kt + 1) * P],
                                            q_stack[:, slot, qb * QB + c:(qb + 1) * QB], start=True, stop=not diagonal)
                    if diagonal:
                        last = nc.tensor.matmul(ps_s[:, u % SB, c:c + P], ident_bf[:], mask_t[:], start=False, stop=True)
                    last.then_inc(s_filled, 1)
                elif kind == "PV":
                    u = s[2]
                    qb, kt = UNITS[u]
                    if kt == 0:
                        pe.wait_ge(z_read, at(place["ZOUT", h, qb], "Z") + 1)
                    if u == 0:
                        pe.wait_ge(v_loaded[slot], 16 * (i + h // ROUND1 + 1))
                    owner = lo_owner(u)
                    stream = ("LOV", "LOG")[owner]
                    pe.wait_ge(lo_ready[owner], at(place[stream, h, u], stream) + 1)
                    for t in range(first_col(qb, kt) // P, TPB):
                        end = t == TPB - 1 and kt == TPB * (qb + 1) - 1
                        for part in (p_hi, p_lo):
                            last = nc.tensor.matmul(ps_z[:, qb % 2, t, 0:VW], part[:, u % PR, t * P:(t + 1) * P], v_head[:, slot, kt],
                                                    start=(kt == 0 and t == 0 and part is p_hi), stop=(end and part is p_lo))
                    last.then_inc(pv_done, 1)

            whole_program(pe, step)

        @block.scalar
        def _(act):
            act.sem_inc(s_exped, SB)

            def step(s, at, i):
                kind, h = s[0], s[1]
                if kind == "S":
                    u = s[2]
                    c = first_col(*UNITS[u])
                    n = at(place[s], "S")
                    act.wait_ge(s_filled, n + 1)
                    act.wait_ge(pv_done, n + 1)
                    last = nc.scalar.activation(p32[:, u % PR, c:QB], ps_s[:, u % SB, c:QB], ACT.Exp, scale=scale)
                    if not hi_by_vector(u):
                        last = nc.scalar.activation(p_hi[:, u % PR, c:QB], ps_s[:, u % SB, c:QB], ACT.Exp, scale=scale)
                    last.then_inc(s_exped, 1)

            whole_program(act, step)

        @block.vector
        def _(dve):
            dve.sem_inc(max_read, AB)
            dve.sem_inc(z_read, 2)
            dve.wait_ge(const_ready, 5)

            def step(s, at, i):
                kind, h = s[0], s[1]
                if kind == "MAX":
                    qt, w = s[2:]
                    n = place[s]
                    if (qt, w) == (0, 0) and h > 0:
                        dve.wait_ge(max_ready, at(place["COMBINE", h], "C"))
                    dve.wait_ge(max_filled, at(n, "AUX") + 1)
                    end = wide_keys(qt, w)
                    nc.vector.tensor_reduce(partial[:, qt, w:w + 1], ps_m[:, n % AB, 0:end], AX_X, ALU.max).then_inc(max_read, 1)
                elif kind == "COMBINE":
                    dve.wait_ge(max_read, at(place["MAX", h, NT - 1, T // WIDE - 1], "AUX") + 1 + AB)
                    if h > 0:
                        dve.wait_ge(max_read, at(place["MROW", h - 1], "AUX") + 1 + AB)
                    nc.vector.tensor_reduce(neg_max[:], partial[:], AX_X, ALU.max, negate=True).then_inc(max_ready, 1)
                elif kind == "MROW":
                    n = place[s]
                    dve.wait_ge(max_filled, at(n, "AUX") + 1)
                    if h > 0:
                        dve.wait_ge(row_loaded, 16 * at(place["COMBINE", h], "C"))
                    nc.vector.tensor_copy(neg_max_t[:], ps_m[0:NT, n % AB, 0:P]).then_inc(max_read, 1)
                elif kind == "HIV":
                    u = s[2]
                    c = first_col(*UNITS[u])
                    dve.wait_ge(s_exped, at(place["S", h, u], "S") + 1 + SB)
                    nc.vector.tensor_copy(p_hi[:, u % PR, c:QB], p32[:, u % PR, c:QB]).then_inc(hi_ready, 1)
                elif kind == "LOV":
                    if hi_by_vector(s[2]):
                        dve.wait_ge(hi_ready, at(place["HIV", h, s[2]], "HIV") + 1)
                    rest(dve, nc.vector, s, at)
                elif kind == "ZOUT":
                    qb = s[2]
                    n = at(place[s], "Z")
                    dve.wait_ge(pv_done, at(place["S", h, UNITS.index((qb, TPB * (qb + 1) - 1))], "S") + 1 + PR)
                    if (h, qb) != (0, 0):
                        dve.wait_ge(z_out, n)
                    nc.vector.reciprocal(rden[:], ps_z[:, qb % 2, :, VW - 1])
                    nc.vector.tensor_reduce(z[:], ps_z[:, qb % 2, :, 0:2 * DH1].rearrange("p t (a d) -> p t d a", a=2), AX_X,
                                            ALU.add).then_inc(z_read, 1)
                    dve.wait_ge(z_read, n + 3)
                    nc.vector.tensor_tensor(context_heads[:, ROUND1 * i + h, qb * TPB:(qb + 1) * TPB], z[:],
                                            rden[:].unsqueeze(2).broadcast_to([P, TPB, DH1]), ALU.mult).then_inc(z_out, 1)

            whole_program(dve, step)


def output1_block(nc, w, bias_gated, context, x, ident, h_hi, h_lo, stats):
    with ExitStack() as ctx:
        m = Memory(nc, ctx, "o1")
        ps_t, ps_o = m.ps("ps_t", [P, 4, QB]), m.ps("ps_o", [P, 4, 2, D])
        biased = m.sem("biased")
        turned, hi_ready, lo_ready, filled, added = m.sem("turned"), m.sem("hi_ready"), m.sem("lo_ready"), m.sem("filled"), m.sem("added")
        block = ctx.enter_context(nc.Block())
        units = [(b, k) for b in range(NB) for k in range(KC)]

        @block.gpsimd
        def _(pool):
            for b in range(NB):
                xs = x[:, b * TPB:(b + 1) * TPB]
                nc.gpsimd.tensor_tensor(xs, xs, bias_gated[:].unsqueeze(1).broadcast_to([P, TPB, D]), ALU.add).then_inc(biased, 1)

        @block.tensor
        def _(pe):
            for n, (b, k) in enumerate(units):
                if n >= 4:
                    pe.wait_ge(lo_ready, n - 3)
                for j in range(TPB):
                    last = nc.tensor.transpose(ps_t[:, n % 4, j * P:(j + 1) * P], context[:, b * TPB + j, k * P:(k + 1) * P], ident[:])
                last.then_inc(turned, 1)
            for n in range(NT // 2):
                pe.wait_ge(lo_ready, KC * (n // 2 + 1))
                if n >= 4:
                    pe.wait_ge(added, n - 3)
                for j in range(2):
                    tok = slice((2 * n + j) * P, (2 * n + j + 1) * P)
                    for k in range(KC):
                        for hi, wi in THREE:
                            last = nc.tensor.matmul(ps_o[:, n % 4, j], (h_hi, h_lo)[hi][:, k, tok], w[wi][:, k],
                                                    start=(k == 0 and (hi, wi) == (0, 0)), stop=(k == KC - 1 and (hi, wi) == (1, 0)))
                last.then_inc(filled, 1)

        @block.scalar
        def _(act):
            for n, (b, k) in enumerate(units):
                act.wait_ge(turned, n + 1)
                nc.scalar.activation(h_hi[:, k, b * QB:(b + 1) * QB], ps_t[:, n % 4], ACT.Copy).then_inc(hi_ready, 1)

        @block.vector
        def _(dve):
            for n, (b, k) in enumerate(units):
                dve.wait_ge(hi_ready, n + 1)
                tok = slice(b * QB, (b + 1) * QB)
                nc.vector.tensor_tensor(h_lo[:, k, tok], ps_t[:, n % 4], f32(h_hi[:, k, tok]), ALU.subtract).then_inc(lo_ready, 1)

            def statistics(n):
                dve.wait_ge(added, n + 1)
                for t in (2 * n, 2 * n + 1):
                    nc.vector.bn_stats(stats[:, t], x[:, t])

            for n in range(NT // 2):
                dve.wait_ge(biased, n // 2 + 1)
                dve.wait_ge(filled, n + 1)
                xs = x[:, 2 * n:2 * n + 2]
                nc.vector.tensor_tensor(xs, xs, ps_o[:, n % 4], ALU.add).then_inc(added, 1)
                if n:
                    statistics(n - 1)
            statistics(NT // 2 - 1)


class Attention1Weights:

    def __init__(self, nc, ctx):
        m = Memory(nc, ctx, "w1")
        self.qkv32 = m.sb("qkv32", [P, KC, 3, D])
        self.qkv = [m.sb("qkv_hi", [P, KC, 3, D], F32R), m.sb("qkv_lo", [P, KC, 3, D], F32R)]
        self.wo32 = m.sb("wo32", [P, KC, D])
        self.wo = [m.sb("wo_hi", [P, KC, D], F32R), m.sb("wo_lo", [P, KC, D], F32R)]
        self.bias = m.sb("bias", [P, D])

    def beside(self, a, gate_row):
        return Beside(
            loads=[(self.qkv32[:].rearrange("p k w n -> p (k w n)"), a["w_qkv1"]),
                   (self.wo32[:].rearrange("p k n -> p (k n)"), a["wo1"]), (self.bias[:], a["bo1"])],
            gated=[(self.wo32[:], self.wo32[:], gate_row.unsqueeze(1).broadcast_to([P, KC, D])), (self.bias[:], self.bias[:], gate_row)],
            splits=[(self.qkv[0][:], self.qkv[1][:], self.qkv32[:]), (self.wo[0][:], self.wo[1][:], self.wo32[:])])


def attention1_phase(nc, w, qk_dram, x, h_hi, h_lo, ident, ident_bf, mask_q, mask_t, stats):
    with ExitStack() as outer:
        m = Memory(nc, outer, "l1")
        v_all = m.sb("v_all", [P, HEADS1, NT, VW], F16)
        context = m.sb("context", [P, NT, D])
        project1_block(nc, w.qkv, qk_dram, v_all, h_hi, h_lo)
        attention1_block(nc, qk_dram, v_all, context, ident, ident_bf, mask_q, mask_t)
        output1_block(nc, w.wo, w.bias, context, x, ident, h_hi, h_lo, stats)



E1, INNER1, ALWAYS1 = 16, 176, 2
PAIRS1 = (E1 + ALWAYS1) // 2
TAIL1 = INNER1 - P
CHUNKS1 = 3


SLOTS1 = 3
IN1 = KC * CHUNKS1 * P


class Ffn1Weights:

    def __init__(self, nc, ctx):
        m = Memory(nc, ctx, "w3")
        self.gate_w, self.bias = m.sb("gate_w", [P, KC, E1]), m.sb("bias", [P, E1])
        self.stage = m.sb("stage", [P, SLOTS1, 2 * IN1 + CHUNKS1 * D])
        self.gated = m.sb("gated", [P, CHUNKS1, D])
        self.w_in = [m.sb(f"w_in_{part}", [P, SLOTS1, 2, KC, CHUNKS1, P], F32R) for part in ("hi", "lo")]
        self.w_out = [m.sb(f"w_out_{part}", [P, SLOTS1, CHUNKS1, D], F32R) for part in ("hi", "lo")]

    def beside_norm(self, a):
        return Beside([(self.gate_w[:], a["gate_w1"]), (self.bias[:], a["gate_bias1"]), (self.stage[:, 0], a["f1_pairs"][0])])

    def beside_routing(self, gate_row):
        first = self.stage[:, 0]
        hi, lo = [w[:, 0].rearrange("p w k c n -> p (w k c n)") for w in self.w_in]
        return Beside(gated=[(self.gated[:], first[:, 2 * IN1:].rearrange("p (c d) -> p c d", c=CHUNKS1),
                              gate_row.unsqueeze(1).broadcast_to([P, CHUNKS1, D]))],
                      splits=[(hi, lo, first[:, 0:2 * IN1]), (self.w_out[0][:, 0], self.w_out[1][:, 0], self.gated[:])])


def ffn1_block(nc, w, w_dram, cw_dram, x, h_hi, h_lo, gate_row):
    SLOTS, IN = SLOTS1, IN1
    stage, gated, w_in, w_out = w.stage, w.gated, w.w_in, w.w_out
    ROUNDS = PAIRS1 // SLOTS
    PAIR_UNITS = NB * CHUNKS1
    UNITS_ROUND = SLOTS * PAIR_UNITS
    FB, R = 2, 4
    DONE = PAIR_UNITS + R
    round_units = [(s, b, c) for s in range(SLOTS) for b in range(NB) for c in range(CHUNKS1)]
    with ExitStack() as ctx:
        m = Memory(nc, ctx, "f1")
        crow = m.sb("crow", [4, SLOTS, T], F16)
        pick = m.sb("pick", [4, CHUNKS1, P], F16)
        silu, both, prod = m.sb("silu", [P, R, QB]), m.sb("both", [P, R, QB]), m.sb("prod", [P, R, QB])
        split = [m.sb("t_hi", [P, R, QB], F32R), m.sb("t_lo", [P, R, QB], F32R)]
        ps_g, ps_u, ps_c = m.ps("ps_g", [P, FB, QB]), m.ps("ps_u", [P, FB, QB]), m.ps("ps_c", [P, FB, QB])
        ps_y = m.ps("ps_y", [P, TPB, D])
        ones_ready, picked = m.sem("ones_ready"), m.sem("picked")
        w_loaded, c_loaded = [[m.sem(f"{what}_loaded{slot}") for slot in range(SLOTS)] for what in "wc"]
        gated_ready, w_hi_ready, w_ready = m.sem("gated_ready"), m.sem("w_hi_ready"), m.sem("w_ready")
        g_filled, filled, silu_ready, both_ready = m.sem("g_filled"), m.sem("filled"), m.sem("silu_ready"), m.sem("both_ready")
        prod_ready, hi_ready, t_ready = m.sem("prod_ready"), m.sem("hi_ready"), m.sem("t_ready")
        second_done, y_read = m.sem("second_done"), m.sem("y_read")
        block = ctx.enter_context(nc.Block())

        @block.sync
        def _(sp):
            def load(pair, slot):
                sp.dma_start(crow[:, slot], cw_dram[pair]).then_inc(c_loaded[slot], 16)
                sp.dma_start(stage[:, slot], w_dram[pair]).then_inc(w_loaded[slot], 16)

            sp.dma_start(crow[:, 0], cw_dram[0]).then_inc(c_loaded[0], 16)
            for slot in range(1, SLOTS):
                load(slot, slot)
            with sp.Fori(0, ROUNDS - 1) as i:
                for slot in range(SLOTS):
                    sp.wait_ge(filled, (SLOTS * i + slot + 1) * PAIR_UNITS)
                    load(SLOTS * i + slot + SLOTS, slot)
            for slot in range(SLOTS):
                sp.wait_ge(w_loaded[slot], 16 * (ROUNDS - (slot == 0)))
                sp.wait_ge(c_loaded[slot], 16 * ROUNDS)

        PARTS = 3

        def at_next_pair(i, u, step):
            v = u % PAIR_UNITS - 4
            if v in (0, 2, 4) and not (isinstance(i, int) and i == ROUNDS - 1 and u >= (SLOTS - 1) * PAIR_UNITS):
                s = u // PAIR_UNITS + 1
                step(SLOTS * i + s, s % SLOTS, i + 1, v // 2)

        def split_part(slot, part):
            if part < 2:
                half = KC * CHUNKS1 * P
                return (stage[:, slot, part * half:(part + 1) * half],
                        *[w[:, slot, part].rearrange("p k c n -> p (k c n)") for w in w_in])
            return gated[:], w_out[0][:, slot], w_out[1][:, slot]

        @block.gpsimd
        def _(pool):
            nc.gpsimd.memset(pick[:], 1.0).then_inc(ones_ready, 1)
            pool.wait_ge(ones_ready, 1)
            for chunk, c0, c1, base, step in ((0, 0, P, 1, -1), (1, 0, P, -2, 1), (2, 0, P // 2, 1, -1), (2, P // 2, P, -2, 1)):
                nc.gpsimd.affine_select(out=pick[:, chunk, c0:c1], in_=pick[:, chunk, c0:c1], compare_op=ALU.is_ge, fill=0.0,
                                        base=base, pattern=[[0, c1 - c0]], channel_multiplier=step).then_inc(picked, 1)

            def weights(pair, slot, loads, part):
                if part:
                    return
                pool.wait_ge(w_ready, PARTS * pair)
                pool.wait_ge(w_loaded[slot], 16 * loads)
                nc.gpsimd.tensor_tensor(gated[:], stage[:, slot, 2 * IN:].rearrange("p (c d) -> p c d", c=CHUNKS1),
                                        gate_row.unsqueeze(1).broadcast_to([P, CHUNKS1, D]), ALU.mult).then_inc(gated_ready, 1)

            pipeline(pool, ROUNDS, UNITS_ROUND, [(0, lambda i, u: at_next_pair(i, u, weights))])

        @block.tensor
        def _(pe):
            pe.sem_inc(second_done, DONE)

            def first(i, u):
                s, b, c = round_units[u]
                n = i * UNITS_ROUND + u
                if (b, c) == (0, 0):
                    pe.wait_ge(w_ready, PARTS * (SLOTS * i + s + 1))
                tok = slice(b * QB, (b + 1) * QB)
                pe.wait_ge(prod_ready, n + 1)
                for which, ps in ((0, ps_g), (1, ps_u)):
                    for k in range(KC):
                        for wi, hi in THREE:
                            last = nc.tensor.matmul(ps[:, u % FB], w_in[wi][:, s, which, k, c], (h_hi, h_lo)[hi][:, k, tok],
                                                    start=(k == 0 and (wi, hi) == (0, 0)), stop=(k == KC - 1 and (wi, hi) == (1, 0)))
                    if which == 0:
                        last.then_inc(g_filled, 1)
                if (b, c) == (0, 0):
                    pe.wait_ge(c_loaded[s], 16 * (i + 1))
                    pe.wait_ge(picked, 4)
                nc.tensor.matmul(ps_c[:, u % FB], pick[:, c], crow[:, s, tok], start=True, stop=True).then_inc(filled, 1)

            def second(i, u):
                s, b, c = round_units[u]
                n = i * UNITS_ROUND + u
                if c == 0:
                    pe.wait_ge(y_read, i * (UNITS_ROUND // CHUNKS1) + u // CHUNKS1 + 1)
                pe.wait_ge(t_ready, n + 1)
                for t in range(TPB):
                    for ti, wi in THREE:
                        last = nc.tensor.matmul(ps_y[:, t], split[ti][:, u % R, t * P:(t + 1) * P], w_out[wi][:, s, c],
                                                start=(c == 0 and t % 2 == 0 and (ti, wi) == (0, 0)),
                                                stop=(c == CHUNKS1 - 1 and t % 2 == 1 and (ti, wi) == (1, 0)))
                last.then_inc(second_done, 1)

            pipeline(pe, ROUNDS, UNITS_ROUND, [(2, first), (0, second)])

        @block.scalar
        def _(act):
            def weights(pair, slot, loads, part):
                if part == 0:
                    act.wait_ge(w_loaded[slot], 16 * loads)
                    if not isinstance(pair, int) or pair > 1:
                        act.wait_ge(second_done, (pair - 2) * PAIR_UNITS + DONE)
                if part == 2:
                    act.wait_ge(gated_ready, pair)
                w, hi, _ = split_part(slot, part)
                nc.scalar.activation(hi, w, ACT.Copy).then_inc(w_hi_ready, 1)

            def gate(i, u):
                n = i * UNITS_ROUND + u
                act.wait_ge(g_filled, n + 1)
                act.wait_ge(prod_ready, n + 1)
                nc.scalar.activation(silu[:, u % R], ps_g[:, u % FB], ACT.Silu).then_inc(silu_ready, 1)

            def leading(i, u):
                n = i * UNITS_ROUND + u
                act.wait_ge(prod_ready, n + 1 + FB)
                act.wait_ge(second_done, n + 1 - R + DONE)
                nc.scalar.activation(split[0][:, u % R], prod[:, u % R], ACT.Copy).then_inc(hi_ready, 1)

            pipeline(act, ROUNDS, UNITS_ROUND, [(1, gate), (0, leading), (0, lambda i, u: at_next_pair(i, u, weights))])

        @block.vector
        def _(dve):
            dve.sem_inc(prod_ready, FB)
            dve.sem_inc(y_read, 1)
            dve.sem_inc(w_ready, PARTS)

            def weights(pair, slot, loads, part):
                w, hi, lo = split_part(slot, part)
                dve.wait_ge(w_hi_ready, PARTS * (pair - 1) + part + 1)
                nc.vector.tensor_tensor(lo, w, f32(hi), ALU.subtract).then_inc(w_ready, 1)

            def times_up(i, u):
                n = i * UNITS_ROUND + u
                dve.wait_ge(silu_ready, n + 1)
                dve.wait_ge(filled, n + 1)
                nc.vector.tensor_tensor(both[:, u % R], silu[:, u % R], ps_u[:, u % FB], ALU.mult).then_inc(both_ready, 1)

            def times_weight(i, u):
                n = i * UNITS_ROUND + u
                dve.wait_ge(both_ready, n + 1)
                nc.vector.tensor_tensor(prod[:, u % R], both[:, u % R], ps_c[:, u % FB], ALU.mult).then_inc(prod_ready, 1)

            def rest(i, u):
                n = i * UNITS_ROUND + u
                dve.wait_ge(hi_ready, n + 1)
                nc.vector.tensor_tensor(split[1][:, u % R], prod[:, u % R], f32(split[0][:, u % R]), ALU.subtract).then_inc(t_ready, 1)

            def collect(i, u):
                s, b, c = round_units[u]
                if c == CHUNKS1 - 1:
                    n = i * UNITS_ROUND + u
                    dve.wait_ge(second_done, n + 1 + DONE)
                    xs = x[:, b * TPB:(b + 1) * TPB]
                    nc.vector.tensor_tensor(xs, xs, ps_y[:], ALU.add).then_inc(y_read, 1)

            pipeline(dve, ROUNDS, UNITS_ROUND, [(1, times_up), (0, rest), (1, times_weight), (0, collect),
                                                (0, lambda i, u: at_next_pair(i, u, weights))])


def store_phase(nc, x, out):
    with ExitStack() as ctx:
        m = Memory(nc, ctx, "store")
        stored = m.sem("stored")
        block = ctx.enter_context(nc.Block())

        @block.sync
        def _(sp):
            sp.dma_start(out.rearrange("a (t p) d -> p (a t) d", p=P), x[:]).then_inc(stored, 16)
            sp.wait_ge(stored, 16)


def adaln_program(nc, a, out):
    with ExitStack() as ctx:
        m = Memory(nc, ctx, "all")
        cw0 = nc.dram_tensor("cw0", (E0 // GROUP0, 2 * GROUP0, T), F16, kind="Internal").ap()
        x = m.sb("x", [P, NT, D])
        ident = m.sb("ident", [P, P])
        ident_bf = m.sb("ident_bf", [P, P], BF16)
        ident_h = m.sb("ident_h", [P, P], F16)
        mask_q = m.sb("mask_q", [P, P], BF16)
        mask_t = m.sb("mask_t", [P, P], BF16)
        coef = m.sb("coef", [P, 2, 8])
        gate = m.sb("gate", [P, 2, 2, D])
        stats = m.sb("stats", [P, NT, 6])
        h_hi = m.sb("h_hi", [P, KC, T], F32R)
        h_lo = m.sb("h_lo", [P, KC, T], F32R)
        setup_phase(nc, a["x"], [a["c0"], a["c1"]], [a["wmod0"], a["wmod1"]], x, ident, ident_bf, ident_h, mask_q, mask_t, coef, gate, stats)
        with ExitStack() as layer:
            w = Attention0Weights(nc, layer)
            norm_phase(nc, "n0", x, ident, coef[:, 0, 0:4], h_hi, h_lo, w.beside(a["w_odd"]), stats)
            attention0_phase(nc, w, a["w_even"], a["w_odd"], x, h_hi, h_lo, ident_bf, ident_h, mask_q, mask_t, gate[:, 0, 0], stats)
        with ExitStack() as layer:
            w = Ffn0Weights(nc, layer)
            norm_phase(nc, "n1", x, ident, coef[:, 0, 4:8], h_hi, h_lo, w.beside_norm(a), stats)
            routing_phase(nc, "r0", w.gate_w, w.bias, cw0.rearrange("g r t -> (g r) t"), h_hi, h_lo, ident_h,
                          E0, 4, 2, 8, 2.5, 0, w.beside_routing(a, gate[:, 0, 1]))
            ffn0_phase(nc, w, a["f0_experts"], cw0, x, h_hi, h_lo, stats)
        with ExitStack() as layer:
            w = Attention1Weights(nc, layer)
            qk1 = nc.dram_tensor("qk1", (2, 2, D, T), F16, kind="Internal").ap()
            norm_phase(nc, "n2", x, ident, coef[:, 1, 0:4], h_hi, h_lo, w.beside(a, gate[:, 1, 0]), stats)
            attention1_phase(nc, w, qk1, x, h_hi, h_lo, ident, ident_bf, mask_q, mask_t, stats)
        with ExitStack() as layer:
            w = Ffn1Weights(nc, layer)
            cw1 = nc.dram_tensor("cw1", (PAIRS1, 4, T), F16, kind="Internal").ap()
            norm_phase(nc, "n3", x, ident, coef[:, 1, 4:8], h_hi, h_lo, w.beside_norm(a), stats)
            routing_phase(nc, "r1", w.gate_w, w.bias, cw1.rearrange("g r t -> (g r) t"), h_hi, h_lo, ident_h,
                          E1, 4, 1, 4, 1.0, ALWAYS1, w.beside_routing(gate[:, 1, 1]))
            ffn1_block(nc, w, a["f1_pairs"], cw1, x, h_hi, h_lo, gate[:, 1, 1])
        store_phase(nc, x, out)



def host_layout(i):
    import numpy as np

    heads = HEADS0
    qk = np.stack([i["L0_attn_W_Q"], i["L0_attn_W_K"]])
    qk = qk.reshape(2, heads, DH0, KC, P).transpose(1, 4, 3, 0, 2).reshape(heads, P, KC * 2 * DH0)
    v = i["L0_attn_W_V"].reshape(heads // 2, 2, DH0, KC, P).transpose(0, 4, 3, 1, 2).reshape(heads // 2, P, KC * 2 * DH0)
    wo = i["L0_attn_W_O"].transpose(0, 2, 1)
    w_even = np.zeros((heads // 2 + 1, P, 768), np.float32)
    w_odd = np.zeros((heads // 2 + 2, P, 1280), np.float32)
    for j in range(heads // 2):
        w_even[j, :, 0:512], w_even[j, :, 512:768] = qk[2 * j + 1], wo[2 * j]
        w_odd[j, :, 0:512], w_odd[j, :, 512:1024] = qk[2 * j], v[j]
        w_odd[j + 1, :, 1024:1280] = wo[2 * j + 1]
    out = {"x": i["L0_attn_x"], "w_even": w_even, "w_odd": w_odd}
    for layer in range(2):
        out[f"c{layer}"] = i[f"L{layer}_c"].reshape(KC, P).T
        out[f"wmod{layer}"] = i[f"L{layer}_wmod"]

    def by_rows(a):
        return a.reshape(-1, P, a.shape[1]).transpose(1, 0, 2).reshape(P, -1)

    for layer, experts in enumerate((E0, 16)):
        out[f"gate_w{layer}"] = i[f"L{layer}_ffn_gate_w"].reshape(experts, KC, P).transpose(2, 1, 0)
    out["gate_bias0"] = np.broadcast_to(i["L0_ffn_gate_bias"], (P, E0))
    out["f0_in"] = np.concatenate([by_rows(i["L0_ffn_fc1_w"].T), by_rows(i["L0_ffn_shared_up_w"].T)], axis=1)
    out["f0_out"] = np.concatenate([i["L0_ffn_fc2_w"].T, by_rows(i["L0_ffn_shared_down_w"].T)], axis=1)
    both = np.stack([i["L0_ffn_w1"].transpose(2, 0, 1), i["L0_ffn_w2"].transpose(2, 0, 1)], axis=2)
    out["f0_experts"] = both.reshape(P, E0 // GROUP0, GROUP0 * 2 * P).transpose(1, 0, 2)
    qkv = np.stack([i["L1_attn_Wq"], i["L1_attn_Wk"], i["L1_attn_Wv"]])
    out["w_qkv1"] = qkv.reshape(3, KC, P, D).transpose(2, 1, 0, 3).reshape(P, -1)
    out["wo1"] = by_rows(i["L1_attn_Wo"])
    out["bo1"] = np.broadcast_to(i["L1_attn_bo"], (P, D))
    out["gate_bias1"] = np.broadcast_to(i["L1_ffn_expert_bias"], (P, E1))

    def shared_halves(a):
        return a.reshape(a.shape[0], ALWAYS1, INNER1).transpose(1, 0, 2)

    def in_chunks(a):
        a = a.reshape(PAIRS1, 2, *a.shape[1:])
        chunks = np.zeros((PAIRS1, *a.shape[2:-1], CHUNKS1, P), np.float32)
        for e in range(2):
            chunks[..., e, :] = a[:, e, ..., :P]
            chunks[..., 2, e * P // 2:e * P // 2 + TAIL1] = a[:, e, ..., P:]
        return chunks

    up = [in_chunks(np.concatenate([i[f"L1_ffn_w{n}"], shared_halves(i[f"L1_ffn_sw{n}"])])) for n in (1, 3)]
    up = np.stack([u.reshape(PAIRS1, KC, P, CHUNKS1, P) for u in up], axis=1)
    down = np.concatenate([i["L1_ffn_w2"], i["L1_ffn_sw2"].reshape(ALWAYS1, INNER1, D)])
    down = in_chunks(down.transpose(0, 2, 1))
    out["f1_pairs"] = np.concatenate([up.transpose(0, 3, 1, 2, 4, 5).reshape(PAIRS1, P, -1),
                                      down.transpose(0, 3, 2, 1).reshape(PAIRS1, P, -1)], axis=2)
    return {k: np.ascontiguousarray(v) for k, v in out.items()}


def kernel(**inputs):
    import numpy as np
    import concourse.bacc as bacc
    from concourse.bass_utils import run_bass_kernel_spmd

    nc = bacc.Bacc("TRN2", target_bir_lowering=False, num_devices=1)
    arrays = host_layout({k: np.asarray(v) for k, v in inputs.items()})
    aps = {k: nc.dram_tensor(f"in_{k}", v.shape, F32, kind="ExternalInput").ap() for k, v in arrays.items()}
    out = nc.dram_tensor("out", (1, T, D), F32, kind="ExternalOutput").ap()
    adaln_program(nc, aps, out)
    r = run_bass_kernel_spmd(nc, [{f"in_{k}": v for k, v in arrays.items()}], core_ids=[0])
    return r.results[0]["out"]
```
